# Optimizing a Trainium2 kernel written in Bass

```python
import numpy as np
import jax
import jax.numpy as jnp

def _softmax(x, axis=-1):
    return jax.nn.softmax(x, axis=axis)

def _gelu(x):
    return jax.nn.gelu(x, approximate=True)

def _silu(x):
    return jax.nn.silu(x)

def _sigmoid(x):
    return jax.nn.sigmoid(x)

def _layernorm(x, axis=-1, eps=1e-05):
    m = jnp.mean(x, axis=axis, keepdims=True)
    v = jnp.var(x, axis=axis, keepdims=True)
    return (x - m) / jnp.sqrt(v + eps)

def _scatter_add(tgt, idx, src, axis=0):
    return tgt.at[idx].add(src)

def _segment_sum(src, seg, n):
    return jax.ops.segment_sum(src, seg, n)
kernel_name = 'mk_perceiver_d2_seqx_r4_186395'

def setup_inputs(seed: int=0):
    np.random.seed(seed)
    _w = jnp.asarray

    def _rec_inputs():
        import jax
        import jax.numpy as jnp
        _rk = jax.random.key(seed)
        x = -0.000125 + 0.9999 * jax.random.normal(jax.random.fold_in(_rk, 1), (2, 64, 1024), jnp.float32)
        _lenS = 64 - jax.random.randint(jax.random.fold_in(_rk, 7), (2,), 0, max(1, 64 // 4) + 1, jnp.int32)
        _lenS2 = 1024 - jax.random.randint(jax.random.fold_in(_rk, 8), (2,), 0, max(1, 1024 // 4) + 1, jnp.int32)
        _ctx_4096P = jax.random.normal(jax.random.fold_in(_rk, 11), (2, 16, 1024), jnp.float32)
        _ctx_4096c = jax.random.dirichlet(jax.random.fold_in(_rk, 511), 0.3 * jnp.ones((16,), jnp.float32), (2, 1024))
        _ctx_4096t = jnp.einsum('bsk,bkd->bsd', _ctx_4096c, _ctx_4096P)
        _ctx_4096t = _ctx_4096t * jax.lax.rsqrt(jnp.mean(jnp.square(_ctx_4096t)) + 1e-12) * 0.953939
        ctx_4096 = -5.72187e-05 + 0.999849 * (_ctx_4096t + 0.3 * jax.random.normal(jax.random.fold_in(_rk, 611), (2, 1024, 1024), jnp.float32))
        return (x, ctx_4096)
    x, ctx_4096 = _rec_inputs()

    def _L0_xattn_setup():
        import jax, jax.numpy as jnp
        import numpy as np
        QMIN = 0.0
        QMAX = 255.0

        def fake_quant(x, scale, zp):
            s = scale.reshape(())
            z = zp.reshape(())
            q = jnp.clip(jnp.round(x / s + z), QMIN, QMAX)
            return (q - z) * s
        key = jax.random.key(seed)
        k1, k2 = jax.random.split(key)
        B, M, K, N = (4, 512, 1024, 1024)
        x1 = jax.random.normal(k1, (B, M, K), dtype=jnp.float32)
        x2 = jax.random.normal(k2, (B, K, N), dtype=jnp.float32)
        x1_scale = jnp.full((1,), 8.0 / 255.0, dtype=jnp.float32)
        x1_zp = jnp.full((1,), 128.0, dtype=jnp.float32)
        x2_scale = jnp.full((1,), 8.0 / 255.0, dtype=jnp.float32)
        x2_zp = jnp.full((1,), 128.0, dtype=jnp.float32)
        return {'x1': x1, 'x2': x2, 'x1_scale': x1_scale, 'x1_zp': x1_zp, 'x2_scale': x2_scale, 'x2_zp': x2_zp}
    _L0_xattn_all = _L0_xattn_setup()
    _L0_xattn_in = {k: v for k, v in _L0_xattn_all.items() if k in ('x1_scale', 'x1_zp', 'x2_scale', 'x2_zp')}
    del _L0_xattn_all

    def _L0_attn_setup():
        import jax, jax.numpy as jnp
        import numpy as np
        HID = 1024
        NH = 128
        HD = 64
        DIN = NH * HD
        G = 8
        N = 128
        K = 4
        CS = 64
        EPS = 1e-05
        GROUP_SIZE = DIN // G
        CONV_DIM = DIN + 2 * G * N
        PROJ = DIN + CONV_DIM + NH

        def segment_sum(x):
            k = x.shape[-1]
            xe = jnp.broadcast_to(x[..., None], x.shape + (k,))
            xe = jnp.where(jnp.tril(jnp.ones((k, k), bool), -1), xe, 0.0)
            s = jnp.cumsum(xe, axis=-2)
            return jnp.where(jnp.tril(jnp.ones((k, k), bool), 0), s, -jnp.inf)
        key = jax.random.key(seed)
        ks = jax.random.split(key, 9)
        std = 0.02
        return {'hidden_states': jax.random.normal(ks[0], (2, 512, HID), jnp.float32), 'in_proj_w': jax.random.normal(ks[1], (PROJ, HID), jnp.float32) * std, 'conv_w': jax.random.normal(ks[2], (CONV_DIM, 1, K), jnp.float32) * 0.1, 'conv_b': jax.random.normal(ks[3], (CONV_DIM,), jnp.float32) * 0.01, 'dt_bias': jax.random.uniform(ks[4], (NH,), jnp.float32, -4.0, -2.0), 'A_log': jnp.log(jax.random.uniform(ks[5], (NH,), jnp.float32, 1.0, 16.0)), 'D': jnp.ones((NH,), jnp.float32), 'norm_w': jnp.ones((DIN,), jnp.float32), 'out_proj_w': jax.random.normal(ks[8], (HID, DIN), jnp.float32) * std}
    _L0_attn_all = _L0_attn_setup()
    _L0_attn_in = {k: v for k, v in _L0_attn_all.items() if k in ('in_proj_w', 'conv_w', 'conv_b', 'dt_bias', 'A_log', 'D', 'norm_w', 'out_proj_w')}
    del _L0_attn_all

    def _L0_ffn_setup():
        import jax, jax.numpy as jnp
        import numpy as np
        R = 16
        ALPHA = 32
        SCALING = ALPHA / R
        E = 8
        TOP_K = 2
        key = jax.random.key(seed)
        ks = jax.random.split(key, 5)
        B, S, D = (4, 512, 1024)
        x = jax.random.normal(ks[0], (B, S, D), dtype=jnp.float32)
        base_W = jax.random.normal(ks[1], (D, D), dtype=jnp.float32) * 0.02
        router_W = jax.random.normal(ks[2], (E, D), dtype=jnp.float32) * 0.02
        lora_A = jax.random.normal(ks[3], (E, D, R), dtype=jnp.float32) * 0.02
        lora_B = jax.random.normal(ks[4], (E, R, D), dtype=jnp.float32) * 0.02
        return {'x': x, 'base_W': base_W, 'router_W': router_W, 'lora_A': lora_A, 'lora_B': lora_B}
    _L0_ffn_all = _L0_ffn_setup()
    _L0_ffn_in = {k: v for k, v in _L0_ffn_all.items() if k in ('base_W', 'router_W', 'lora_A', 'lora_B')}
    del _L0_ffn_all

    def _L1_xattn_setup():
        import jax, jax.numpy as jnp
        import numpy as np
        K = 10
        NUM_BITS = 10
        M_METHODS = 4

        def _quantize(coords, num_bits=NUM_BITS):
            cmin = coords.min(axis=1, keepdims=True)
            cmax = coords.max(axis=1, keepdims=True)
            scale = (2 ** num_bits - 1) / (cmax - cmin + 1e-06)
            q = jnp.floor((coords - cmin) * scale)
            return jnp.clip(q, 0, 2 ** num_bits - 1).astype(jnp.int32)

        def _morton_key(q):
            x, y, z = (q[..., 0], q[..., 1], q[..., 2])
            key = jnp.zeros(x.shape, dtype=jnp.int32)
            for b in range(NUM_BITS):
                key = key | (x >> b & 1) << 3 * b + 2 | (y >> b & 1) << 3 * b + 1 | (z >> b & 1) << 3 * b
            return key

        def _hilbert_key(q, num_bits=NUM_BITS):
            n = 3
            X = [q[..., i] for i in range(n)]
            M = 1 << num_bits - 1
            Q = M
            while Q > 1:
                P = Q - 1
                for i in range(n):
                    cond = X[i] & Q > 0
                    t = (X[0] ^ X[i]) & P
                    new_X0 = jnp.where(cond, X[0] ^ P, X[0] ^ t)
                    if i != 0:
                        X[i] = jnp.where(cond, X[i], X[i] ^ t)
                    X[0] = new_X0
                Q >>= 1
            for i in range(1, n):
                X[i] = X[i] ^ X[i - 1]
            t = jnp.zeros_like(X[0])
            Q = M
            while Q > 1:
                t = jnp.where(X[n - 1] & Q > 0, t ^ Q - 1, t)
                Q >>= 1
            X = [xi ^ t for xi in X]
            key = jnp.zeros(X[0].shape, dtype=jnp.int32)
            for b in range(num_bits - 1, -1, -1):
                for i in range(n):
                    key = key << 1 | X[i] >> b & 1
            return key

        def _sorted_indices(coords_bn3):
            q = _quantize(coords_bn3)
            qt = q[..., jnp.array([1, 0, 2])]
            keys = [_morton_key(q), _morton_key(qt), _hilbert_key(q), _hilbert_key(qt)]
            return [jnp.argsort(kk, axis=1) for kk in keys]

        def _window_inds(sorted_idx, k=K):
            B, N = sorted_idx.shape
            i = jnp.arange(N)
            start = jnp.maximum(0, i - k // 2)
            end = jnp.minimum(N, i + k // 2 + 1)
            pos = jnp.minimum(start[:, None] + jnp.arange(k)[None, :], (end - 1)[:, None])
            return jnp.take(sorted_idx, pos, axis=1)

        def _get_graph_features(feats, inds_list, perm, W_lin, b_lin, k=K):
            B, N, C = feats.shape
            center = feats[:, :, None, :]
            gather = jax.vmap(lambda f, idx: f[idx])
            per_method = []
            for inds in inds_list:
                neigh = gather(feats, inds)
                gf = jnp.concatenate([jnp.broadcast_to(center, (B, N, k, C)), neigh - center], axis=-1)
                per_method.append(gf)
            allf = jnp.stack(per_method, axis=-1)
            allf = allf[..., perm]
            total = 2 * C * M_METHODS
            x = allf.reshape(B * N, k, total)
            x16 = x.astype(jnp.float16).astype(jnp.float32)
            headdim = min(64, total)
            nheads = total // headdim
            qh = x16.reshape(B * N, k, nheads, headdim)
            scores = jnp.einsum('bihd,bjhd->bhij', qh, qh) / np.float32(np.sqrt(headdim))
            attn = jax.nn.softmax(scores, axis=-1)
            out = jnp.einsum('bhij,bjhd->bihd', attn, qh).reshape(B * N, k, total)
            fused = out @ W_lin.T + b_lin
            return fused.reshape(B, N, k, 128)

        def _instance_norm(x, axes):
            mu = x.mean(axis=axes, keepdims=True)
            var = x.var(axis=axes, keepdims=True)
            return (x - mu) / jnp.sqrt(var + 1e-05)

        def _lrelu(x):
            return jnp.where(x > 0, x, 0.2 * x)
        key = jax.random.key(seed)
        ks = jax.random.split(key, 8)
        B, N, C = (2, 1024, 64)
        tot = M_METHODS * 2 * C
        s = 0.02
        return {'coords': jax.random.normal(ks[0], (B, 3, N), jnp.float32), 'feats': jax.random.normal(ks[1], (B, C, N), jnp.float32), 'W_lin1': jax.random.normal(ks[2], (128, tot), jnp.float32) * s, 'b_lin1': jnp.zeros((128,), jnp.float32), 'W_lin2': jax.random.normal(ks[3], (128, tot), jnp.float32) * s, 'b_lin2': jnp.zeros((128,), jnp.float32), 'W_conv1': jax.random.normal(ks[4], (C, 2 * C), jnp.float32) * s, 'W_conv2': jax.random.normal(ks[5], (2 * C, 2 * C), jnp.float32) * s, 'W_conv3': jax.random.normal(ks[6], (C, 4 * C), jnp.float32) * s}
    _L1_xattn_all = _L1_xattn_setup()
    _L1_xattn_in = {k: v for k, v in _L1_xattn_all.items() if k in ('W_lin1', 'b_lin1', 'W_lin2', 'b_lin2', 'W_conv1', 'W_conv2', 'W_conv3')}
    del _L1_xattn_all

    def _L1_attn_setup():
        import jax, jax.numpy as jnp
        import numpy as np
        BLOCK_H = 32
        BLOCK_W = 32
        N_FEAT = 1024
        K_FEAT = 1024
        key = jax.random.key(seed)
        k1, k2, k3 = jax.random.split(key, 3)
        data = jax.random.normal(k1, (4, 256, K_FEAT), dtype=jnp.float32)
        weight = jax.random.normal(k2, (N_FEAT, K_FEAT), dtype=jnp.float32) * 0.02
        nb, kb = (N_FEAT // BLOCK_H, K_FEAT // BLOCK_W)
        block_pattern = jax.random.randint(k3, (nb, kb), 0, 2, dtype=jnp.int32)
        mask = jnp.repeat(jnp.repeat(block_pattern, BLOCK_H, axis=0), BLOCK_W, axis=1)
        return {'data': data, 'weight': weight, 'mask': mask}
    _L1_attn_all = _L1_attn_setup()
    _L1_attn_in = {k: v for k, v in _L1_attn_all.items() if k in ('weight', 'mask')}
    del _L1_attn_all

    def _L1_ffn_setup():
        import jax, jax.numpy as jnp
        import numpy as np
        M = 1024
        K = 1024

        def _make_2to4_mask(key, shape):
            scores = jax.random.normal(key, shape)
            g = scores.reshape(shape[0], shape[1] // 4, 4)
            rank = jnp.argsort(jnp.argsort(-jnp.abs(g), axis=-1), axis=-1)
            return (rank < 2).reshape(shape).astype(jnp.float32)
        key = jax.random.key(seed)
        k_x, k_w12, k_b12, k_w3, k_b3, k_m = jax.random.split(key, 6)
        x = jax.random.normal(k_x, (4, 512, K), dtype=jnp.float32)
        w12_dense = jax.random.normal(k_w12, (2 * M, K), dtype=jnp.float32) * (1.0 / np.sqrt(K))
        mask12 = _make_2to4_mask(k_m, (2 * M, K))
        w12 = w12_dense * mask12
        b12 = jax.random.normal(k_b12, (2 * M,), dtype=jnp.float32) * 0.01
        w3 = jax.random.normal(k_w3, (M, M), dtype=jnp.float32) * (1.0 / np.sqrt(M))
        b3 = jax.random.normal(k_b3, (M,), dtype=jnp.float32) * 0.01
        return {'x': x, 'w12': w12, 'b12': b12, 'w3': w3, 'b3': b3}
    _L1_ffn_all = _L1_ffn_setup()
    _L1_ffn_in = {k: v for k, v in _L1_ffn_all.items() if k in ('w12', 'b12', 'w3', 'b3')}
    del _L1_ffn_all
    return {'x': x, 'ctx_4096': ctx_4096, 'L0_xattn_x1_scale': _L0_xattn_in['x1_scale'], 'L0_xattn_x1_zp': _L0_xattn_in['x1_zp'], 'L0_xattn_x2_scale': _L0_xattn_in['x2_scale'], 'L0_xattn_x2_zp': _L0_xattn_in['x2_zp'], 'L0_attn_in_proj_w': _L0_attn_in['in_proj_w'], 'L0_attn_conv_w': _L0_attn_in['conv_w'], 'L0_attn_conv_b': _L0_attn_in['conv_b'], 'L0_attn_dt_bias': _L0_attn_in['dt_bias'], 'L0_attn_A_log': _L0_attn_in['A_log'], 'L0_attn_D': _L0_attn_in['D'], 'L0_attn_norm_w': _L0_attn_in['norm_w'], 'L0_attn_out_proj_w': _L0_attn_in['out_proj_w'], 'L0_ffn_base_W': _L0_ffn_in['base_W'], 'L0_ffn_router_W': _L0_ffn_in['router_W'], 'L0_ffn_lora_A': _L0_ffn_in['lora_A'], 'L0_ffn_lora_B': _L0_ffn_in['lora_B'], 'L1_xattn_W_lin1': _L1_xattn_in['W_lin1'], 'L1_xattn_b_lin1': _L1_xattn_in['b_lin1'], 'L1_xattn_W_lin2': _L1_xattn_in['W_lin2'], 'L1_xattn_b_lin2': _L1_xattn_in['b_lin2'], 'L1_xattn_W_conv1': _L1_xattn_in['W_conv1'], 'L1_xattn_W_conv2': _L1_xattn_in['W_conv2'], 'L1_xattn_W_conv3': _L1_xattn_in['W_conv3'], 'L1_attn_weight': _L1_attn_in['weight'], 'L1_attn_mask': _L1_attn_in['mask'], 'L1_ffn_w12': _L1_ffn_in['w12'], 'L1_ffn_b12': _L1_ffn_in['b12'], 'L1_ffn_w3': _L1_ffn_in['w3'], 'L1_ffn_b3': _L1_ffn_in['b3']}

def reference(x, ctx_4096, L0_xattn_x1_scale, L0_xattn_x1_zp, L0_xattn_x2_scale, L0_xattn_x2_zp, L0_attn_in_proj_w, L0_attn_conv_w, L0_attn_conv_b, L0_attn_dt_bias, L0_attn_A_log, L0_attn_D, L0_attn_norm_w, L0_attn_out_proj_w, L0_ffn_base_W, L0_ffn_router_W, L0_ffn_lora_A, L0_ffn_lora_B, L1_xattn_W_lin1, L1_xattn_b_lin1, L1_xattn_W_lin2, L1_xattn_b_lin2, L1_xattn_W_conv1, L1_xattn_W_conv2, L1_xattn_W_conv3, L1_attn_weight, L1_attn_mask, L1_ffn_w12, L1_ffn_b12, L1_ffn_w3, L1_ffn_b3):
    import jax
    import jax.numpy as jnp

    def _L0_xattn_ref(x1, x2, x1_scale, x1_zp, x2_scale, x2_zp):
        import jax, jax.numpy as jnp
        import numpy as np
        QMIN = 0.0
        QMAX = 255.0

        def fake_quant(x, scale, zp):
            s = scale.reshape(())
            z = zp.reshape(())
            q = jnp.clip(jnp.round(x / s + z), QMIN, QMAX)
            return (q - z) * s
        q1 = fake_quant(x1, x1_scale, x1_zp)
        q2 = fake_quant(x2, x2_scale, x2_zp)
        return jnp.matmul(q1, q2)

    def _L0_attn_ref(hidden_states, in_proj_w, conv_w, conv_b, dt_bias, A_log, D, norm_w, out_proj_w):
        import jax, jax.numpy as jnp
        import numpy as np
        HID = 1024
        NH = 128
        HD = 64
        DIN = NH * HD
        G = 8
        N = 128
        K = 4
        CS = 64
        EPS = 1e-05
        GROUP_SIZE = DIN // G
        CONV_DIM = DIN + 2 * G * N
        PROJ = DIN + CONV_DIM + NH

        def segment_sum(x):
            k = x.shape[-1]
            xe = jnp.broadcast_to(x[..., None], x.shape + (k,))
            xe = jnp.where(jnp.tril(jnp.ones((k, k), bool), -1), xe, 0.0)
            s = jnp.cumsum(xe, axis=-2)
            return jnp.where(jnp.tril(jnp.ones((k, k), bool), 0), s, -jnp.inf)
        b, l, _ = hidden_states.shape
        zxbcdt = hidden_states @ in_proj_w.T
        gate = zxbcdt[..., :DIN]
        xBC = zxbcdt[..., DIN:DIN + CONV_DIM]
        dt = zxbcdt[..., DIN + CONV_DIM:]
        conv = jax.lax.conv_general_dilated(jnp.transpose(xBC, (0, 2, 1)), conv_w, (1,), [(K - 1, 0)], feature_group_count=CONV_DIM, dimension_numbers=('NCH', 'OIH', 'NCH'))
        xBC = jax.nn.silu(jnp.transpose(conv + conv_b[None, :, None], (0, 2, 1)))
        x = xBC[..., :DIN].reshape(b, l, NH, HD)
        B = xBC[..., DIN:DIN + G * N].reshape(b, l, G, N)
        C = xBC[..., DIN + G * N:].reshape(b, l, G, N)
        B = jnp.repeat(B, NH // G, axis=2)
        C = jnp.repeat(C, NH // G, axis=2)
        A = -jnp.exp(A_log)
        dt = jax.nn.softplus(dt + dt_bias)
        pad = (CS - l % CS) % CS

        def padl(t):
            return jnp.pad(t, [(0, 0), (0, pad)] + [(0, 0)] * (t.ndim - 2))
        D_res = D[None, None, :, None] * padl(x)
        xs = x * dt[..., None]
        Adt = A[None, None, :] * dt
        nc = (l + pad) // CS

        def chunk(t):
            return padl(t).reshape((b, nc, CS) + t.shape[2:])
        xs, B, C = (chunk(xs), chunk(B), chunk(C))
        Ac = jnp.transpose(chunk(Adt), (0, 3, 1, 2))
        A_cumsum = jnp.cumsum(Ac, axis=-1)
        L = jnp.exp(segment_sum(Ac))
        Gm = jnp.einsum('bcihn,bcjhn->bhcij', C, B)
        Y_diag = jnp.einsum('bhcij,bcjhd->bcihd', Gm * L, xs)
        decay_states = jnp.exp(A_cumsum[..., -1:] - A_cumsum)
        states = jnp.einsum('bckhn,bhck,bckhd->bchdn', B, decay_states, xs)
        A_tail = jnp.pad(A_cumsum[..., -1], ((0, 0), (0, 0), (1, 0)))
        decay_chunk = jnp.exp(segment_sum(A_tail))
        states = jnp.concatenate([jnp.zeros_like(states[:, :1]), states], axis=1)
        new_states = jnp.einsum('bhzc,bchdn->bzhdn', decay_chunk, states)
        states = new_states[:, :-1]
        state_decay = jnp.exp(A_cumsum)
        Y_off = jnp.einsum('bckhn,bchdn,bhck->bckhd', C, states, state_decay)
        y = (Y_diag + Y_off).reshape(b, l + pad, NH, HD) + D_res
        y = y[:, :l].reshape(b, l, DIN)
        y = y * jax.nn.silu(gate)
        yg = y.reshape(b, l, G, GROUP_SIZE)
        var = jnp.mean(yg * yg, axis=-1, keepdims=True)
        y = (yg * jax.lax.rsqrt(var + EPS)).reshape(b, l, DIN) * norm_w
        return y @ out_proj_w.T

    def _L0_ffn_ref(x, base_W, router_W, lora_A, lora_B):
        import jax, jax.numpy as jnp
        import numpy as np
        R = 16
        ALPHA = 32
        SCALING = ALPHA / R
        E = 8
        TOP_K = 2
        base = jnp.einsum('bsd,od->bso', x, base_W)
        logits = jnp.einsum('bsd,ed->bse', x, router_W)
        probs = jax.nn.softmax(logits.astype(jnp.float32), axis=-1)
        top_vals, top_idx = jax.lax.top_k(probs, TOP_K)
        rw = top_vals / jnp.sum(top_vals, axis=-1, keepdims=True)
        w_dense = jnp.sum(jax.nn.one_hot(top_idx, E, dtype=rw.dtype) * rw[..., None], axis=-2).astype(x.dtype)
        mid = jnp.einsum('bsd,edr->bser', x, lora_A)
        mid = mid * w_dense[..., None]
        inc = jnp.einsum('bser,erd->bsd', mid, lora_B)
        return base + inc * SCALING

    def _L1_xattn_ref(coords, feats, W_lin1, b_lin1, W_lin2, b_lin2, W_conv1, W_conv2, W_conv3):
        import jax, jax.numpy as jnp
        import numpy as np
        K = 10
        NUM_BITS = 10
        M_METHODS = 4

        def _quantize(coords, num_bits=NUM_BITS):
            cmin = coords.min(axis=1, keepdims=True)
            cmax = coords.max(axis=1, keepdims=True)
            scale = (2 ** num_bits - 1) / (cmax - cmin + 1e-06)
            q = jnp.floor((coords - cmin) * scale)
            return jnp.clip(q, 0, 2 ** num_bits - 1).astype(jnp.int32)

        def _morton_key(q):
            x, y, z = (q[..., 0], q[..., 1], q[..., 2])
            key = jnp.zeros(x.shape, dtype=jnp.int32)
            for b in range(NUM_BITS):
                key = key | (x >> b & 1) << 3 * b + 2 | (y >> b & 1) << 3 * b + 1 | (z >> b & 1) << 3 * b
            return key

        def _hilbert_key(q, num_bits=NUM_BITS):
            n = 3
            X = [q[..., i] for i in range(n)]
            M = 1 << num_bits - 1
            Q = M
            while Q > 1:
                P = Q - 1
                for i in range(n):
                    cond = X[i] & Q > 0
                    t = (X[0] ^ X[i]) & P
                    new_X0 = jnp.where(cond, X[0] ^ P, X[0] ^ t)
                    if i != 0:
                        X[i] = jnp.where(cond, X[i], X[i] ^ t)
                    X[0] = new_X0
                Q >>= 1
            for i in range(1, n):
                X[i] = X[i] ^ X[i - 1]
            t = jnp.zeros_like(X[0])
            Q = M
            while Q > 1:
                t = jnp.where(X[n - 1] & Q > 0, t ^ Q - 1, t)
                Q >>= 1
            X = [xi ^ t for xi in X]
            key = jnp.zeros(X[0].shape, dtype=jnp.int32)
            for b in range(num_bits - 1, -1, -1):
                for i in range(n):
                    key = key << 1 | X[i] >> b & 1
            return key

        def _sorted_indices(coords_bn3):
            q = _quantize(coords_bn3)
            qt = q[..., jnp.array([1, 0, 2])]
            keys = [_morton_key(q), _morton_key(qt), _hilbert_key(q), _hilbert_key(qt)]
            return [jnp.argsort(kk, axis=1) for kk in keys]

        def _window_inds(sorted_idx, k=K):
            B, N = sorted_idx.shape
            i = jnp.arange(N)
            start = jnp.maximum(0, i - k // 2)
            end = jnp.minimum(N, i + k // 2 + 1)
            pos = jnp.minimum(start[:, None] + jnp.arange(k)[None, :], (end - 1)[:, None])
            return jnp.take(sorted_idx, pos, axis=1)

        def _get_graph_features(feats, inds_list, perm, W_lin, b_lin, k=K):
            B, N, C = feats.shape
            center = feats[:, :, None, :]
            gather = jax.vmap(lambda f, idx: f[idx])
            per_method = []
            for inds in inds_list:
                neigh = gather(feats, inds)
                gf = jnp.concatenate([jnp.broadcast_to(center, (B, N, k, C)), neigh - center], axis=-1)
                per_method.append(gf)
            allf = jnp.stack(per_method, axis=-1)
            allf = allf[..., perm]
            total = 2 * C * M_METHODS
            x = allf.reshape(B * N, k, total)
            x16 = x.astype(jnp.float16).astype(jnp.float32)
            headdim = min(64, total)
            nheads = total // headdim
            qh = x16.reshape(B * N, k, nheads, headdim)
            scores = jnp.einsum('bihd,bjhd->bhij', qh, qh) / np.float32(np.sqrt(headdim))
            attn = jax.nn.softmax(scores, axis=-1)
            out = jnp.einsum('bhij,bjhd->bihd', attn, qh).reshape(B * N, k, total)
            fused = out @ W_lin.T + b_lin
            return fused.reshape(B, N, k, 128)

        def _instance_norm(x, axes):
            mu = x.mean(axis=axes, keepdims=True)
            var = x.var(axis=axes, keepdims=True)
            return (x - mu) / jnp.sqrt(var + 1e-05)

        def _lrelu(x):
            return jnp.where(x > 0, x, 0.2 * x)
        inds_sorted = _sorted_indices(coords.transpose(0, 2, 1))
        inds_list = [_window_inds(s) for s in inds_sorted]
        perm1 = jnp.array([2, 0, 3, 1])
        perm2 = jnp.array([1, 3, 0, 2])
        f0 = feats.transpose(0, 2, 1)
        g1 = _get_graph_features(f0, inds_list, perm1, W_lin1, b_lin1)
        h1 = jnp.einsum('oc,bnkc->bonk', W_conv1, g1)
        h1 = _lrelu(_instance_norm(h1, (2, 3)))
        feats1 = h1.max(axis=-1)
        g2 = _get_graph_features(feats1.transpose(0, 2, 1), inds_list, perm2, W_lin2, b_lin2)
        h2 = jnp.einsum('oc,bnkc->bonk', W_conv2, g2)
        h2 = _lrelu(_instance_norm(h2, (2, 3)))
        feats2 = h2.max(axis=-1)
        f3 = jnp.concatenate([feats, feats1, feats2], axis=1)
        h3 = jnp.einsum('oc,bcn->bon', W_conv3, f3)
        return _lrelu(_instance_norm(h3, (2,)))

    def _L1_attn_ref(data, weight, mask):
        import jax, jax.numpy as jnp
        import numpy as np
        BLOCK_H = 32
        BLOCK_W = 32
        N_FEAT = 1024
        K_FEAT = 1024
        N, K = weight.shape
        nb, kb = (N // BLOCK_H, K // BLOCK_W)
        block_mask = mask.reshape(nb, BLOCK_H, kb, BLOCK_W).astype(jnp.float32).sum(axis=(1, 3)) > 0
        elem_mask = jnp.repeat(jnp.repeat(block_mask, BLOCK_H, axis=0), BLOCK_W, axis=1)
        w_masked = weight * elem_mask.astype(weight.dtype)
        out = jnp.einsum('bsk,nk->bsn', data, w_masked)
        return out

    def _L1_ffn_ref(x, w12, b12, w3, b3):
        import jax, jax.numpy as jnp
        import numpy as np
        M = 1024
        K = 1024

        def _make_2to4_mask(key, shape):
            scores = jax.random.normal(key, shape)
            g = scores.reshape(shape[0], shape[1] // 4, 4)
            rank = jnp.argsort(jnp.argsort(-jnp.abs(g), axis=-1), axis=-1)
            return (rank < 2).reshape(shape).astype(jnp.float32)
        x12 = jnp.einsum('bsk,mk->bsm', x, w12) + b12
        x1, x2 = jnp.split(x12, 2, axis=-1)
        x4 = jax.nn.silu(x1) * x2
        return jnp.einsum('bsm,nm->bsn', x4, w3) + b3
    x = x + _L0_xattn_ref(_layernorm(x, axis=-1), ctx_4096, L0_xattn_x1_scale, L0_xattn_x1_zp, L0_xattn_x2_scale, L0_xattn_x2_zp)
    x = x + _L0_attn_ref(_layernorm(x, axis=-1), L0_attn_in_proj_w, L0_attn_conv_w, L0_attn_conv_b, L0_attn_dt_bias, L0_attn_A_log, L0_attn_D, L0_attn_norm_w, L0_attn_out_proj_w)
    x = x + _L0_ffn_ref(_layernorm(x, axis=-1), L0_ffn_base_W, L0_ffn_router_W, L0_ffn_lora_A, L0_ffn_lora_B)
    x = x + _L1_xattn_ref(ctx_4096, _layernorm(x, axis=-1), L1_xattn_W_lin1, L1_xattn_b_lin1, L1_xattn_W_lin2, L1_xattn_b_lin2, L1_xattn_W_conv1, L1_xattn_W_conv2, L1_xattn_W_conv3)
    x = x + _L1_attn_ref(_layernorm(x, axis=-1), L1_attn_weight, L1_attn_mask)
    x = x + _L1_ffn_ref(_layernorm(x, axis=-1), L1_ffn_w12, L1_ffn_b12, L1_ffn_w3, L1_ffn_b3)
    return x

_drawn_inputs = setup_inputs


def setup_inputs(seed=0):
    import zlib

    import numpy as np

    out = dict(_drawn_inputs(seed))
    spreads = {'L0_attn_D': (1.0, 0.6),
     'L0_attn_norm_w': (1.0, 0.6),
     'L1_xattn_b_lin1': (0.0, 0.8),
     'L1_xattn_b_lin2': (0.0, 0.8)}
    factors = {'L0_attn_conv_b': 8.0,
     'L0_attn_dt_bias': 8.0,
     'L0_attn_A_log': 8.0,
     'L0_ffn_router_W': 8.0,
     'L0_ffn_lora_A': 8.0,
     'L0_ffn_lora_B': 8.0,
     'L1_xattn_W_lin1': 2.986,
     'L1_xattn_W_lin2': 3.415,
     'L1_xattn_W_conv1': 2.961,
     'L1_xattn_W_conv2': 3.495,
     'L1_attn_weight': 3.472,
     'L1_ffn_w12': 5.531,
     'L1_ffn_b12': 8.0,
     'L1_ffn_w3': 5.481,
     'L1_ffn_b3': 8.0}
    for name, (base, spread) in spreads.items():
        noise = np.random.default_rng([zlib.crc32(name.encode()), seed]).standard_normal(out[name].shape)
        drawn = base * np.exp(spread * noise) if base else spread * noise
        out[name] = jnp.asarray(drawn.astype(out[name].dtype))
    for name, factor in factors.items():
        out[name] = (out[name] * factor).astype(out[name].dtype)
    return out
```

```python
from contextlib import ExitStack

import concourse.bass as bass
from concourse import mybir

F32 = mybir.dt.float32
F16 = mybir.dt.float16
BF16 = mybir.dt.bfloat16
I32 = mybir.dt.int32
ALU = mybir.AluOpType
ACT = mybir.ActivationFunctionType
AX = mybir.AxisListType.X

P = 128
B, L, D = 2, 64, 1024
T = B * L
KC = D // P
HALF = 512
EPS = 1e-5
ROUND = 12582912.0
QMID = 128.0
QMAX = 255.0

NH, HD, NG, NS, CK = 128, 64, 8, 128, 4
DIN = NH * HD
GH = NH // NG
GB = DIN // NG // P
NBLK = DIN // P

NE, RANK = 8, 16
ER = NE * RANK

N = 1024
C = 64
NM = 4
WIN = 10
NHEAD = 4
CH = C // NHEAD
NT = N // P
BITS = 10


def fcopy(ap, dims, offset=0):
    return bass.AP(tensor=ap.tensor, offset=ap.offset + offset, ap=[list(ap.ap[0])] + [list(d) for d in dims])


class Kit:

    def __init__(self, nc, ctx):
        self.nc, self.ctx = nc, ctx

    def sb(self, name, shape, dt, ctx=None):
        return (ctx or self.ctx).enter_context(self.nc.sbuf_tensor(name, shape, dt))

    def sem(self, name):
        return self.ctx.enter_context(self.nc.semaphore(name))


class Norm:

    def __init__(self, k, nth):
        self.stat, self.std, self.turned, self.copied = k.norm_stat, k.norm_std, k.norm_turned, k.norm_copied
        self.stats = lambda count: 5 * nth + count
        self.stds = nth + 1
        self.turns = lambda count: 2 * nth - 2 + count
        self.copies = 2 * nth


def norm_vector(nc, v, k, n):
    for i in range(2):
        nc.vector.bn_stats(k.bn[:, i, :], k.x[:, i * HALF:(i + 1) * HALF]).then_inc(n.stat, 1)
    v.wait_ge(n.stat, n.stats(2))
    nc.vector.bn_aggr(k.mv[:, :], k.bn[:, :, :]).then_inc(n.stat, 1)
    v.wait_ge(n.std, n.stds)
    nc.vector.reciprocal(k.rstd[:, :], k.std[:, :]).then_inc(n.stat, 1)
    v.wait_ge(n.stat, n.stats(4))
    nc.vector.tensor_scalar(k.h[:, :], k.x[:, :], k.mv[:, 0:1], k.rstd[:, 0:1], ALU.subtract, ALU.mult).then_inc(n.stat, 1)


def norm_scalar(nc, act, k, n):
    act.wait_ge(n.stat, n.stats(3))
    nc.scalar.activation(k.std[:, :], k.mv[:, 1:2], ACT.Sqrt, bias=k.eps[:, 0:1]).then_inc(n.std, 1)


def norm_tensor(nc, pe, k, n, banks=(0, 1)):
    pe.wait_ge(n.stat, n.stats(5))
    for i in range(2):
        for j in range(4):
            c = 4 * i + j
            mm = nc.tensor.transpose(k.ps[:, banks[i], j * P:(j + 1) * P], k.h[:, c * P:(c + 1) * P], k.ident[:, :])
        mm.then_inc(n.turned, 1)


def norm_copy_scalar(nc, act, k, n, banks=(0, 1)):
    act.wait_ge(n.turned, n.turns(1))
    nc.scalar.copy(k.hT[:, 0:4, :], k.ps[:, banks[0], :].rearrange("p (c t) -> p c t", t=P)).then_inc(n.copied, 1)


def norm_copy_vector(nc, v, k, n, banks=(0, 1)):
    v.wait_ge(n.turned, n.turns(2))
    nc.vector.tensor_copy(k.hT[:, 4:8, :], k.ps[:, banks[1], :].rearrange("p (c t) -> p c t", t=P)).then_inc(n.copied, 1)


def stage_quantised_product(nc, k, dr):
    CHUNKS, BUFS, KPC = 8, 4, 2
    with ExitStack() as ctx:
        cbuf = k.sb("ctx_chunks", [P, BUFS, KPC, D], F32, ctx)
        q2 = k.sb("q2", [P, B, KC, D], BF16, ctx)
        q1f = k.sb("q1f", [P, D], F32, ctx)
        q1 = k.sb("q1", [P, D], BF16, ctx)
        q1z = k.sb("q1z", [P, B, KC, T], BF16, ctx)
        onesz = k.sb("onesz", [P, B, T], BF16, ctx)
        sc = k.sb("scales", [P, 4], F32, ctx)
        rec = k.sb("rec", [P, 2], F32, ctx)
        off = k.sb("off", [P, 2], F32, ctx)
        s12 = k.sb("s12", [P, 1], F32, ctx)
        rsum = k.sb("rsum", [P, 1], F32, ctx)
        rowb = k.sb("rowb", [P, 2], F32, ctx)
        crow = k.sb("crow", [B * 3 * NT, P], F32, ctx)
        tsum = k.sb("tsum", [P, D], F32, ctx)

        s_x, s_sc, s_co = k.sem("q_x_in"), k.sem("q_scales_in"), k.sem("q_coords_in")
        s_ctx = [k.sem(f"q_ctx_in{i}") for i in range(BUFS)]
        s_const, s_const0 = k.sem("q_const"), k.sem("q_const0")
        s_prm, s_aff, s_clip, s_q2 = k.sem("q_params"), k.sem("q_affine"), k.sem("q_clip"), k.sem("q_q2")
        s_q1, s_q1t, s_q1z = k.sem("q_q1"), k.sem("q_q1t"), k.sem("q_q1z")
        s_mm, s_fin = k.sem("q_mm"), k.sem("q_fin")
        s_ct = k.sem("q_coords_turned")
        n = Norm(k, 0)
        acc = lambda h: k.ps[:, 2 + h, :]
        csum = lambda h: k.ps[:, 4 + h, :]

        block = ctx.enter_context(nc.Block())

        @block.sync
        def _(sp):
            sp.dma_start(k.x[:, :], dr["x"]).then_inc(s_x, 16)
            for i, name in enumerate(("L0_xattn_x1_scale", "L0_xattn_x1_zp", "L0_xattn_x2_scale", "L0_xattn_x2_zp")):
                sp.dma_start(sc[:, i:i + 1], dr[name].partition_broadcast(P)).then_inc(s_sc, 16)
            for b in range(B):
                sp.dma_start(crow[b * 3 * NT:(b + 1) * 3 * NT, :],
                             dr["ctx_4096"][b, 0:3, :].rearrange("c (t p) -> (c t) p", p=P)).then_inc(s_co, 16)
            for c in range(CHUNKS):
                if c >= BUFS:
                    sp.wait_ge(s_q2, c - BUFS + 1)
                b, kc = c // (CHUNKS // B), c % (CHUNKS // B) * KPC
                sp.dma_start(cbuf[:, c % BUFS], dr["ctx_4096"][b, kc * P:(kc + KPC) * P, :]
                             .rearrange("(k p) n -> p k n", p=P)).then_inc(s_ctx[c % BUFS], 16)
            sp.dma_start(k.ring[:, 16, :], dr["w_in"][144]).then_inc(k.ring_in[4], 16)
            for j in range(4):
                sp.dma_start(k.ring[:, 4 * j:4 * j + 4, :],
                             dr["w_in"][128 + 4 * j:132 + 4 * j].rearrange("j p c -> p j c")).then_inc(k.ring_in[j], 16)

        @block.gpsimd
        def _(pool):
            nc.gpsimd.memset(k.ident[:, :], 0.0).then_inc(s_const0, 1)
            nc.gpsimd.memset(k.identb[:, :], 0.0).then_inc(s_const0, 1)
            nc.gpsimd.memset(k.identh[:, :], 0.0).then_inc(s_const0, 1)
            nc.gpsimd.memset(k.eps[:, :], EPS).then_inc(s_const0, 1)
            pool.wait_ge(s_const0, 3)
            for m in (k.ident, k.identb, k.identh):
                nc.gpsimd.affine_select(out=m[:, :], in_=m[:, :], compare_op=ALU.not_equal, fill=1.0, base=0,
                                        pattern=[[-1, P]], channel_multiplier=1).then_inc(s_const, 1)
            nc.gpsimd.memset(q1z[:, :, :, :], 0.0).then_inc(s_const, 1)
            nc.gpsimd.memset(onesz[:, :, :], 0.0).then_inc(s_const0, 1)
            pool.wait_ge(s_const0, 5)
            for b in range(B):
                nc.gpsimd.memset(onesz[:, b, b * L:(b + 1) * L], 1.0).then_inc(s_const, 1)

        @block.vector
        def _(v):
            v.wait_ge(s_x, 16)
            norm_vector(nc, v, k, n)
            v.wait_ge(s_sc, 64)
            nc.vector.reciprocal(rec[:, 0:1], sc[:, 0:1]).then_inc(s_prm, 1)
            nc.vector.reciprocal(rec[:, 1:2], sc[:, 2:3]).then_inc(s_prm, 1)
            for i in range(2):
                nc.vector.tensor_scalar(off[:, i:i + 1], sc[:, 2 * i + 1:2 * i + 2], -1.0, QMID, ALU.mult, ALU.add).then_inc(s_prm, 1)
            nc.vector.tensor_tensor(s12[:, :], sc[:, 0:1], sc[:, 2:3], ALU.mult).then_inc(s_prm, 1)
            v.wait_ge(n.stat, n.stats(5))
            v.wait_ge(s_prm, 5)
            nc.vector.tensor_scalar(q1f[:, :], k.h[:, :], rec[:, 0:1], sc[:, 1:2], ALU.mult, ALU.add).then_inc(s_q1, 1)
            v.wait_ge(s_q1, 1)
            nc.vector.tensor_scalar(q1f[:, :], q1f[:, :], 0.0, QMAX, ALU.max, ALU.min).then_inc(s_q1, 1)
            v.wait_ge(s_q1, 2)
            nc.vector.tensor_scalar(q1[:, :], q1f[:, :], ROUND, ROUND + QMID, ALU.add, ALU.subtract).then_inc(s_q1, 1)
            v.wait_ge(s_q1, 3)
            nc.vector.tensor_reduce(rsum[:, :], q1[:, :], AX, ALU.add).then_inc(s_q1, 1)
            nc.vector.tensor_scalar(rowb[:, 0:1], off[:, 0:1], float(D), None, ALU.mult).then_inc(s_q1, 1)
            v.wait_ge(s_q1, 5)
            nc.vector.tensor_scalar(rowb[:, 1:2], rowb[:, 0:1], rsum[:, 0:1], off[:, 1:2], ALU.add, ALU.mult).then_inc(s_q1, 1)
            v.wait_ge(s_ct, 1)
            nc.vector.tensor_copy(k.coord[:, :], k.ps[:, 7, 0:B * 3 * NT]).then_inc(k.coord_ready, 1)
            for c in range(CHUNKS):
                b, kc = c // (CHUNKS // B), c % (CHUNKS // B) * KPC
                buf = cbuf[:, c % BUFS]
                v.wait_ge(s_aff, c + 1)
                nc.vector.tensor_scalar(buf, buf, 0.0, QMAX, ALU.max, ALU.min).then_inc(s_clip, 1)
                v.wait_ge(s_clip, c + 1)
                nc.vector.tensor_scalar(q2[:, b, kc:kc + KPC, :], buf, ROUND, ROUND + QMID, ALU.add, ALU.subtract).then_inc(s_q2, 1)
            v.wait_ge(s_mm, 1)
            v.wait_ge(s_q1, 6)
            for h in range(2):
                cols = slice(h * HALF, (h + 1) * HALF)
                nc.vector.tensor_scalar(tsum[:, cols], csum(h), off[:, 0:1], rowb[:, 1:2], ALU.mult, ALU.add).then_inc(s_fin, 1)
            for h in range(2):
                cols = slice(h * HALF, (h + 1) * HALF)
                v.wait_ge(s_fin, h + 1)
                nc.vector.tensor_tensor(tsum[:, cols], acc(h), tsum[:, cols], ALU.add).then_inc(s_fin, 1)
            for h in range(2):
                cols = slice(h * HALF, (h + 1) * HALF)
                v.wait_ge(s_fin, h + 3)
                nc.vector.scalar_tensor_tensor(out=k.x[:, cols], in0=tsum[:, cols], scalar=s12[:, 0:1], in1=k.x[:, cols],
                                               op0=ALU.mult, op1=ALU.add).then_inc(s_fin, 1)
            v.wait_ge(s_fin, 6)

        @block.scalar
        def _(act):
            act.wait_ge(s_const0, 4)
            norm_scalar(nc, act, k, n)
            act.wait_ge(s_q1t, 1)
            act.wait_ge(s_const, 4)
            turned = k.ps[:, 6, :].bitcast(BF16).rearrange("p (c t) -> p c t", t=T)
            for b in range(B):
                nc.scalar.copy(q1z[:, b, :, b * L:(b + 1) * L], turned[:, :, b * L:(b + 1) * L]).then_inc(s_q1z, 1)
            act.wait_ge(s_prm, 5)
            for c in range(CHUNKS):
                buf = cbuf[:, c % BUFS]
                act.wait_ge(s_ctx[c % BUFS], 16 * (c // BUFS + 1))
                nc.scalar.activation(buf, buf, ACT.Identity, bias=sc[:, 3:4], scale=rec[:, 1:2]).then_inc(s_aff, 1)

        @block.tensor
        def _(pe):
            pe.wait_ge(s_const, 3)
            pe.wait_ge(s_co, 32)
            nc.tensor.transpose(k.ps[:, 7, 0:B * 3 * NT], crow[:, :], k.ident[0:B * 3 * NT, 0:B * 3 * NT]).then_inc(s_ct, 1)
            pe.wait_ge(s_q1, 3)
            turned = k.ps[:, 6, :].bitcast(BF16)
            for c in range(KC):
                mm = nc.tensor.transpose(turned[:, c * P:(c + 1) * P], q1[:, c * P:(c + 1) * P], k.identb[:, :])
            mm.then_inc(s_q1t, 1)
            pe.wait_ge(s_q1z, 2)
            pe.wait_ge(s_const, 6)
            for c in range(CHUNKS):
                b, k0 = c // (CHUNKS // B), c % (CHUNKS // B) * KPC
                pe.wait_ge(s_q2, c + 1)
                for kc in range(k0, k0 + KPC):
                    first, last = b == 0 and kc == 0, b == B - 1 and kc == KC - 1
                    for h in range(2):
                        rhs = q2[:, b, kc, h * HALF:(h + 1) * HALF]
                        nc.tensor.matmul(acc(h), q1z[:, b, kc, :], rhs, start=first, stop=last)
                    for h in range(2):
                        rhs = q2[:, b, kc, h * HALF:(h + 1) * HALF]
                        mm = nc.tensor.matmul(csum(h), onesz[:, b, :], rhs, start=first, stop=last)
            mm.then_inc(s_mm, 1)


KEY_STEPS = 10 + 7 + (BITS - 1) * (3 * 3 + 2 * 4) + 2 + 8 + 8 + 2 + 2


def vector_sort_keys(nc, v, k, w, s_key, s_ext, s_allmax):
    done = [0]

    def link(ins):
        done[0] += 1
        ins.then_inc(s_key, 1)
        v.wait_ge(s_key, done[0])

    vec = nc.vector
    xyz = k.coord[:, :].rearrange("p (b c t) -> p (b c) t", b=B, c=3)
    vec.tensor_reduce(w.ext[:, 0:6], xyz, AX, ALU.max).then_inc(s_ext, 1)
    vec.tensor_reduce(w.ext[:, 6:12], xyz, AX, ALU.min, negate=True).then_inc(s_ext, 1)
    v.wait_ge(s_allmax, 1)
    top, neg = w.allmax[:, 0:6], w.allmax[:, 6:12]
    link(vec.tensor_tensor(w.span[:, :], top, neg, ALU.add))
    link(vec.tensor_scalar(w.span[:, :], w.span[:, :], 1e-6, None, ALU.add))
    link(vec.reciprocal(w.span[:, :], w.span[:, :]))
    link(vec.tensor_scalar(w.span[:, :], w.span[:, :], float(2 ** BITS - 1), None, ALU.mult))
    u = w.u[:, :].rearrange("p (g t) -> p g t", t=NT)
    link(vec.tensor_tensor(u, xyz, fcopy(neg, [[1, 6], [0, NT]]), ALU.add))
    link(vec.tensor_tensor(u, u, fcopy(w.span[:, :], [[1, 6], [0, NT]]), ALU.mult))
    link(vec.tensor_scalar(w.r[:, :], w.u[:, :], 2.0 ** 23, 2.0 ** 23, ALU.add, ALU.subtract))
    link(vec.tensor_tensor(w.u[:, :], w.r[:, :], w.u[:, :], ALU.is_gt))
    link(vec.tensor_tensor(w.r[:, :], w.r[:, :], w.u[:, :], ALU.subtract))
    link(vec.tensor_scalar(w.r[:, :], w.r[:, :], 0.0, float(2 ** BITS - 1), ALU.max, ALU.min))
    r = w.r[:, :].rearrange("p (b c t) -> p b c t", b=B, c=3)
    for var, order in enumerate(((0, 1, 2), (1, 0, 2))):
        for i, c in enumerate(order):
            link(vec.tensor_copy(w.q[:, 0, i, var], r[:, :, c, :]))
    link(vec.tensor_copy(w.q[:, 1], w.q[:, 0]))
    flat = lambda kind, i: w.q[:, kind, i].rearrange("p v b t -> p (v b t)")
    X = [flat(1, i) for i in range(3)]
    t1, m = w.t1[:, :], w.m[:, :]
    SHL, SAR, SHR = ALU.logical_shift_left, ALU.arith_shift_right, ALU.logical_shift_right
    AND, OR, XOR = ALU.bitwise_and, ALU.bitwise_or, ALU.bitwise_xor
    for bit in range(BITS - 1, 0, -1):
        low = (1 << bit) - 1
        for i in range(3):
            link(vec.tensor_scalar(m, X[i], 31 - bit, 31, SHL, SAR))
            link(vec.tensor_scalar(m, m, low, None, AND))
            if i:
                link(vec.tensor_tensor(t1, X[0], X[i], XOR))
                link(vec.scalar_tensor_tensor(out=t1, in0=m, scalar=low, in1=t1, op0=XOR, op1=AND))
                link(vec.tensor_tensor(X[0], X[0], t1, XOR))
                link(vec.tensor_tensor(X[i], X[i], t1, XOR))
            link(vec.tensor_tensor(X[0], X[0], m, XOR))
    for i in (1, 2):
        link(vec.tensor_tensor(X[i], X[i], X[i - 1], XOR))
    link(vec.scalar_tensor_tensor(out=t1, in0=X[2], scalar=1, in1=X[2], op0=SHR, op1=XOR))
    for s in (2, 4, 8):
        link(vec.scalar_tensor_tensor(out=m, in0=t1, scalar=s, in1=t1, op0=SHR, op1=XOR))
        t1, m = m, t1
    link(vec.tensor_scalar(t1, t1, 1, None, SHR))
    for i in range(3):
        link(vec.tensor_tensor(X[i], X[i], t1, XOR))
    q = w.q[:, :].rearrange("p k c v b t -> p (k c v b t)")
    for s, mask in ((16, 0x030000FF), (8, 0x0300F00F), (4, 0x030C30C3), (2, 0x09249249)):
        link(vec.scalar_tensor_tensor(out=w.spread[:, :], in0=q, scalar=s, in1=q, op0=SHL, op1=OR))
        link(vec.tensor_scalar(q, w.spread[:, :], mask, None, AND))
    axis = lambda i: w.q[:, :, i].rearrange("p k v b t -> p k (v b t)")
    key = w.key[:, :].rearrange("p (k g) -> p k g", k=2)
    link(vec.scalar_tensor_tensor(out=key, in0=axis(0), scalar=2, in1=axis(2), op0=SHL, op1=OR))
    link(vec.scalar_tensor_tensor(out=key, in0=axis(1), scalar=1, in1=key, op0=SHL, op1=OR))
    top_bit = 1 << (3 * BITS - 1)
    link(vec.tensor_scalar(w.spread[:, 0:NM * B * NT], w.key[:, :], top_bit, 1, AND, SHL))
    link(vec.scalar_tensor_tensor(out=k.keys[:, :].bitcast(I32), in0=w.key[:, :], scalar=top_bit,
                                  in1=w.spread[:, 0:NM * B * NT], op0=XOR, op1=OR))
    assert done[0] == KEY_STEPS


class Bag:
    pass


def stage_mixer(nc, k, dr):
    TP = L + CK - 1
    NPAR = CK + 3
    G0 = 5
    with ExitStack() as ctx:
        sb = lambda name, shape, dt=F32: k.sb(name, shape, dt, ctx)
        xpad = sb("xpad", [P, GB, B, TP])
        xc = sb("xc", [P, GB, T])
        xsil, sgate = sb("xsil", [P, GB, T]), sb("sgate", [P, GB, T])
        decay = sb("decay", [P, GH, L])
        MT = sb("MT", [P, GH, T])
        seg_rhs = sb("seg_rhs", [P, GH, L])
        xs = sb("xs", [P, GH * HD])
        z, y, ysq, yn = (sb(f"y_{i}", [P, GB, T]) for i in "zysn")
        BT, CT = sb("BT", [P, NG, T]), sb("CT", [P, NG, T])
        gm = sb("gm", [P, NG, L])
        par, parg = sb("par", [P, NG, GB * NPAR]), sb("parg", [P, GB, NPAR])
        parbc = sb("parbc", [P, 2 * NG, CK + 1])
        hp, ea = sb("head_par", [P, 2]), sb("exp_A", [P, 1])
        dtr, dta, dte, dts, dtp, dtq = (sb(f"dt_{i}", [P, T]) for i in "raespq")
        dt_tok, adt_tok = sb("dt_tok", [P, NH]), sb("adt_tok", [P, NH])
        tri_le, tri_gt, tri_s = sb("tri_le", [P, L]), sb("tri_gt", [P, T]), sb("tri_s", [P, P])
        ones = sb("ones_col", [P, 1])
        gstd, grs = sb("group_std", [P, 1]), sb("group_rs", [P, 1])
        krow = sb("krow", [P, N])
        junk, junk_eq = sb("junk", [P, 2, N], BF16), sb("junk_eq", [P, 2, P], BF16)
        kcol, racc = sb("kcol", [P, NT]), sb("racc", [P, NT, 3])
        krows = sb("krows", [NM * B * NT, P])
        mchunk = sb("mchunk", [P, D], I32)
        w = Bag()
        w.ext, w.allmax, w.span = sb("w_ext", [P, 12]), sb("w_allmax", [P, 12]), sb("w_span", [P, 6])
        w.u, w.r = sb("w_u", [P, 48]), sb("w_r", [P, 48])
        w.q = sb("w_q", [P, 2, 3, 2, B, NT], I32)
        w.t1, w.m = sb("w_t1", [P, 32], I32), sb("w_m", [P, 32], I32)
        w.spread, w.key = sb("w_spread", [P, 192], I32), sb("w_key", [P, 64], I32)

        sem = lambda name: k.sem(f"m_{name}")
        s_par, s_const, s_const0 = sem("params_in"), sem("const"), sem("const0")
        s_proj, s_evac = sem("proj"), sem("evac")
        s_cv = sem("conv_step")
        s_silu = sem("silu")
        s_dtr, s_dt, s_dte, s_dtt, s_dtc = sem("dt_raw"), sem("dt"), sem("dt_exp"), sem("dt_turned"), sem("dt_tok")
        s_gp, s_gm = sem("gram"), sem("gram_masked")
        s_key, s_ext, s_allmax, s_kt, s_kr = sem("key_step"), sem("extremes"), sem("allmax"), sem("keys_turned"), sem("key_rows")
        s_kd, s_krow, s_mch = sem("keys_stored"), sem("krow_in"), sem("mask_in")
        s_rk, s_msum = sem("rank_step"), sem("mask_sum")
        s_rhs, s_seg, s_dec, s_M = sem("seg_rhs"), sem("seg"), sem("decay"), sem("M")
        s_xT, s_xs, s_Y, s_z = sem("x_turned"), sem("xs"), sem("Y"), sem("z")
        s_pg, s_y, s_ysq, s_yn = sem("parg"), sem("y"), sem("ysq"), sem("yn")
        s_var, s_out, s_std, s_rs, s_xup = sem("var"), sem("out"), sem("group_std"), sem("group_rs"), sem("x_updated")
        n = Norm(k, 1)
        keyd = nc.dram_tensor("keys_scratch", [NM * B, N], F32).ap()
        ps = k.ps

        def chunk(j):
            return k.ring[:, 4 * j:4 * j + 4, :]

        block = ctx.enter_context(nc.Block())

        @block.sync
        def _(sp):
            sp.dma_start(par[:, :, :], dr["par"]).then_inc(s_par, 16)
            sp.dma_start(parbc[:, :, :], dr["par_bc"]).then_inc(s_par, 16)
            sp.dma_start(hp[:, :], dr["head_par"]).then_inc(s_par, 16)

            def load_xg(g, q, first):
                if first:
                    sp.wait_ge(s_proj, q + 2)
                else:
                    sp.wait_ge(s_proj, 4 * g + 2 + q)
                blk = g * GB + 4 * (q % 2) + (NBLK if q < 2 else 0)
                src = dr["w_in"][bass.ds(blk, 4)] if not first else dr["w_in"][blk:blk + 4]
                sp.dma_start(chunk(q), src.rearrange("j p c -> p j c")).then_inc(k.ring_in[q], 16)

            def load_out(g, h, first):
                if first:
                    if h == 0:
                        sp.wait_ge(s_proj, 1)
                else:
                    sp.wait_ge(s_out, 2 * g - 1 + h)
                blk = g * GB + 4 * h
                src = dr["w_out"][blk:blk + 4] if first else dr["w_out"][bass.ds(blk, 4)]
                sp.dma_start(chunk(4 + h), src.rearrange("j p c -> p j c")).then_inc(k.ring_in[4 + h], 16)

            for h in range(2):
                load_out(0, h, True)
            for q in range(4):
                load_xg(0, q, True)
            for q in range(4):
                load_xg(1, q, False)
            with sp.Fori(1, NG - 1) as g:
                for q in range(4):
                    load_xg(g + 1, q, False)
                for h in range(2):
                    load_out(g, h, False)
            for h in range(2):
                load_out(NG - 1, h, False)
            sp.wait_ge(s_proj, G0 + 4 * NG)
            sp.dma_start(k.ring[:, 0:KC, :], dr["base_w"]).then_inc(k.moe_in, 16)
            sp.dma_start(k.ring[:, 8:10, :].rearrange("p a c -> p (a c)")[:, 0:KC * (ER + NE)], dr["lora_a_router"]).then_inc(k.moe_in, 16)
            sp.dma_start(k.ring[:, 10, :], dr["lora_b"]).then_inc(k.moe_in, 16)

        @block.tensor
        def _(pe):
            norm_tensor(nc, pe, k, n)
            pe.wait_ge(n.copied, n.copies)

            def project(c, q, blocks, slot):
                bank = q % 2
                for j in range(blocks):
                    for kc in range(KC):
                        mm = nc.tensor.matmul(ps[:, bank, j * T:(j + 1) * T], k.ring[:, slot + j, kc * P:(kc + 1) * P],
                                              k.hT[:, kc, :], start=kc == 0, stop=kc == KC - 1)
                mm.then_inc(s_proj, 1)

            pe.wait_ge(k.ring_in[4], 16)
            project(0, 0, 1, 16)
            for j in range(4):
                if j >= 1:
                    pe.wait_ge(s_evac, j)
                pe.wait_ge(k.ring_in[j], 16)
                project(1 + j, 1 + j, 4, 4 * j)
            pe.wait_ge(s_dt, 15)
            nc.tensor.transpose(ps[:, 2, 0:P], dtq[:, :], k.ident[:, :])
            nc.tensor.transpose(ps[:, 2, P:2 * P], dta[:, :], k.ident[:, :]).then_inc(s_dtt, 1)

            def out_projection(g):
                pe.wait_ge(s_yn, g + 1)
                for j in range(GB):
                    mm = nc.tensor.matmul(ps[:, 4, 0:1], ysq[:, j, :], ones[:, :], start=j == 0, stop=j == GB - 1)
                mm.then_inc(s_var, 1)
                if not (isinstance(g, int) and g == 0):
                    pe.wait_ge(s_xup, 2 * g)
                for h in range(2):
                    pe.wait_ge(k.ring_in[4 + h], 16 * (g + 2 - h))
                    for j in range(4 * h, 4 * h + 4):
                        for c in range(2):
                            mm = nc.tensor.matmul(ps[:, 6 + c, :], yn[:, j, :], k.ring[:, 16 + j, c * HALF:(c + 1) * HALF],
                                                  start=j == 0, stop=j == GB - 1)
                    mm.then_inc(s_out, 1)

            def group(g, first):
                if first:
                    pe.wait_ge(s_dtc, 2)
                else:
                    pe.wait_ge(s_xs, 2 * g)
                pe.wait_ge(s_rhs, g + 1)
                for h in range(2):
                    mm = nc.tensor.matmul(ps[:, 2 + h, :], tri_gt[:, :], seg_rhs[:, 8 * h:8 * h + 8, :], start=True, stop=True)
                mm.then_inc(s_seg, 1)
                for q in range(4):
                    pe.wait_ge(s_evac, 4 * g + G0 + q - 1)
                    pe.wait_ge(k.ring_in[q], 16 * (g + 2))
                    project(None, G0 + q, 4, 4 * q)
                if first:
                    pe.wait_ge(s_silu, 4)
                    for gg in range(NG):
                        for b in range(B):
                            mm = nc.tensor.matmul(ps[b * L:(b + 1) * L, 4, gg * L:(gg + 1) * L], BT[:, gg, b * L:(b + 1) * L],
                                                  CT[:, gg, b * L:(b + 1) * L], start=True, stop=True)
                    mm.then_inc(s_gp, 1)
                    pe.wait_ge(s_dec, 1)
                    pe.wait_ge(s_key, KEY_STEPS)
                    nc.tensor.transpose(ps[0:NM * B * NT, 3, 0:P], k.keys[:, :], k.ident[:, :]).then_inc(s_kt, 1)
                    pe.wait_ge(s_kr, 1)
                    pe.wait_ge(s_gm, 1)
                else:
                    out_projection(g - 1)
                pe.wait_ge(s_dec, g + 1)
                for j in range(GB):
                    pe.wait_ge(s_silu, 2 * g + 4 + j // 4 + 1)
                    mm = nc.tensor.transpose(ps[:, 2 + j // 4, j % 4 * P:(j % 4 + 1) * P], xsil[:, j, :], k.ident[:, :])
                    if j % 4 == 3:
                        mm.then_inc(s_xT, 1)
                pe.wait_ge(s_M, 2 * g + 2)
                pe.wait_ge(s_xs, 2 * g + 2)
                if not first:
                    pe.wait_ge(s_z, 8 * g)
                    pe.wait_ge(s_std, g)
                for h in range(GH):
                    j = h // 2
                    mm = nc.tensor.matmul(ps[h % 2 * HD:(h % 2 + 1) * HD, 4 + j // 4, j % 4 * T:(j % 4 + 1) * T],
                                          xs[:, h * HD:(h + 1) * HD], MT[:, h, :], start=True, stop=True)
                mm.then_inc(s_Y, 1)

            pe.wait_ge(s_const, 10)
            group(0, True)
            with pe.Fori(1, NG) as g:
                group(g, False)
            out_projection(NG - 1)

        @block.scalar
        def _(act):
            norm_scalar(nc, act, k, n)
            norm_copy_scalar(nc, act, k, n)
            act.wait_ge(s_par, 48)
            nc.scalar.activation(ea[:, :], hp[:, 1:2], ACT.Exp).then_inc(s_dtr, 1)
            act.wait_ge(s_proj, 1)
            nc.scalar.activation(dtr[:, :], ps[:, 0, 0:T], ACT.Identity, bias=hp[:, 0:1]).then_inc(s_evac, 1)
            act.wait_ge(s_dt, 1)
            nc.scalar.activation(dte[:, :], dta[:, :], ACT.Exp, scale=-1.0).then_inc(s_dte, 1)
            act.wait_ge(s_const, 10)

            def pad(bank, half):
                for b in range(B):
                    ins = nc.scalar.copy(xpad[:, 4 * half:4 * half + 4, b, CK - 1:TP],
                                         ps[:, bank, :].rearrange("p (j t) -> p j t", t=T)[:, :, b * L:(b + 1) * L])
                ins.then_inc(s_evac, 1)

            def silu(dst, half, c):
                act.wait_ge(s_cv, 16 * c)
                nc.scalar.activation(dst, xc[:, 4 * half:4 * half + 4, :], ACT.Silu).then_inc(s_silu, 1)

            for j in range(4):
                act.wait_ge(s_proj, 2 + j)
                if j >= 2:
                    act.wait_ge(s_cv, 16 * (j - 1))
                pad((1 + j) % 2, j % 2)
                if j >= 1:
                    i = j - 1
                    silu((BT if i < 2 else CT)[:, 4 * (i % 2):4 * (i % 2) + 4, :], i % 2, i + 1)
            silu(CT[:, 4:8, :], 1, 4)

            def after_out(g):
                act.wait_ge(s_var, g + 1)
                nc.scalar.activation(gstd[:, :], ps[:, 4, 0:1], ACT.Sqrt, bias=k.eps[:, 0:1], scale=1.0 / (GB * P)).then_inc(s_std, 1)

            def group(g, first):
                act.wait_ge(s_seg, g + 1)
                if not first:
                    act.wait_ge(s_M, 2 * g)
                nc.scalar.activation(decay[:, :, :].rearrange("p h l -> p (h l)"),
                                     ps[:, 2:4, :].rearrange("p a c -> p (a c)"), ACT.Exp).then_inc(s_dec, 1)
                for h in range(2):
                    act.wait_ge(s_proj, 4 * g + G0 + h + 1)
                    act.wait_ge(s_cv, 32 * g + 16 * (3 + h))
                    pad((G0 + h) % 2, h)
                for h in range(2):
                    act.wait_ge(s_proj, 4 * g + G0 + 2 + h + 1)
                    if not first:
                        act.wait_ge(s_y, g)
                    nc.scalar.activation(sgate[:, 4 * h:4 * h + 4, :].rearrange("p j t -> p (j t)"), ps[:, (G0 + h) % 2, :],
                                         ACT.Silu).then_inc(s_evac, 1)
                    if not first:
                        act.wait_ge(s_z, 8 * g)
                    silu(xsil[:, 4 * h:4 * h + 4, :], h, 2 * g + 5 + h)
                if not first:
                    after_out(g - 1)
                act.wait_ge(s_y, g + 1)
                if not first:
                    act.wait_ge(s_out, 2 * g)
                nc.scalar.activation(ysq[:, :, :], y[:, :, :], ACT.Square).then_inc(s_ysq, 1)
                for j in range(GB):
                    ins = nc.scalar.mul(yn[:, j, :], y[:, j, :], parg[:, j, CK + 2:CK + 3])
                ins.then_inc(s_yn, 1)

            group(0, True)
            with act.Fori(1, NG) as g:
                group(g, False)
            after_out(NG - 1)

        @block.vector
        def _(v):
            norm_vector(nc, v, k, n)
            norm_copy_vector(nc, v, k, n)
            vec = nc.vector
            v.wait_ge(s_evac, 1)
            vec.scalar_tensor_tensor(out=dta[:, :], in0=dtr[:, :], scalar=-1.0, in1=dtr[:, :], op0=ALU.mult, op1=ALU.max).then_inc(s_dt, 1)
            v.wait_ge(s_dte, 1)
            vec.tensor_scalar(dts[:, :], dte[:, :], 2.0, None, ALU.add).then_inc(s_dt, 1)
            v.wait_ge(s_dt, 2)
            vec.reciprocal(dts[:, :], dts[:, :]).then_inc(s_dt, 1)
            v.wait_ge(s_dt, 3)
            vec.tensor_tensor(dts[:, :], dts[:, :], dte[:, :], ALU.mult).then_inc(s_dt, 1)
            v.wait_ge(s_dt, 4)
            vec.tensor_tensor(dtp[:, :], dts[:, :], dts[:, :], ALU.mult).then_inc(s_dt, 1)
            v.wait_ge(s_dt, 5)
            vec.tensor_scalar(dtq[:, :], dtp[:, :], 1.0 / 15, None, ALU.mult).then_inc(s_dt, 1)
            for i, c in enumerate((13, 11, 9, 7, 5, 3)):
                v.wait_ge(s_dt, 6 + i)
                vec.scalar_tensor_tensor(out=dtq[:, :], in0=dtq[:, :], scalar=1.0 / c, in1=dtp[:, :], op0=ALU.add,
                                         op1=ALU.mult).then_inc(s_dt, 1)
            v.wait_ge(s_dt, 12)
            vec.scalar_tensor_tensor(out=dtq[:, :], in0=dtq[:, :], scalar=1.0, in1=dts[:, :], op0=ALU.add, op1=ALU.mult).then_inc(s_dt, 1)
            vec.tensor_scalar(dtr[:, :], dtr[:, :], 0.0, None, ALU.max).then_inc(s_dt, 1)
            v.wait_ge(s_dt, 14)
            vec.scalar_tensor_tensor(out=dtq[:, :], in0=dtq[:, :], scalar=2.0, in1=dtr[:, :], op0=ALU.mult, op1=ALU.add).then_inc(s_dtr, 1)
            v.wait_ge(s_dtr, 2)
            vec.tensor_scalar(dta[:, :], dtq[:, :], ea[:, 0:1], -1.0, ALU.mult, ALU.mult).then_inc(s_dt, 1)

            def convolve(half, params, c):
                for i in range(CK):
                    tap = CK - 1 - i
                    if i:
                        v.wait_ge(s_cv, 16 * c + 4 * i)
                    for j in range(4):
                        src, dst = xpad[:, 4 * half + j, :, tap:tap + L], xc[:, 4 * half + j, :].rearrange("p (b l) -> p b l", b=B)
                        if i == 0:
                            ins = vec.tensor_scalar(dst, src, params(j, tap), params(j, CK), ALU.mult, ALU.add)
                        else:
                            ins = vec.scalar_tensor_tensor(out=dst, in0=src, scalar=params(j, tap), in1=dst, op0=ALU.mult, op1=ALU.add)
                        ins.then_inc(s_cv, 1)

            v.wait_ge(s_par, 48)
            for j in range(4):
                v.wait_ge(s_evac, 2 + j)
                if j >= 2:
                    v.wait_ge(s_silu, j - 1)
                convolve(j % 2, lambda i, c: parbc[:, 4 * j + i, c:c + 1], j)
            v.wait_ge(s_dtt, 1)
            vec.tensor_copy(dt_tok[:, :], ps[:, 2, 0:P]).then_inc(s_dtc, 1)
            vec.tensor_copy(adt_tok[:, :], ps[:, 2, P:2 * P]).then_inc(s_dtc, 1)
            vector_sort_keys(nc, v, k, w, s_key, s_ext, s_allmax)
            v.wait_ge(s_gp, 1)
            v.wait_ge(s_const, 10)
            vec.tensor_tensor(gm[:, :, :], ps[:, 4, :].rearrange("p (g l) -> p g l", g=NG), fcopy(tri_le[:, :], [[0, NG], [1, L]]),
                              ALU.mult).then_inc(s_gm, 1)
            v.wait_ge(s_kt, 1)
            vec.tensor_copy(krows[:, :], ps[0:NM * B * NT, 3, 0:P]).then_inc(s_kr, 1)
            vec.memset(racc[:, :, :], 0.0).then_inc(s_rk, 1)

            def rank(g):
                vec.tensor_copy(kcol[:, :], k.keys[:, bass.ds(g * NT, NT)]).then_inc(s_rk, 1)
                v.wait_ge(s_krow, 16 * (g + 1))
                v.wait_ge(s_rk, 25 * g + 2)
                for t in range(NT):
                    col, u = kcol[:, t:t + 1], t % 2
                    if t >= 2:
                        v.wait_ge(s_rk, 25 * g + 4 + 3 * (t - 2))
                    if t:
                        vec.tensor_scalar(junk[:, u, 0:t * P], krow[:, 0:t * P], col, None, ALU.is_le, ALU.add,
                                          accum_out=racc[:, t, 0:1]).then_inc(s_rk, 1)
                    vec.tensor_scalar(junk[:, u, t * P:N], krow[:, t * P:N], col, None, ALU.is_lt, ALU.add,
                                      accum_out=racc[:, t, 1:2]).then_inc(s_rk, 1)
                    vec.scalar_tensor_tensor(out=junk_eq[:, u, :], in0=krow[:, t * P:(t + 1) * P], scalar=col, in1=tri_s[:, :],
                                             op0=ALU.is_equal, op1=ALU.mult, accum_out=racc[:, t, 2:3]).then_inc(s_rk, 1)
                v.wait_ge(s_rk, 25 * g + 25)
                vec.tensor_reduce(k.rank[:, bass.ds(g * NT, NT)], racc[:, :, :], AX, ALU.add).then_inc(s_rk, 1)
                v.wait_ge(s_mch, 16 * (g + 1))
                vec.tensor_reduce(k.msum[:, bass.ds(g * 32, 32)], mchunk[:, :].rearrange("p (b c) -> p b c", c=32), AX,
                                  ALU.add).then_inc(s_msum, 1)

            def after_out(g, first=False):
                v.wait_ge(s_std, g + 1)
                vec.reciprocal(grs[:, :], gstd[:, :]).then_inc(s_rs, 1)
                v.wait_ge(s_rs, g + 1)
                v.wait_ge(s_out, 2 * g + 2)
                if not (isinstance(g, int) and g == 0):
                    v.wait_ge(s_xup, 2 * g)
                for c in range(2):
                    cols = slice(c * HALF, (c + 1) * HALF)
                    vec.scalar_tensor_tensor(out=k.x[:, cols], in0=ps[:, 6 + c, :], scalar=grs[:, 0:1], in1=k.x[:, cols],
                                             op0=ALU.mult, op1=ALU.add).then_inc(s_xup, 1)

            def group(g, first):
                if not first:
                    v.wait_ge(s_yn, g)
                vec.tensor_copy(parg[:, :, :].rearrange("p j c -> p (j c)"), par[:, bass.ds(g, 1), :].rearrange("p a c -> p (a c)")).then_inc(s_pg, 1)
                v.wait_ge(s_pg, g + 1)
                for h in range(2):
                    v.wait_ge(s_evac, 4 * g + G0 + h + 1)
                    v.wait_ge(s_silu, 2 * g + 3 + h)
                    convolve(h, lambda i, c: parg[:, 4 * h + i, c:c + 1], 2 * g + 4 + h)
                v.wait_ge(s_dec, g + 1)
                if not first:
                    v.wait_ge(s_Y, g)
                for b in range(B):
                    tok = slice(b * L, (b + 1) * L)
                    vec.tensor_tensor(MT[tok, :, b * L:(b + 1) * L], decay[tok, :, :],
                                      fcopy(gm[tok, bass.ds(g, 1), :], [[0, GH], [1, L]]), ALU.mult).then_inc(s_M, 1)
                rank(g)
                if not first:
                    after_out(g - 1)
                for h in range(2):
                    v.wait_ge(s_xT, 2 * g + h + 1)
                    vec.tensor_tensor(xs[:, h * HALF:(h + 1) * HALF].rearrange("p (a d) -> p a d", d=HD),
                                      ps[:, 2 + h, :].rearrange("p (a d) -> p a d", d=HD),
                                      fcopy(dt_tok[:, bass.ds(g * GH + 8 * h, 8)], [[1, 8], [0, HD]]), ALU.mult).then_inc(s_xs, 1)
                v.wait_ge(s_Y, g + 1)
                if not first:
                    v.wait_ge(s_y, g)
                for j in range(GB):
                    vec.scalar_tensor_tensor(out=z[:, j, :], in0=xsil[:, j, :], scalar=parg[:, j, CK + 1:CK + 2],
                                             in1=ps[:, 4 + j // 4, j % 4 * T:(j % 4 + 1) * T], op0=ALU.mult, op1=ALU.add).then_inc(s_z, 1)

            group(0, True)
            with v.Fori(1, NG) as g:
                group(g, False)
            after_out(NG - 1)
            v.wait_ge(s_xup, 2 * NG)

        @block.gpsimd
        def _(pool):
            gp = nc.gpsimd
            gp.memset(tri_le[:, :], 1.0).then_inc(s_const0, 1)
            gp.memset(tri_gt[:, :], 0.0).then_inc(s_const0, 1)
            gp.memset(tri_s[:, :], 1.0).then_inc(s_const0, 1)
            gp.memset(ones[:, :], 1.0).then_inc(s_const, 1)
            gp.memset(xpad[:, :, :, :], 0.0).then_inc(s_const, 1)
            gp.memset(MT[:, :, :], 0.0).then_inc(s_const, 1)
            pool.wait_ge(s_const0, 3)
            gp.affine_select(out=tri_s[:, :], in_=tri_s[:, :], compare_op=ALU.is_gt, fill=0.0, base=0,
                             pattern=[[-1, P]], channel_multiplier=1).then_inc(s_const, 1)
            pool.wait_ge(s_const, 4)
            for b in range(B):
                rows, cols = slice(b * L, (b + 1) * L), slice(b * L, (b + 1) * L)
                gp.affine_select(out=tri_le[rows, :], in_=tri_le[rows, :], compare_op=ALU.is_ge, fill=0.0, base=0,
                                 pattern=[[1, L]], channel_multiplier=-1).then_inc(s_const, 1)
                pool.wait_ge(s_const, 5 + 3 * b)
                gp.memset(tri_gt[rows, cols], 1.0).then_inc(s_const, 1)
                pool.wait_ge(s_const, 6 + 3 * b)
                gp.affine_select(out=tri_gt[rows, cols], in_=tri_gt[rows, cols], compare_op=ALU.is_gt, fill=0.0, base=0,
                                 pattern=[[-1, L]], channel_multiplier=1).then_inc(s_const, 1)
                pool.wait_ge(s_const, 7 + 3 * b)

            def scaled_steps(g, first):
                if first:
                    pool.wait_ge(s_dtc, 2)
                else:
                    pool.wait_ge(s_seg, g)
                gp.tensor_tensor(seg_rhs[:, :, :], fcopy(adt_tok[:, bass.ds(g * GH, GH)], [[1, GH], [0, L]]),
                                 fcopy(tri_le[:, :], [[0, GH], [1, L]]), ALU.mult).then_inc(s_rhs, 1)

            def load_keys(g, first):
                if not first:
                    pool.wait_ge(s_rk, 25 * g + 1)
                    pool.wait_ge(s_msum, g)
                row = keyd[bass.ds(g, 1), :]
                pool.dma_start(krow[:, :], bass.AP(tensor=row.tensor, offset=row.offset, ap=[[0, P], [1, N]])).then_inc(s_krow, 16)
                pool.dma_start(mchunk[:, :], dr["mask_t"][bass.ds(g * P, P), :]).then_inc(s_mch, 16)

            def gated(g, first):
                pool.wait_ge(s_z, 8 * g + 8)
                if not first:
                    pool.wait_ge(s_yn, g)
                gp.tensor_tensor(y[:, :, :].rearrange("p j t -> p (j t)"), z[:, :, :].rearrange("p j t -> p (j t)"),
                                 sgate[:, :, :].rearrange("p j t -> p (j t)"), ALU.mult).then_inc(s_y, 1)

            pool.wait_ge(s_ext, 2)
            gp.partition_all_reduce(w.allmax[:, :], w.ext[:, :], P, bass.bass_isa.ReduceOp.max).then_inc(s_allmax, 1)
            scaled_steps(0, True)
            pool.wait_ge(s_kr, 1)
            pool.dma_start(keyd.rearrange("m (t p) -> (m t) p", p=P), krows[:, :]).then_inc(s_kd, 16)
            pool.wait_ge(s_kd, 16)
            load_keys(0, True)
            scaled_steps(1, False)
            load_keys(1, False)
            gated(0, True)
            with pool.Fori(1, NG - 1) as g:
                scaled_steps(g + 1, False)
                load_keys(g + 1, False)
                gated(g, False)
            gated(NG - 1, False)


def stage_lora_experts(nc, k):
    SCALING = 2.0
    with ExitStack() as ctx:
        sb = lambda name, shape, dt=F32: k.sb(name, shape, dt, ctx)
        prob, nmax, esum, ersum = sb("prob", [P, NE]), sb("nmax", [P, 1]), sb("esum", [P, 1]), sb("ersum", [P, 1])
        gt, eq, before = sb("gt", [P, NE, NE]), sb("eq", [P, NE, NE]), sb("before", [P, NE, NE])
        place, wsel = sb("place", [P, NE]), sb("wsel", [P, NE])
        mid, midT = sb("mid", [P, ER]), sb("midT", [P, T])
        sem = lambda name: k.sem(f"e_{name}")
        s_c, s_lr, s_base, s_exp, s_r = sem("const"), sem("logits"), sem("base"), sem("exp"), sem("route")
        s_mt, s_mc, s_out, s_x = sem("mid_turned"), sem("mid_copied"), sem("out"), sem("x")
        n = Norm(k, 2)
        ps = k.ps
        lar = k.ring[:, 8:10, :].rearrange("p a c -> p (a c)")[:, 0:KC * (ER + NE)].rearrange("p (k e) -> p k e", k=KC)
        block = ctx.enter_context(nc.Block())

        @block.tensor
        def _(pe):
            norm_tensor(nc, pe, k, n)
            pe.wait_ge(n.copied, n.copies)
            pe.wait_ge(k.moe_in, 48)
            for kc in range(KC):
                mm = nc.tensor.matmul(ps[:, 2, 0:ER + NE], k.hT[:, kc, :], lar[:, kc, :], start=kc == 0, stop=kc == KC - 1)
            mm.then_inc(s_lr, 1)
            for kc in range(KC):
                for c in range(2):
                    mm = nc.tensor.matmul(ps[:, 3 + c, :], k.hT[:, kc, :], k.ring[:, kc, c * HALF:(c + 1) * HALF],
                                          start=kc == 0, stop=False)
            pe.wait_ge(s_r, 12)
            nc.tensor.transpose(ps[:, 5, 0:P], mid[:, :], k.ident[:, :]).then_inc(s_mt, 1)
            pe.wait_ge(s_mc, 1)
            for c in range(2):
                mm = nc.tensor.matmul(ps[:, 3 + c, :], midT[:, :], k.ring[:, 10, c * HALF:(c + 1) * HALF], start=False, stop=True)
            mm.then_inc(s_out, 1)

        @block.scalar
        def _(act):
            norm_scalar(nc, act, k, n)
            norm_copy_scalar(nc, act, k, n)
            act.wait_ge(s_r, 1)
            nc.scalar.activation(prob[:, :], ps[:, 2, ER:ER + NE], ACT.Exp, bias=nmax[:, 0:1], accum_out=esum[:, 0:1]).then_inc(s_exp, 1)
            act.wait_ge(s_mt, 1)
            nc.scalar.copy(midT[:, :], ps[:, 5, 0:P]).then_inc(s_mc, 1)

        @block.vector
        def _(v):
            norm_vector(nc, v, k, n)
            norm_copy_vector(nc, v, k, n)
            vec = nc.vector
            done = [0]

            def link(ins):
                done[0] += 1
                ins.then_inc(s_r, 1)
                v.wait_ge(s_r, done[0])

            v.wait_ge(s_lr, 1)
            link(vec.tensor_reduce(nmax[:, :], ps[:, 2, ER:ER + NE], AX, ALU.max, negate=True))
            v.wait_ge(s_exp, 1)
            link(vec.reciprocal(ersum[:, :], esum[:, :]))
            link(vec.tensor_scalar(prob[:, :], prob[:, :], ersum[:, 0:1], None, ALU.mult))
            other, own = fcopy(prob[:, :], [[0, NE], [1, NE]]), fcopy(prob[:, :], [[1, NE], [0, NE]])
            link(vec.tensor_tensor(gt[:, :, :], other, own, ALU.is_gt))
            link(vec.tensor_tensor(eq[:, :, :], other, own, ALU.is_equal))
            v.wait_ge(s_c, 2)
            link(vec.tensor_tensor(eq[:, :, :], eq[:, :, :], before[:, :, :], ALU.mult))
            link(vec.tensor_tensor(gt[:, :, :], gt[:, :, :], eq[:, :, :], ALU.add))
            link(vec.tensor_reduce(place[:, :], gt[:, :, :], AX, ALU.add))
            link(vec.scalar_tensor_tensor(out=wsel[:, :], in0=place[:, :], scalar=2.0, in1=prob[:, :], op0=ALU.is_lt, op1=ALU.mult))
            link(vec.tensor_reduce(esum[:, :], wsel[:, :], AX, ALU.add))
            link(vec.reciprocal(ersum[:, :], esum[:, :]))
            v.wait_ge(s_r, 11)
            vec.tensor_scalar(wsel[:, :], wsel[:, :], ersum[:, 0:1], SCALING, ALU.mult, ALU.mult).then_inc(s_x, 1)
            v.wait_ge(s_x, 1)
            vec.tensor_tensor(mid[:, :].rearrange("p (e r) -> p e r", e=NE), ps[:, 2, 0:ER].rearrange("p (e r) -> p e r", e=NE),
                              fcopy(wsel[:, :], [[1, NE], [0, RANK]]), ALU.mult).then_inc(s_r, 1)
            v.wait_ge(s_out, 1)
            for c in range(2):
                cols = slice(c * HALF, (c + 1) * HALF)
                vec.tensor_tensor(k.x[:, cols], ps[:, 3 + c, :], k.x[:, cols], ALU.add).then_inc(s_x, 1)
            v.wait_ge(s_x, 3)

        @block.gpsimd
        def _(pool):
            nc.gpsimd.memset(before[:, :, :], 1.0).then_inc(s_c, 1)
            pool.wait_ge(s_c, 1)
            nc.gpsimd.affine_select(out=before[:, :, :], in_=before[:, :, :], compare_op=ALU.is_gt, fill=0.0, base=0,
                                    pattern=[[1, NE], [-1, NE]], channel_multiplier=0).then_inc(s_c, 1)


def stage_sparse_linear_and_ffn(nc, k, dr, out):
    MB = D // P
    with ExitStack() as ctx:
        sb = lambda name, shape, dt=F32: k.sb(name, shape, dt, ctx)
        w12 = sb("w12", [P, 2 * MB, D])
        b12, b3, ones_row = sb("b12", [P, 2 * MB]), sb("b3", [1, D]), sb("ones_row", [1, P])
        gate, x4 = sb("ffn_gate", [P, MB, T]), sb("x4", [P, MB, T])
        sem = lambda name: k.sem(f"f_{name}")
        s_w12 = [sem(f"w12_in{i}") for i in range(4)]
        s_b, s_c = sem("bias_in"), sem("const")
        s_sp, s_x, s_up, s_gate, s_x4, s_out, s_fin, s_store = (sem(i) for i in ("sparse", "x", "up", "gate", "x4", "out", "fin", "stored"))
        n5, n6 = Norm(k, 4), Norm(k, 5)
        ps = k.ps
        block = ctx.enter_context(nc.Block())

        @block.sync
        def _(sp):
            sp.dma_start(b12[:, :], dr["b12"]).then_inc(s_b, 16)
            sp.dma_start(b3[:, :], dr["L1_ffn_b3"].rearrange("(a d) -> a d", a=1)).then_inc(s_b, 16)
            for i in range(4):
                for half in range(2):
                    blk = half * MB + 2 * i
                    sp.dma_start(w12[:, blk:blk + 2, :], dr["w12"][blk:blk + 2].rearrange("j p c -> p j c")).then_inc(s_w12[i], 16)
            for c in range(2):
                sp.wait_ge(s_fin, c + 1)
                sp.dma_start(out.rearrange("b l d -> (b l) d")[:, c * HALF:(c + 1) * HALF], k.x[:, c * HALF:(c + 1) * HALF]).then_inc(s_store, 16)
            sp.wait_ge(s_store, 32)

        @block.gpsimd
        def _(pool):
            nc.gpsimd.memset(ones_row[:, :], 1.0).then_inc(s_c, 1)

        @block.tensor
        def _(pe):
            norm_tensor(nc, pe, k, n5)
            pe.wait_ge(k.wt_in, 16)
            pe.wait_ge(n5.copied, n5.copies)
            for kc in range(KC):
                for c in range(2):
                    mm = nc.tensor.matmul(ps[:, 2 + c, :], k.hT[:, kc, :], k.wt[:, kc, c * HALF:(c + 1) * HALF],
                                          start=kc == 0, stop=kc == KC - 1)
            mm.then_inc(s_sp, 1)
            norm_tensor(nc, pe, k, n6)
            pe.wait_ge(n6.copied, n6.copies)
            pe.wait_ge(s_x, 2)
            for j in range(MB):
                if j >= 2:
                    pe.wait_ge(s_x4, j - 1)
                if j % 2 == 0:
                    pe.wait_ge(s_w12[j // 2], 32)
                for half in range(2):
                    for kc in range(KC):
                        mm = nc.tensor.matmul(ps[:, 2 + 2 * half + j % 2, 0:T],
                                              w12[:, half * MB + j, kc * P:(kc + 1) * P], k.hT[:, kc, :], start=kc == 0, stop=kc == KC - 1)
                    mm.then_inc(s_up, 1)
            pe.wait_ge(s_c, 1)
            pe.wait_ge(s_b, 32)
            for c in range(2):
                nc.tensor.matmul(ps[:, 6 + c, :], ones_row[:, :], b3[:, c * HALF:(c + 1) * HALF], start=True, stop=False)
            pe.wait_ge(k.w3_in, 16)
            for j in range(MB):
                pe.wait_ge(s_x4, j + 1)
                for c in range(2):
                    mm = nc.tensor.matmul(ps[:, 6 + c, :], x4[:, j, :], k.w3[:, j, c * HALF:(c + 1) * HALF], start=False, stop=j == MB - 1)
            mm.then_inc(s_out, 1)

        @block.scalar
        def _(act):
            norm_scalar(nc, act, k, n5)
            norm_copy_scalar(nc, act, k, n5)
            norm_scalar(nc, act, k, n6)
            norm_copy_scalar(nc, act, k, n6)
            act.wait_ge(s_b, 32)
            for j in range(MB):
                act.wait_ge(s_up, 2 * j + 1)
                nc.scalar.activation(gate[:, j, :], ps[:, 2 + j % 2, 0:T], ACT.Silu, bias=b12[:, j:j + 1]).then_inc(s_gate, 1)

        @block.vector
        def _(v):
            norm_vector(nc, v, k, n5)
            norm_copy_vector(nc, v, k, n5)
            v.wait_ge(s_sp, 1)
            for c in range(2):
                cols = slice(c * HALF, (c + 1) * HALF)
                nc.vector.tensor_tensor(k.x[:, cols], ps[:, 2 + c, :], k.x[:, cols], ALU.add).then_inc(s_x, 1)
            v.wait_ge(s_x, 2)
            norm_vector(nc, v, k, n6)
            norm_copy_vector(nc, v, k, n6)
            v.wait_ge(s_b, 32)
            for j in range(MB):
                v.wait_ge(s_up, 2 * j + 2)
                v.wait_ge(s_gate, j + 1)
                nc.vector.scalar_tensor_tensor(out=x4[:, j, :], in0=ps[:, 4 + j % 2, 0:T], scalar=b12[:, MB + j:MB + j + 1],
                                               in1=gate[:, j, :], op0=ALU.add, op1=ALU.mult).then_inc(s_x4, 1)
            v.wait_ge(s_out, 1)
            for c in range(2):
                cols = slice(c * HALF, (c + 1) * HALF)
                nc.vector.tensor_tensor(k.x[:, cols], ps[:, 6 + c, :], k.x[:, cols], ALU.add).then_inc(s_fin, 1)


STEP, TRIO = 24, 3
STEPS = -(-N // STEP)
LEAD = WIN // 2
ROWS = TRIO * WIN
COLS = STEP * WIN
LASTN = N - LEAD - (STEPS - 1) * STEP + LEAD
REG = LASTN - LEAD
SLOTS = 2 * B * 2
FAR = -1e30


class Cloud:

    def __init__(self, k, ctx):
        sb = lambda name, shape, dt=F32: k.sb(name, shape, dt, ctx)
        self.iota = sb("iota", [P, N])
        self.perm = sb("perm", [P, NT, N], BF16)
        self.spl = sb("split", [P, 3, NT, P], BF16)
        self.f16, self.fc = sb("f16", [P, N], F16), sb("fc", [P, N])
        self.fsg = sb("sorted_rows", [P, NT, 2 * P])
        self.W = N + WIN - 1 - LEAD
        self.fsT = sb("sortedT", [P, 4, self.W])
        self.pre = sb("first_windows", [P, 4, LEAD, WIN])
        self.fTr = sb("centreT", [P, 4, N])
        self.fcl = sb("fc_last", [P, STEP])
        self.X = [sb(f"X{u}", [P, 4, STEP // TRIO * 32], F16) for u in range(2)]
        self.S = [sb(f"S{u}", [P, 2 * SLOTS, ROWS]) for u in range(2)]
        self.mx = [sb(f"mx{u}", [P, 2 * SLOTS]) for u in range(2)]
        self.den = [sb(f"den{u}", [P, 2 * SLOTS]) for u in range(2)]
        self.PP = [sb(f"PP{u}", [P, 2 * SLOTS, 32, 2], F16) for u in range(2)]
        self.PT = [sb(f"PT{u}", [P, 2 * SLOTS, 32, 2], F16) for u in range(2)]
        self.XR = [sb(f"XR{u}", [P, SLOTS, P], F16) for u in range(2)]
        self.OT = [sb(f"OT{u}", [P, 2, B, COLS]) for u in range(2)]
        self.step_sems = [k.sem(f"c_{i}") for i in ("X", "scores", "masked", "max", "shifted", "exp", "den", "P", "P_high", "P_low", "P_turned",
                                                    "X_turned", "X_rows", "PV", "O", "H", "reduced")]
        self.order_sems = [k.sem(f"c_{i}") for i in ("split", "f16", "weight_products", "weights_made", "centre_turned", "centre_copied", "perm",
                                                     "ordered", "rows", "sorted_turned", "sorted_copied", "windows")]
        self.mask = sb("block_mask", [P, ROWS])
        self.stats = sb("stats", [P, B, STEPS, 6])
        self.mvb, self.stdb, self.rsb, self.cb = sb("mvb", [P, B, 2]), sb("stdb", [P, B]), sb("rsb", [P, B]), sb("cb", [P, 1])
        self.f1, self.f2 = sb("f1", [P, N]), sb("f2", [P, B, N])
        self.lin_n, self.lin_c = sb("lin_n", [P, 2, P]), sb("lin_c", [P, NM, P])
        self.sel = sb("repeats", [P, 4, P])
        self.conv, self.blin = sb("conv_t", [P, P]), sb("b_lin", [P, 1])
        self.WN, self.WC = sb("WN", [P, 2, P]), sb("WC", [P, B, P])


def stage_cloud_layer(nc, k, dr, c, layer):
    O = C * layer
    nb = 1 if layer == 1 else B
    with ExitStack() as ctx:
        sem = lambda name: k.sem(f"c{layer}_{name}")
        s_w, s_c, s_sel, s_c0 = sem("weights_in"), sem("const"), sem("repeats"), sem("const0")
        s_turn, s_hT = (k.norm_turned, k.norm_copied) if layer == 1 else (sem("turned"), sem("hT"))
        s_spl, s_f16, s_wp, s_wc, s_ct, s_cc, s_perm, s_ord, s_row, s_st, s_sc, s_fs = c.order_sems
        spl0, f160, wp0, wc0, ct0, cc0, perm0, ord0, row0, st0, sc0, fs0 = ((layer - 1) * i for i in (
            5, 2, 1, 1 + B + 1, 8, 8, B * NM * NT, B * NM * NT, B * NM, 8, 8, 2 * LEAD))
        (s_X, s_S, s_sm, s_max, s_sub, s_E, s_den, s_P, s_hi, s_lo, s_PT, s_xt, s_XR, s_PV, s_O, s_H, s_red) = c.step_sems
        t0 = STEPS * (layer - 1)
        s_end, s_std = sem("end"), sem("std")
        n = Norm(k, 3) if layer == 1 else None
        turns, hT_done = (n.turns, n.copies) if n else (lambda count: count, 2)
        src = k.h if layer == 1 else c.f1
        ps = k.ps
        xt = ps[:, 2, :].bitcast(F16)
        block = ctx.enter_context(nc.Block())

        def walk(eng, body, tail):
            body(0, 0)
            body(1, 1)
            with eng.Fori(1, (STEPS - 1) // 2 - 1) as pair:
                for u in range(2):
                    body(pair * 2 + u, u)
            for it in range(STEPS - 3, STEPS):
                body(it, it % 2)
            tail()

        after = lambda it, lag: not isinstance(it, int) or it >= lag

        @block.sync
        def _(sp):
            sp.dma_start(c.lin_n[:, :, :], dr[f"lin_n{layer}"]).then_inc(s_w, 16)
            sp.dma_start(c.lin_c[:, :, :], dr[f"lin_c{layer}"]).then_inc(s_w, 16)
            sp.dma_start(c.conv[:, :], dr[f"conv_t{layer}"]).then_inc(s_w, 16)
            sp.dma_start(c.blin[:, :], dr[f"b_lin{layer}"]).then_inc(s_w, 16)
            if layer == 1:
                sp.dma_start(k.wt[:, :, :], dr["wt"]).then_inc(k.wt_in, 16)
                sp.dma_start(k.w3[:, :, :], dr["w3"]).then_inc(k.w3_in, 16)

        @block.tensor
        def _(pe):
            if layer == 1:
                norm_tensor(nc, pe, k, n)
            else:
                for i in range(2):
                    for j in range(4):
                        mm = nc.tensor.transpose(ps[:, i, j * P:(j + 1) * P], src[:, (4 * i + j) * P:(4 * i + j + 1) * P], k.ident[:, :])
                    mm.then_inc(s_turn, 1)
            pe.wait_ge(s_w, 64)
            for a in range(2):
                nc.tensor.matmul(ps[:, 6, a * O:(a + 1) * O], c.lin_n[:, a, :], c.conv[:, 0:O], start=True, stop=True)
            for m in range(NM):
                nc.tensor.matmul(ps[:, 6, 2 * O:3 * O], c.lin_c[:, m, :], c.conv[:, 0:O], start=m == 0, stop=m == NM - 1)
            nc.tensor.matmul(ps[:, 6, 3 * P:3 * P + 1], c.conv[:, :], c.blin[:, :], start=True, stop=True).then_inc(s_wp, 1)
            pe.wait_ge(s_hT, hT_done)
            if layer == 1:
                pe.wait_ge(s_sel, 4)
            for g in range(8):
                ab, half = g // 2, g % 2
                if g >= 2:
                    pe.wait_ge(s_cc, cc0 + g - 1)
                nc.tensor.matmul(ps[:, 4 + g % 2, :], c.sel[:, ab, :], src[:, half * HALF:(half + 1) * HALF], start=True, stop=True).then_inc(s_ct, 1)
            pe.wait_ge(s_spl, spl0 + 5)
            for b in range(B):
                for m in range(NM):
                    i = b * NM + m
                    if i >= 2:
                        pe.wait_ge(s_row, row0 + i - 1)
                    for t in range(NT):
                        pe.wait_ge(s_perm, perm0 + i * NT + t + 1)
                        for pt in range(NT):
                            for s in range(3):
                                mm = nc.tensor.matmul(ps[:, i % 2, pt * C:(pt + 1) * C], c.perm[:, t, pt * P:(pt + 1) * P],
                                                      c.spl[:, s, t, b * C:(b + 1) * C], start=t + pt + s == 0,
                                                      stop=t == NT - 1 and pt == NT - 1 and s == 2)
                        mm.then_inc(s_ord, 1)
                pe.wait_ge(s_row, row0 + NM * (b + 1))
                for a in range(2):
                    for half in range(2):
                        g = (b * 2 + a) * 2 + half
                        if g >= 2:
                            pe.wait_ge(s_sc, sc0 + g - 1)
                        for j in range(4):
                            mm = nc.tensor.transpose(ps[:, 2 + half, j * P:(j + 1) * P], c.fsg[:, 4 * half + j, a * P:(a + 1) * P], k.ident[:, :])
                        mm.then_inc(s_st, 1)
            pe.wait_ge(s_cc, cc0 + 8)
            pe.wait_ge(s_sc, sc0 + 8)
            pe.wait_ge(s_wc, wc0 + 4)
            pe.wait_ge(s_f16, f160 + 2)

            def rows_and_scores(it, u):
                pe.wait_ge(s_X, t0 + it + 1)
                if after(it, 1):
                    pe.wait_ge(s_XR, t0 + it)
                    pe.wait_ge(s_sm, t0 + it)
                X = c.X[u]
                for slot in range(SLOTS):
                    ab, G = slot // 2, slot % 2
                    mm = nc.tensor.transpose(xt[:, slot * P:(slot + 1) * P], X[:, ab, G * P:(G + 1) * P], k.identh[:, :])
                mm.then_inc(s_xt, 1)
                for slot in range(SLOTS):
                    ab, G = slot // 2, slot % 2
                    for q in range(4):
                        at = (G * 4 + q) * 32
                        for r in range(2):
                            half = slice(r * C, (r + 1) * C)
                            mm = nc.tensor.matmul(ps[32 * q:32 * q + 32, r, slot * ROWS:(slot + 1) * ROWS], X[half, ab, at:at + 32],
                                                  X[half, ab, at:at + ROWS], start=True, stop=True)
                mm.then_inc(s_S, 1)

            def weighted_rows(it, u):
                XR, PT = c.XR[u], c.PT[u]
                for slot in range(SLOTS):
                    for q in range(4):
                        quad = slice(32 * q, 32 * q + 32)
                        for r in range(2):
                            for part in range(2):
                                mm = nc.tensor.matmul(ps[r * C:(r + 1) * C, 3 + q, slot * ROWS:(slot + 1) * ROWS],
                                                      XR[quad, slot, r * C:(r + 1) * C], PT[quad, r * SLOTS + slot, 0:ROWS, part],
                                                      start=part == 0, stop=part == 1)
                mm.then_inc(s_PV, 1)

            def linear(it, u):
                if after(it, 1):
                    pe.wait_ge(s_red, t0 + it)
                pe.wait_ge(s_O, t0 + it + 1)
                last = isinstance(it, int) and it == STEPS - 1
                centre = c.fcl[:, :] if last else c.fc[:, bass.ds(it * STEP + LEAD, STEP)]
                centre = fcopy(centre, [[1, STEP], [0, WIN]])
                if layer == 1:
                    nc.tensor.matmul(ps[:, 7, 0:COLS], c.WC[:, 0, :], centre, start=True, stop=False)
                    for b in range(B):
                        for a in range(2):
                            mm = nc.tensor.matmul(ps[b * C:(b + 1) * C, 7, 0:COLS], c.WN[:, a, 0:O], c.OT[u][:, a, b, :], start=False, stop=a == 1)
                else:
                    for b in range(B):
                        cols = slice(b * COLS, (b + 1) * COLS)
                        nc.tensor.matmul(ps[:, 7, cols], c.WC[:, b, :], centre, start=True, stop=False)
                        for a in range(2):
                            mm = nc.tensor.matmul(ps[:, 7, cols], c.WN[:, a, :], c.OT[u][:, a, b, :], start=False, stop=a == 1)
                mm.then_inc(s_H, 1)

            def step(it, u):
                rows_and_scores(it, u)
                if after(it, 1):
                    pe.wait_ge(s_PT, t0 + it)
                    if after(it, 2):
                        linear(it - 2, u)
                    weighted_rows(it - 1, 1 - u)

            def tail():
                linear(STEPS - 2, 1)
                pe.wait_ge(s_PT, t0 + STEPS)
                weighted_rows(STEPS - 1, 0)
                linear(STEPS - 1, 0)

            walk(pe, step, tail)

        @block.scalar
        def _(act):
            sc = nc.scalar
            if layer == 1:
                norm_scalar(nc, act, k, n)
            act.wait_ge(s_turn, turns(1))
            sc.copy(k.hT[:, 0:4, :], ps[:, 0, :].rearrange("p (c t) -> p c t", t=P)).then_inc(s_hT, 1)
            act.wait_ge(s_hT, hT_done)
            sc.copy(c.spl[:, 0], k.hT[:, :, :]).then_inc(s_spl, 1)
            act.wait_ge(s_spl, spl0 + 2)
            rest = c.fsg[:, :, 0:P]
            sc.copy(c.spl[:, 1], rest).then_inc(s_spl, 1)
            act.wait_ge(s_spl, spl0 + 4)
            sc.copy(c.spl[:, 2], rest).then_inc(s_spl, 1)
            for g in range(8):
                act.wait_ge(s_ct, ct0 + g + 1)
                sc.copy(c.fTr[:, g // 2, g % 2 * HALF:(g % 2 + 1) * HALF], ps[:, 4 + g % 2, :]).then_inc(s_cc, 1)
            act.wait_ge(s_spl, spl0 + 5)
            for b in range(B):
                for m in range(NM):
                    i = b * NM + m
                    act.wait_ge(s_ord, ord0 + NT * (i + 1))
                    if b and m == 0:
                        act.wait_ge(s_st, st0 + 4)
                    sc.copy(fcopy(c.fsg[:, :, m * CH:], [[2 * P, NT], [C, NHEAD], [1, CH]]),
                            ps[:, i % 2, :].rearrange("p (t h c) -> p t h c", t=NT, h=NHEAD)).then_inc(s_row, 1)
                for a in range(2):
                    for half in range(2):
                        g = (b * 2 + a) * 2 + half
                        act.wait_ge(s_st, st0 + g + 1)
                        sc.copy(c.fsT[:, a * B + b, half * HALF:(half + 1) * HALF], ps[:, 2 + half, :]).then_inc(s_sc, 1)

            def unload(it, u):
                act.wait_ge(s_PV, t0 + it + 1)
                if after(it, 2):
                    act.wait_ge(s_H, t0 + it - 1)
                out = c.OT[u][:, :, :, :].rearrange("p a b n -> p (a b n)")
                sc.copy(fcopy(out, [[ROWS, 4], [4 * ROWS, SLOTS], [1, ROWS]]),
                        ps[:, 3:7, 0:COLS].rearrange("p q (s i) -> p q s i", s=SLOTS)).then_inc(s_O, 1)

            def step(it, u):
                act.wait_ge(s_xt, t0 + it + 1)
                if after(it, 2):
                    act.wait_ge(s_PV, t0 + it - 1)
                sc.copy(c.XR[u][:, :, :].rearrange("p s d -> p (s d)"), xt).then_inc(s_XR, 1)
                act.wait_ge(s_sub, t0 + it + 1)
                S = c.S[u][:, :, :].rearrange("p s i -> p (s i)")
                sc.activation(S, S, ACT.Exp, scale=float((NM * CH) ** -0.5)).then_inc(s_E, 1)
                act.wait_ge(s_P, t0 + it + 1)
                if after(it, 2):
                    act.wait_ge(s_PT, t0 + it - 1)
                sc.copy(c.PP[u][:, :, 0:ROWS, 0], c.S[u][:, :, :]).then_inc(s_hi, 1)
                if after(it, 1):
                    unload(it - 1, 1 - u)

            walk(act, step, lambda: unload(STEPS - 1, 0))
            for b in range(nb):
                act.wait_ge(s_end, nb)
                sc.activation(c.stdb[:, b:b + 1], c.mvb[:, b, 1:2], ACT.Sqrt, bias=k.eps[:, 0:1]).then_inc(s_std, 1)

        @block.vector
        def _(v):
            vec = nc.vector
            if layer == 1:
                norm_vector(nc, v, k, n)
            v.wait_ge(s_turn, turns(2))
            vec.tensor_copy(k.hT[:, 4:8, :], ps[:, 1, :].rearrange("p (c t) -> p c t", t=P)).then_inc(s_hT, 1)
            v.wait_ge(s_hT, hT_done)
            rest = c.fsg[:, :, 0:P]
            v.wait_ge(s_spl, spl0 + 1)
            vec.tensor_tensor(rest, k.hT[:, :, :], c.spl[:, 0], ALU.subtract).then_inc(s_spl, 1)
            v.wait_ge(s_spl, spl0 + 3)
            vec.tensor_tensor(rest, rest, c.spl[:, 1], ALU.subtract).then_inc(s_spl, 1)
            v.wait_ge(s_c, 1)
            v.wait_ge(s_wp, wp0 + 1)
            vec.tensor_copy(c.WN[:, :, 0:O], ps[:, 6, 0:2 * O].rearrange("p (a o) -> p a o", a=2)).then_inc(s_wc, 1)
            for b in range(B):
                rows = slice(b * C, (b + 1) * C)
                dst = c.WC[rows, 0, b * C:(b + 1) * C] if layer == 1 else c.WC[rows, b, :]
                vec.tensor_copy(dst, ps[rows, 6, 2 * O:3 * O]).then_inc(s_wc, 1)
            vec.tensor_copy(c.cb[:, :], ps[:, 6, 3 * P:3 * P + 1]).then_inc(s_wc, 1)
            v.wait_ge(s_c, 2)
            for b in range(B):
                for m in range(NM):
                    i = b * NM + m
                    for t in range(NT):
                        if i:
                            v.wait_ge(s_ord, ord0 + (i - 1) * NT + t + 1)
                        at = (m * B + b) * NT + t
                        vec.tensor_scalar(c.perm[:, t, :], c.iota[:, :], k.rank[:, at:at + 1], None, ALU.is_equal).then_inc(s_perm, 1)
            v.wait_ge(s_sc, sc0 + 8)
            row = c.W
            ends = lambda at, dims: fcopy(c.fsT[:, 0, at:], [[row, 4]] + dims)
            vec.tensor_copy(c.fsT[:, :, N:row], ends(N - 1, [[0, row - N]])).then_inc(s_fs, 1)
            for i in range(LEAD):
                vec.tensor_copy(c.pre[:, :, i, 0:i + LEAD + 1], c.fsT[:, :, 0:i + LEAD + 1]).then_inc(s_fs, 1)
                if i < LEAD - 1:
                    vec.tensor_copy(c.pre[:, :, i, i + LEAD + 1:WIN], ends(i + LEAD, [[0, WIN - i - LEAD - 1]])).then_inc(s_fs, 1)
            v.wait_ge(s_c, 5)

            def reduce(it):
                v.wait_ge(s_H, t0 + it + 1)
                last = isinstance(it, int) and it == STEPS - 1
                cols = LASTN * WIN if last else COLS
                raw = c.f1 if layer == 1 else c.f2
                for b in range(nb):
                    H = ps[:, 7, b * COLS:b * COLS + cols]
                    st = c.stats[:, b, it, :] if isinstance(it, int) else c.stats[:, b, bass.ds(it, 1), :].rearrange("p a s -> p (a s)")
                    vec.bn_stats(st, H)
                    win = H.rearrange("p (n j) -> p n j", j=WIN)
                    out = lambda at, cnt: raw[:, bass.ds(at, cnt)] if layer == 1 else raw[:, b, bass.ds(at, cnt)]
                    if last:
                        vec.tensor_reduce(out(N - REG, REG), win[:, 0:REG, :], AX, ALU.max)
                        ins = vec.tensor_reduce(out(0, LEAD), win[:, REG:LASTN, :], AX, ALU.max)
                    else:
                        ins = vec.tensor_reduce(out(it * STEP + LEAD, STEP), win, AX, ALU.max)
                ins.then_inc(s_red, 1)

            def step(it, u):
                S = c.S[u]
                v.wait_ge(s_S, t0 + it + 1)
                if after(it, 2):
                    v.wait_ge(s_lo, t0 + it - 1)
                vec.tensor_tensor(S[:, :, :].rearrange("p (r s) i -> p r s i", r=2),
                                  ps[:, 0:2, 0:COLS].rearrange("p r (s i) -> p r s i", i=ROWS),
                                  fcopy(c.mask[:, :], [[0, 2], [0, SLOTS], [1, ROWS]]), ALU.add).then_inc(s_sm, 1)
                v.wait_ge(s_sm, t0 + it + 1)
                vec.tensor_reduce(c.mx[u][:, :], S[:, :, :], AX, ALU.max).then_inc(s_max, 1)
                if after(it, 1):
                    turn(it - 1, 1 - u)
                v.wait_ge(s_E, t0 + it + 1)
                vec.tensor_reduce(c.den[u][:, :], S[:, :, :], AX, ALU.add).then_inc(s_den, 1)
                v.wait_ge(s_den, 2 * t0 + it * 2 + 1)
                vec.reciprocal(c.den[u][:, :], c.den[u][:, :]).then_inc(s_den, 1)
                if after(it, 2):
                    reduce(it - 2)

            def turn(it, u):
                v.wait_ge(s_lo, t0 + it + 1)
                if after(it, 2):
                    v.wait_ge(s_PV, t0 + it - 1)
                words = lambda x: x[:, :, :, :].rearrange("p s i w -> p (s i w)").bitcast(F32)
                vec.transpose(words(c.PT[u]), words(c.PP[u])).then_inc(s_PT, 1)

            def tail():
                turn(STEPS - 1, 0)
                reduce(STEPS - 2)
                reduce(STEPS - 1)

            walk(v, step, tail)
            v.wait_ge(s_red, t0 + STEPS)
            for b in range(nb):
                vec.bn_aggr(c.mvb[:, b, :], c.stats[:, b, :, :].rearrange("p s w -> p (s w)")).then_inc(s_end, 1)
            done = nb

            def link(ins):
                nonlocal done
                done += 1
                ins.then_inc(s_end, 1)
                v.wait_ge(s_end, done)

            for b in range(nb):
                raw = c.f1[:, :] if layer == 1 else c.f2[:, b, :]
                v.wait_ge(s_std, b + 1)
                link(vec.reciprocal(c.rsb[:, b:b + 1], c.stdb[:, b:b + 1]))
                link(vec.tensor_scalar(c.mvb[:, b, 0:1], c.mvb[:, b, 0:1], c.cb[:, 0:1], None, ALU.add))
                link(vec.tensor_scalar(raw, raw, c.cb[:, 0:1], c.mvb[:, b, 0:1], ALU.add, ALU.subtract))
                link(vec.tensor_scalar(raw, raw, c.rsb[:, b:b + 1], None, ALU.mult))
                link(vec.scalar_tensor_tensor(out=raw, in0=raw, scalar=0.2, in1=raw, op0=ALU.mult, op1=ALU.max))

        @block.gpsimd
        def _(pool):
            gp = nc.gpsimd
            gp.memset(c.WC[:, :, :], 0.0).then_inc(s_c, 1)
            if layer == 1:
                gp.iota(c.iota[:, :], [[1, N]], base=0, channel_multiplier=0, allow_small_or_imprecise_dtypes=True).then_inc(s_c, 1)
                for a in range(2):
                    for b in range(B):
                        at = b * C + a * 2 * CH
                        gp.tensor_copy(c.sel[:, a * B + b, :].rearrange("p (r m c) -> p r m c", r=2, m=NM),
                                       fcopy(k.ident[:, at:], [[CH, 2], [0, NM], [1, CH]])).then_inc(s_sel, 1)
                gp.memset(c.mask[:, :], 0.0).then_inc(s_c0, 1)
                for u in range(2):
                    gp.memset(c.X[u][:, :, :], 0.0).then_inc(s_c0, 1)
                    gp.memset(c.PP[u][:, :, :, :], 0.0).then_inc(s_c0, 1)
                pool.wait_ge(s_c, 2)
                pool.wait_ge(s_c0, 5)
                for q in range(4):
                    m = c.mask[32 * q:32 * q + 32, :]
                    gp.affine_select(out=m, in_=m, compare_op=ALU.is_ge, fill=FAR, base=0, pattern=[[-WIN, TRIO], [0, WIN]],
                                     channel_multiplier=1).then_inc(s_c0, 1)
                    pool.wait_ge(s_c0, 6 + 2 * q)
                    gp.affine_select(out=m, in_=m, compare_op=ALU.is_ge, fill=FAR, base=WIN - 1, pattern=[[WIN, TRIO], [0, WIN]],
                                     channel_multiplier=-1).then_inc(s_c0, 1)
                    pool.wait_ge(s_c0, 7 + 2 * q)
                gp.memset(c.fcl[:, :], 0.0).then_inc(s_c, 1)
                pool.wait_ge(n.stat, n.stats(5))
            else:
                gp.memset(c.fcl[:, :], 0.0).then_inc(s_c, 1)
                gp.memset(c.X[0][:, :, :], 0.0).then_inc(s_c, 1)
            pool.wait_ge(s_c, 3)
            gp.tensor_copy(c.f16[:, :], src[:, :]).then_inc(s_f16, 1)
            pool.wait_ge(s_f16, f160 + 1)
            gp.tensor_copy(c.fc[:, :], c.f16[:, :]).then_inc(s_f16, 1)
            pool.wait_ge(s_f16, f160 + 2)
            gp.tensor_copy(c.fcl[:, 0:REG], c.fc[:, N - REG:N]).then_inc(s_c, 1)
            gp.tensor_copy(c.fcl[:, REG:LASTN], c.fc[:, 0:LEAD]).then_inc(s_c, 1)
            if layer == 2:
                pool.wait_ge(s_c, 5)
            pool.wait_ge(s_cc, cc0 + 8)
            pool.wait_ge(s_fs, fs0 + 2 * LEAD)

            def differences(it, u):
                if after(it, 2):
                    pool.wait_ge(s_S, t0 + it - 1)
                start, point, trio = [[c.W, 4], [1, WIN]], [[N, 4], [0, WIN]], lambda dims, cnt, step: [dims[0], [TRIO * step, cnt], [step, TRIO], dims[1]]
                full = lambda cnt: [[STEP // TRIO * 32, 4], [32, cnt], [WIN, TRIO], [1, WIN]]
                last = isinstance(it, int) and it == STEPS - 1
                cnt = REG // TRIO if last else STEP // TRIO
                ins = gp.tensor_tensor(fcopy(c.X[u][:, 0, 0:1], full(cnt)),
                                       fcopy(c.fsT[:, 0, bass.ds(it * STEP, 1)], trio(start, cnt, 1)),
                                       fcopy(c.fTr[:, 0, bass.ds(it * STEP + LEAD, 1)], trio(point, cnt, 1)), ALU.subtract)
                if last:
                    gp.memset(c.X[u][:, :, LASTN // TRIO * 32 + LASTN % TRIO * WIN:], 0.0)
                    for i in range(cnt * TRIO, LASTN):
                        at = i // TRIO * 32 + i % TRIO * WIN
                        n0 = it * STEP + LEAD + i if i < REG else i - REG
                        near = c.fsT[:, :, n0 - LEAD:n0 - LEAD + WIN] if i < REG else c.pre[:, :, n0, :]
                        ins = gp.tensor_tensor(c.X[u][:, :, at:at + WIN], near, fcopy(c.fTr[:, 0, n0:n0 + 1], [[N, 4], [0, WIN]]), ALU.subtract)
                ins.then_inc(s_X, 1)

            def step(it, u):
                S = c.S[u][:, :, :]
                over = lambda x: fcopy(x[:, :], [[1, 2 * SLOTS], [0, ROWS]])
                pool.wait_ge(s_max, t0 + it + 1)
                gp.tensor_tensor(S, S, over(c.mx[u]), ALU.subtract).then_inc(s_sub, 1)
                if not (isinstance(it, int) and it == STEPS - 1):
                    differences(it + 1, 1 - u)
                pool.wait_ge(s_den, 2 * t0 + it * 2 + 2)
                gp.tensor_tensor(S, S, over(c.den[u]), ALU.mult).then_inc(s_P, 1)
                pool.wait_ge(s_hi, t0 + it + 1)
                gp.tensor_tensor(c.PP[u][:, :, 0:ROWS, 1], S, c.PP[u][:, :, 0:ROWS, 0], ALU.subtract).then_inc(s_lo, 1)

            differences(0, 0)
            walk(pool, step, lambda: None)


def stage_cloud_output(nc, k, dr, c):
    with ExitStack() as ctx:
        sb = lambda name, shape, dt=F32: k.sb(name, shape, dt, ctx)
        res = c.fc
        conv_d, conv_2 = sb("conv3_diag", [P, 2, P]), sb("conv3_last", [P, C])
        blocks, flag = sb("block_ones", [P, P]), sb("flag", [P, KC * 32])
        stats, mv, std, rs = sb("o_stats", [P, 2, 6]), sb("o_mv", [P, 2]), sb("o_std", [P, 1]), sb("o_rs", [P, 1])
        sem = lambda name: k.sem(f"o_{name}")
        s_c, s_z, s_w, s_h, s_st, s_std, s_x = (sem(i) for i in ("const", "zero", "weights_in", "h", "stat", "std", "x"))
        s_sum, s_flag, s_wt = sem("block_sums"), sem("flags"), sem("masked")
        ps = k.ps
        block = ctx.enter_context(nc.Block())

        @block.sync
        def _(sp):
            sp.dma_start(conv_2[:, :], dr["conv3_last"]).then_inc(s_w, 16)
            sp.wait_ge(s_z, 1)
            for b in range(B):
                rows = slice(b * C, (b + 1) * C)
                sp.dma_start(conv_d[rows, :, rows], dr["conv3_diag"]).then_inc(s_w, 16)

        @block.gpsimd
        def _(pool):
            gp = nc.gpsimd
            gp.memset(conv_d[:, :, :], 0.0).then_inc(s_z, 1)
            gp.memset(blocks[:, :], 0.0).then_inc(s_z, 1)
            pool.wait_ge(s_z, 2)
            for q in range(4):
                gp.memset(blocks[32 * q:32 * q + 32, 32 * q:32 * q + 32], 1.0).then_inc(s_c, 1)
            pool.wait_ge(k.wt_in, 16)
            pool.wait_ge(s_flag, 1)
            pool.wait_ge(s_c, 4)
            w = k.wt[:, :, :].rearrange("p k (n j) -> p (k n) j", j=32)
            gp.tensor_tensor(w, w, fcopy(flag[:, :], [[1, KC * 32], [0, 32]]), ALU.mult).then_inc(s_wt, 1)
            pool.wait_ge(s_wt, 1)

        @block.tensor
        def _(pe):
            pe.wait_ge(s_c, 4)
            nc.tensor.matmul(ps[:, 2, 0:KC * 32], blocks[:, :], k.msum[:, :], start=True, stop=True).then_inc(s_sum, 1)
            pe.wait_ge(s_w, 16 * (1 + B))
            for half in range(2):
                cols = slice(half * HALF, (half + 1) * HALF)
                nc.tensor.matmul(ps[:, half, :], conv_d[:, 0, :], k.h[:, cols], start=True, stop=False)
                nc.tensor.matmul(ps[:, half, :], conv_d[:, 1, :], c.f1[:, cols], start=False, stop=False)
                for b in range(B):
                    mm = nc.tensor.matmul(ps[b * C:(b + 1) * C, half, :], conv_2[:, :], c.f2[:, b, cols], start=False, stop=True)
                mm.then_inc(s_h, 1)

        @block.scalar
        def _(act):
            act.wait_ge(s_st, 3)
            nc.scalar.activation(std[:, :], mv[:, 1:2], ACT.Sqrt, bias=k.eps[:, 0:1]).then_inc(s_std, 1)

        @block.vector
        def _(v):
            vec = nc.vector
            v.wait_ge(s_sum, 1)
            vec.tensor_scalar(flag[:, :], ps[:, 2, 0:KC * 32], 0.0, None, ALU.is_gt).then_inc(s_flag, 1)
            for half in range(2):
                v.wait_ge(s_h, half + 1)
                vec.bn_stats(stats[:, half, :], ps[:, half, :]).then_inc(s_st, 1)
            v.wait_ge(s_st, 2)
            vec.bn_aggr(mv[:, :], stats[:, :, :]).then_inc(s_st, 1)
            v.wait_ge(s_std, 1)
            vec.reciprocal(rs[:, :], std[:, :]).then_inc(s_st, 1)
            v.wait_ge(s_st, 4)
            for half in range(2):
                cols = slice(half * HALF, (half + 1) * HALF)
                vec.tensor_scalar(res[:, cols], ps[:, half, :], mv[:, 0:1], rs[:, 0:1], ALU.subtract, ALU.mult).then_inc(s_st, 1)
            v.wait_ge(s_st, 6)
            vec.scalar_tensor_tensor(out=res[:, :], in0=res[:, :], scalar=0.2, in1=res[:, :], op0=ALU.mult, op1=ALU.max).then_inc(s_st, 1)
            v.wait_ge(s_st, 7)
            vec.tensor_tensor(k.x[:, :], res[:, :], k.x[:, :], ALU.add).then_inc(s_x, 1)
            v.wait_ge(s_x, 1)


def stage_point_cloud(nc, k, dr):
    with ExitStack() as ctx:
        c = Cloud(k, ctx)
        stage_cloud_layer(nc, k, dr, c, 1)
        stage_cloud_layer(nc, k, dr, c, 2)
        stage_cloud_output(nc, k, dr, c)


def host_layout(inp, np):
    a = {n: np.asarray(v) for n, v in inp.items()}
    d = {"x": a["x"].reshape(T, D), "ctx_4096": a["ctx_4096"]}
    for n in ("L0_xattn_x1_scale", "L0_xattn_x1_zp", "L0_xattn_x2_scale", "L0_xattn_x2_zp"):
        d[n] = a[n]
    w = a["L0_attn_in_proj_w"].reshape(-1, P, KC, P)
    d["w_in"] = w.transpose(0, 3, 2, 1).reshape(-1, P, D)
    d["w_out"] = a["L0_attn_out_proj_w"].T.reshape(-1, P, D)
    conv = np.concatenate([a["L0_attn_conv_w"][:, 0, :], a["L0_attn_conv_b"][:, None]], axis=1)
    more = np.stack([np.repeat(a["L0_attn_D"], HD), a["L0_attn_norm_w"]], axis=1)
    par = np.concatenate([conv[:DIN], more], axis=1)
    d["par"] = par.reshape(NG, GB, P, -1).transpose(2, 0, 1, 3).reshape(P, NG, -1)
    d["par_bc"] = conv[DIN:].reshape(2 * NG, P, CK + 1).transpose(1, 0, 2)
    d["head_par"] = np.stack([a["L0_attn_dt_bias"], a["L0_attn_A_log"]], axis=1)
    by_chunk = lambda m: m.reshape(KC, P, -1).transpose(1, 0, 2)
    d["base_w"] = by_chunk(a["L0_ffn_base_W"].T)
    lora = a["L0_ffn_lora_A"].transpose(1, 0, 2).reshape(D, ER)
    d["lora_a_router"] = by_chunk(np.concatenate([lora, a["L0_ffn_router_W"].T], axis=1)).reshape(P, -1)
    d["lora_b"] = a["L0_ffn_lora_B"].reshape(ER, D)
    d["mask_t"] = a["L1_attn_mask"].T
    d["wt"] = by_chunk(a["L1_attn_weight"].T)
    d["w3"] = by_chunk(a["L1_ffn_w3"].T)
    d["w12"] = a["L1_ffn_w12"].reshape(-1, P, KC, P).transpose(0, 3, 2, 1).reshape(-1, P, D)
    d["b12"] = a["L1_ffn_b12"].reshape(-1, P).T
    d["L1_ffn_b3"] = a["L1_ffn_b3"]
    for layer, perm in ((1, (2, 0, 3, 1)), (2, (1, 3, 0, 2))):
        w = a[f"L1_xattn_W_lin{layer}"].reshape(P, 2, C, NM)
        near = w[:, 1].reshape(P, 2, 2, CH, NM)[..., np.argsort(perm)]
        d[f"lin_n{layer}"] = near.transpose(0, 1, 2, 4, 3).reshape(P, 2, P)
        d[f"lin_c{layer}"] = np.concatenate([w[:, 0].transpose(0, 2, 1)] * B, axis=2)
        d[f"b_lin{layer}"] = a[f"L1_xattn_b_lin{layer}"][:, None]
        d[f"conv_t{layer}"] = np.concatenate([a[f"L1_xattn_W_conv{layer}"].T] * (B // layer), axis=1)
    w = a["L1_xattn_W_conv3"].T
    d["conv3_diag"] = w[:2 * C].reshape(2, C, C).transpose(1, 0, 2)
    d["conv3_last"] = w[2 * C:]
    return {n: np.ascontiguousarray(v) for n, v in d.items()}


def build(nc, dr, out):
    with ExitStack() as ctx:
        k = Kit(nc, ctx)
        k.x = k.sb("x_sb", [P, D], F32)
        k.h = k.sb("h_sb", [P, D], F32)
        k.hT = k.sb("hT", [P, KC, T], F32)
        k.ident = k.sb("ident", [P, P], F32)
        k.identb = k.sb("identb", [P, P], BF16)
        k.identh = k.sb("identh", [P, P], F16)
        k.eps = k.sb("eps", [P, 1], F32)
        k.bn = k.sb("bn", [P, 2, 6], F32)
        k.mv = k.sb("mv", [P, 2], F32)
        k.std = k.sb("std", [P, 1], F32)
        k.rstd = k.sb("rstd", [P, 1], F32)
        k.coord = k.sb("coord", [P, B * 3 * NT], F32)
        k.keys = k.sb("keys", [P, NM * B * NT], F32)
        k.rank = k.sb("rank", [P, NM * B * NT], F32)
        k.msum = k.sb("msum", [P, KC * 32], F32)
        k.ring_in = [k.sem(f"ring_in{i}") for i in range(6)]
        k.norm_stat, k.norm_std, k.norm_turned, k.norm_copied = (k.sem(f"norm_{i}") for i in ("stat", "std", "turned", "copied"))
        k.moe_in = k.sem("moe_in")
        k.coord_ready = k.sem("coord_ready")
        k.ps = ctx.enter_context(nc.psum_tensor("ps", [P, 8, HALF], F32))
        with ExitStack() as early:
            k.ring = k.sb("ring", [P, 24, D], F32, early)
            stage_quantised_product(nc, k, dr)
            stage_mixer(nc, k, dr)
            stage_lora_experts(nc, k)
        k.wt = k.sb("wt", [P, KC, D], F32)
        k.w3 = k.sb("w3", [P, D // P, D], F32)
        k.wt_in, k.w3_in = k.sem("wt_in"), k.sem("w3_in")
        stage_point_cloud(nc, k, dr)
        stage_sparse_linear_and_ffn(nc, k, dr, out)


def kernel(**inputs):
    import numpy as np
    import concourse.bacc as bacc
    from concourse.bass_utils import run_bass_kernel_spmd
    arrays = host_layout(inputs, np)
    nc = bacc.Bacc("TRN2", target_bir_lowering=False, num_devices=1)
    dr = {n: nc.dram_tensor(f"in_{n}", a.shape, mybir.dt.from_np(a.dtype), kind="ExternalInput").ap() for n, a in arrays.items()}
    out = nc.dram_tensor("out_0", (B, L, D), F32, kind="ExternalOutput").ap()
    build(nc, dr, out)
    result = run_bass_kernel_spmd(nc, [{f"in_{n}": a for n, a in arrays.items()}], core_ids=[0])
    return result.results[0]["out_0"]
```

```python
from contextlib import ExitStack

import concourse.bass as bass
from concourse import mybir

F32 = mybir.dt.float32
F16 = mybir.dt.float16
BF16 = mybir.dt.bfloat16
I32 = mybir.dt.int32
ALU = mybir.AluOpType
ACT = mybir.ActivationFunctionType
AX = mybir.AxisListType.X

P = 128
B, L, D = 2, 64, 1024
T = B * L
KC = D // P
HALF = 512
EPS = 1e-5
HOLD = 5
ROUND = 12582912.0
QMID = 128.0
QMAX = 255.0

NH, HD, NG, NS, CK = 128, 64, 8, 128, 4
DIN = NH * HD
GH = NH // NG
GB = DIN // NG // P
NBLK = DIN // P

NE, RANK = 8, 16
ER = NE * RANK

N = 1024
C = 64
NM = 4
WIN = 10
NHEAD = 4
CH = C // NHEAD
NT = N // P
BITS = 10


def fcopy(ap, dims, offset=0):
    return bass.AP(tensor=ap.tensor, offset=ap.offset + offset, ap=[list(ap.ap[0])] + [list(d) for d in dims])


class Kit:

    def __init__(self, nc, ctx):
        self.nc, self.ctx = nc, ctx

    def sb(self, name, shape, dt, ctx=None):
        return (ctx or self.ctx).enter_context(self.nc.sbuf_tensor(name, shape, dt))

    def sem(self, name):
        return self.ctx.enter_context(self.nc.semaphore(name))


class Norm:

    def __init__(self, k, nth):
        self.stat, self.std, self.turned, self.copied = k.norm_stat, k.norm_std, k.norm_turned, k.norm_copied
        self.stats = lambda count: 6 * nth + count
        self.stds = nth + 1
        self.turns = lambda count: 2 * nth - 2 + count
        self.copies = 2 * nth


def norm_statistics(nc, k, n, half):
    nc.vector.bn_stats(k.bn[:, half, :], k.x[:, half * HALF:(half + 1) * HALF]).then_inc(n.stat, 1)


def norm_vector(nc, v, k, n):
    v.wait_ge(n.stat, n.stats(2))
    nc.vector.bn_aggr(k.mv[:, :], k.bn[:, :, :]).then_inc(n.stat, 1)
    v.wait_ge(n.std, n.stds)
    nc.vector.reciprocal(k.rstd[:, :], k.std[:, :]).then_inc(n.stat, 1)
    v.wait_ge(n.stat, n.stats(4))
    for i in range(2):
        cols = slice(i * HALF, (i + 1) * HALF)
        nc.vector.tensor_scalar(k.h[:, cols], k.x[:, cols], k.mv[:, 0:1], k.rstd[:, 0:1], ALU.subtract, ALU.mult).then_inc(n.stat, 1)


def hold_clock(nc, k, bank, count):
    for _ in range(count):
        nc.tensor.matmul(k.ps[:, bank, 0:P], k.ident[:, :], k.ident[:, :], start=True, stop=True)


def load_root(nc, k):
    nc.scalar.activation(k.root[:, :], k.eps[:, 0:1], ACT.Sqrt)


def norm_scalar(nc, act, k, n):
    act.wait_ge(n.stat, n.stats(3))
    nc.scalar.activation(k.std[:, :], k.mv[:, 1:2], ACT.Sqrt, bias=k.eps[:, 0:1]).then_inc(n.std, 1)


def norm_tensor(nc, pe, k, n, banks=(0, 1)):
    for i in range(2):
        pe.wait_ge(n.stat, n.stats(5 + i))
        for j in range(4):
            c = 4 * i + j
            mm = nc.tensor.transpose(k.ps[:, banks[i], j * P:(j + 1) * P], k.h[:, c * P:(c + 1) * P], k.ident[:, :])
        mm.then_inc(n.turned, 1)


def norm_copy_scalar(nc, act, k, n, banks=(0, 1)):
    act.wait_ge(n.turned, n.turns(1))
    nc.scalar.copy(k.hT[:, 0:4, :], k.ps[:, banks[0], :].rearrange("p (c t) -> p c t", t=P)).then_inc(n.copied, 1)


def norm_copy_vector(nc, v, k, n, banks=(0, 1)):
    v.wait_ge(n.turned, n.turns(2))
    nc.vector.tensor_copy(k.hT[:, 4:8, :], k.ps[:, banks[1], :].rearrange("p (c t) -> p c t", t=P)).then_inc(n.copied, 1)


def stage_quantised_product(nc, k, dr):
    CHUNKS, BUFS, KPC = 8, 4, 2
    with ExitStack() as ctx:
        cbuf = k.sb("ctx_chunks", [P, BUFS, KPC, D], F32, ctx)
        q2 = k.sb("q2", [P, B, KC, D], BF16, ctx)
        q1f = k.sb("q1f", [P, D], F32, ctx)
        q1 = k.sb("q1", [P, D], BF16, ctx)
        q1z = k.sb("q1z", [P, B, KC, T], BF16, ctx)
        onesz = k.sb("onesz", [P, B, T], BF16, ctx)
        sc = k.sb("scales", [P, 4], F32, ctx)
        rec = k.sb("rec", [P, 2], F32, ctx)
        off = k.sb("off", [P, 2], F32, ctx)
        s12 = k.sb("s12", [P, 1], F32, ctx)
        rsum = k.sb("rsum", [P, 1], F32, ctx)
        rowb = k.sb("rowb", [P, 2], F32, ctx)
        crow = k.sb("crow", [B * 3 * NT, P], F32, ctx)
        tsum = k.sb("tsum", [P, D], F32, ctx)

        s_x, s_sc, s_co = k.sem("q_x_in"), k.sem("q_scales_in"), k.sem("q_coords_in")
        s_ctx = [k.sem(f"q_ctx_in{i}") for i in range(BUFS)]
        s_const, s_const0 = k.sem("q_const"), k.sem("q_const0")
        s_prm, s_aff, s_clip, s_q2 = k.sem("q_params"), k.sem("q_affine"), k.sem("q_clip"), k.sem("q_q2")
        s_q1, s_q1t, s_q1z = k.sem("q_q1"), k.sem("q_q1t"), k.sem("q_q1z")
        s_mm, s_fin = k.sem("q_mm"), k.sem("q_fin")
        s_ct = k.sem("q_coords_turned")
        n = Norm(k, 0)
        acc = lambda h: k.ps[:, 2 + h, :]
        csum = lambda h: k.ps[:, 4 + h, :]

        block = ctx.enter_context(nc.Block())

        @block.sync
        def _(sp):
            sp.dma_start(k.x[:, :], dr["x"]).then_inc(s_x, 16)
            for i, name in enumerate(("L0_xattn_x1_scale", "L0_xattn_x1_zp", "L0_xattn_x2_scale", "L0_xattn_x2_zp")):
                sp.dma_start(sc[:, i:i + 1], dr[name].partition_broadcast(P)).then_inc(s_sc, 16)
            for b in range(B):
                sp.dma_start(crow[b * 3 * NT:(b + 1) * 3 * NT, :],
                             dr["ctx_4096"][b, 0:3, :].rearrange("c (t p) -> (c t) p", p=P)).then_inc(s_co, 16)
            for c in range(CHUNKS):
                if c >= BUFS:
                    sp.wait_ge(s_q2, c - BUFS + 1)
                b, kc = c // (CHUNKS // B), c % (CHUNKS // B) * KPC
                sp.dma_start(cbuf[:, c % BUFS], dr["ctx_4096"][b, kc * P:(kc + KPC) * P, :]
                             .rearrange("(k p) n -> p k n", p=P)).then_inc(s_ctx[c % BUFS], 16)
            sp.dma_start(k.ring[:, 16, :], dr["w_in"][144]).then_inc(k.ring_in[4], 16)
            for j in range(4):
                sp.dma_start(k.ring[:, 4 * j:4 * j + 4, :],
                             dr["w_in"][128 + 4 * j:132 + 4 * j].rearrange("j p c -> p j c")).then_inc(k.ring_in[j], 16)

        @block.gpsimd
        def _(pool):
            nc.gpsimd.memset(k.ident[:, :], 0.0).then_inc(s_const0, 1)
            nc.gpsimd.memset(k.identb[:, :], 0.0).then_inc(s_const0, 1)
            nc.gpsimd.memset(k.identh[:, :], 0.0).then_inc(s_const0, 1)
            nc.gpsimd.memset(k.eps[:, :], EPS).then_inc(s_const0, 1)
            pool.wait_ge(s_const0, 3)
            for m in (k.ident, k.identb, k.identh):
                nc.gpsimd.affine_select(out=m[:, :], in_=m[:, :], compare_op=ALU.not_equal, fill=1.0, base=0,
                                        pattern=[[-1, P]], channel_multiplier=1).then_inc(s_const, 1)
            nc.gpsimd.memset(q1z[:, :, :, :], 0.0).then_inc(s_const, 1)
            nc.gpsimd.memset(onesz[:, :, :], 0.0).then_inc(s_const0, 1)
            pool.wait_ge(s_const0, 5)
            for b in range(B):
                nc.gpsimd.memset(onesz[:, b, b * L:(b + 1) * L], 1.0).then_inc(s_const, 1)

        @block.vector
        def _(v):
            v.wait_ge(s_x, 16)
            for half in range(2):
                norm_statistics(nc, k, n, half)
            norm_vector(nc, v, k, n)
            v.wait_ge(s_sc, 64)
            nc.vector.reciprocal(rec[:, 0:1], sc[:, 0:1]).then_inc(s_prm, 1)
            nc.vector.reciprocal(rec[:, 1:2], sc[:, 2:3]).then_inc(s_prm, 1)
            for i in range(2):
                nc.vector.tensor_scalar(off[:, i:i + 1], sc[:, 2 * i + 1:2 * i + 2], -1.0, QMID, ALU.mult, ALU.add).then_inc(s_prm, 1)
            nc.vector.tensor_tensor(s12[:, :], sc[:, 0:1], sc[:, 2:3], ALU.mult).then_inc(s_prm, 1)
            v.wait_ge(n.stat, n.stats(6))
            v.wait_ge(s_prm, 5)
            nc.vector.tensor_scalar(q1f[:, :], k.h[:, :], rec[:, 0:1], sc[:, 1:2], ALU.mult, ALU.add).then_inc(s_q1, 1)
            v.wait_ge(s_q1, 1)
            nc.vector.tensor_scalar(q1f[:, :], q1f[:, :], 0.0, QMAX, ALU.max, ALU.min).then_inc(s_q1, 1)
            v.wait_ge(s_q1, 2)
            nc.vector.tensor_scalar(q1[:, :], q1f[:, :], ROUND, ROUND + QMID, ALU.add, ALU.subtract).then_inc(s_q1, 1)
            v.wait_ge(s_q1, 3)
            nc.vector.tensor_reduce(rsum[:, :], q1[:, :], AX, ALU.add).then_inc(s_q1, 1)
            nc.vector.tensor_scalar(rowb[:, 0:1], off[:, 0:1], float(D), None, ALU.mult).then_inc(s_q1, 1)
            v.wait_ge(s_q1, 5)
            nc.vector.tensor_scalar(rowb[:, 1:2], rowb[:, 0:1], rsum[:, 0:1], off[:, 1:2], ALU.add, ALU.mult).then_inc(s_q1, 1)
            v.wait_ge(s_ct, 1)
            nc.vector.tensor_copy(k.coord[:, :], k.ps[:, 7, 0:B * 3 * NT]).then_inc(k.coord_ready, 1)
            for c in range(CHUNKS):
                b, kc = c // (CHUNKS // B), c % (CHUNKS // B) * KPC
                buf = cbuf[:, c % BUFS]
                v.wait_ge(s_aff, c + 1)
                nc.vector.tensor_scalar(buf, buf, 0.0, QMAX, ALU.max, ALU.min).then_inc(s_clip, 1)
                v.wait_ge(s_clip, c + 1)
                nc.vector.tensor_scalar(q2[:, b, kc:kc + KPC, :], buf, ROUND, ROUND + QMID, ALU.add, ALU.subtract).then_inc(s_q2, 1)
            v.wait_ge(s_mm, 1)
            v.wait_ge(s_q1, 6)
            for h in range(2):
                cols = slice(h * HALF, (h + 1) * HALF)
                nc.vector.tensor_scalar(tsum[:, cols], csum(h), off[:, 0:1], rowb[:, 1:2], ALU.mult, ALU.add).then_inc(s_fin, 1)
            v.wait_ge(s_mm, 2)
            for h in range(2):
                cols = slice(h * HALF, (h + 1) * HALF)
                v.wait_ge(s_fin, h + 1)
                nc.vector.tensor_tensor(tsum[:, cols], acc(h), tsum[:, cols], ALU.add).then_inc(s_fin, 1)
            for h in range(2):
                cols = slice(h * HALF, (h + 1) * HALF)
                v.wait_ge(s_fin, h + 3)
                nc.vector.scalar_tensor_tensor(out=k.x[:, cols], in0=tsum[:, cols], scalar=s12[:, 0:1], in1=k.x[:, cols],
                                               op0=ALU.mult, op1=ALU.add).then_inc(s_fin, 1)
            for h in range(2):
                v.wait_ge(s_fin, h + 5)
                norm_statistics(nc, k, Norm(k, 1), h)

        @block.scalar
        def _(act):
            act.wait_ge(s_const0, 4)
            load_root(nc, k)
            norm_scalar(nc, act, k, n)
            act.wait_ge(s_prm, 5)
            for c in range(CHUNKS):
                if c == 2:
                    act.wait_ge(s_q1t, 1)
                    act.wait_ge(s_const, 4)
                    turned = k.ps[:, 6, :].bitcast(BF16).rearrange("p (c t) -> p c t", t=T)
                    for b in range(B):
                        nc.scalar.copy(q1z[:, b, :, b * L:(b + 1) * L], turned[:, :, b * L:(b + 1) * L]).then_inc(s_q1z, 1)
                buf = cbuf[:, c % BUFS]
                act.wait_ge(s_ctx[c % BUFS], 16 * (c // BUFS + 1))
                nc.scalar.activation(buf, buf, ACT.Identity, bias=sc[:, 3:4], scale=rec[:, 1:2]).then_inc(s_aff, 1)

        @block.tensor
        def _(pe):
            pe.wait_ge(s_const, 3)
            pe.wait_ge(s_co, 32)
            nc.tensor.transpose(k.ps[:, 7, 0:B * 3 * NT], crow[:, :], k.ident[0:B * 3 * NT, 0:B * 3 * NT]).then_inc(s_ct, 1)
            pe.wait_ge(s_q1, 3)
            turned = k.ps[:, 6, :].bitcast(BF16)
            for c in range(KC):
                mm = nc.tensor.transpose(turned[:, c * P:(c + 1) * P], q1[:, c * P:(c + 1) * P], k.identb[:, :])
            mm.then_inc(s_q1t, 1)
            pe.wait_ge(s_q1z, 2)
            pe.wait_ge(s_const, 6)
            for c in range(CHUNKS):
                b, k0 = c // (CHUNKS // B), c % (CHUNKS // B) * KPC
                pe.wait_ge(s_q2, c + 1)
                for to, left in ((csum, lambda kc: onesz[:, b, :]), (acc, lambda kc: q1z[:, b, kc, :])):
                    for kc in range(k0, k0 + KPC):
                        first, last = b == 0 and kc == 0, b == B - 1 and kc == KC - 1
                        for h in range(2):
                            mm = nc.tensor.matmul(to(h), left(kc), q2[:, b, kc, h * HALF:(h + 1) * HALF], start=first, stop=last)
                    if c == CHUNKS - 1:
                        mm.then_inc(s_mm, 1)


KEY_STEPS = 10 + 7 + (BITS - 1) * (3 * 3 + 2 * 4) + 2 + 8 + 8 + 2 + 2 + 1


SHL, SAR, SHR = ALU.logical_shift_left, ALU.arith_shift_right, ALU.logical_shift_right
AND, OR, XOR = ALU.bitwise_and, ALU.bitwise_or, ALU.bitwise_xor


class SortKeys:

    def __init__(self, nc, v, k, w, s_key, s_ext, s_allmax):
        self.nc, self.v, self.k, self.w = nc, v, k, w
        self.s_key, self.s_ext, self.s_allmax = s_key, s_ext, s_allmax
        self.done = 0
        self.flat = lambda kind, i: w.q[:, kind, i].rearrange("p v b t -> p (v b t)")
        self.xyz = k.coord[:, :].rearrange("p (b c t) -> p (b c) t", b=B, c=3)

    def link(self, ins):
        self.done += 1
        ins.then_inc(self.s_key, 1)
        self.v.wait_ge(self.s_key, self.done)

    def extremes(self):
        vec, w = self.nc.vector, self.w
        vec.tensor_reduce(w.ext[:, 0:6], self.xyz, AX, ALU.max).then_inc(self.s_ext, 1)
        vec.tensor_reduce(w.ext[:, 6:12], self.xyz, AX, ALU.min, negate=True).then_inc(self.s_ext, 1)

    def quantise(self):
        vec, w, link = self.nc.vector, self.w, self.link
        self.v.wait_ge(self.s_allmax, 1)
        top, neg = w.allmax[:, 0:6], w.allmax[:, 6:12]
        link(vec.tensor_tensor(w.span[:, :], top, neg, ALU.add))
        link(vec.tensor_scalar(w.span[:, :], w.span[:, :], 1e-6, None, ALU.add))
        link(vec.reciprocal(w.span[:, :], w.span[:, :]))
        link(vec.tensor_scalar(w.span[:, :], w.span[:, :], float(2 ** BITS - 1), None, ALU.mult))
        u = w.u[:, :].rearrange("p (g t) -> p g t", t=NT)
        link(vec.tensor_tensor(u, self.xyz, fcopy(neg, [[1, 6], [0, NT]]), ALU.add))
        link(vec.tensor_tensor(u, u, fcopy(w.span[:, :], [[1, 6], [0, NT]]), ALU.mult))
        link(vec.tensor_scalar(w.r[:, :], w.u[:, :], 2.0 ** 23, 2.0 ** 23, ALU.add, ALU.subtract))
        link(vec.tensor_tensor(w.u[:, :], w.r[:, :], w.u[:, :], ALU.is_gt))
        link(vec.tensor_tensor(w.r[:, :], w.r[:, :], w.u[:, :], ALU.subtract))
        link(vec.tensor_scalar(w.r[:, :], w.r[:, :], 0.0, float(2 ** BITS - 1), ALU.max, ALU.min))
        r = w.r[:, :].rearrange("p (b c t) -> p b c t", b=B, c=3)
        for var, order in enumerate(((0, 1, 2), (1, 0, 2))):
            for i, c in enumerate(order):
                link(vec.tensor_copy(w.q[:, 0, i, var], r[:, :, c, :]))
        link(vec.tensor_copy(w.q[:, 1], w.q[:, 0]))

    def transform(self, bits):
        vec, link = self.nc.vector, self.link
        X = [self.flat(1, i) for i in range(3)]
        t1, m = self.w.t1[:, :], self.w.m[:, :]
        for bit in bits:
            low = (1 << bit) - 1
            for i in range(3):
                link(vec.tensor_scalar(m, X[i], 31 - bit, 31, SHL, SAR))
                link(vec.tensor_scalar(m, m, low, None, AND))
                if i:
                    link(vec.tensor_tensor(t1, X[0], X[i], XOR))
                    link(vec.scalar_tensor_tensor(out=t1, in0=m, scalar=low, in1=t1, op0=XOR, op1=AND))
                    link(vec.tensor_tensor(X[0], X[0], t1, XOR))
                    link(vec.tensor_tensor(X[i], X[i], t1, XOR))
                link(vec.tensor_tensor(X[0], X[0], m, XOR))

    def finish(self):
        vec, w, link = self.nc.vector, self.w, self.link
        X = [self.flat(1, i) for i in range(3)]
        t1, m = w.t1[:, :], w.m[:, :]
        for i in (1, 2):
            link(vec.tensor_tensor(X[i], X[i], X[i - 1], XOR))
        link(vec.scalar_tensor_tensor(out=t1, in0=X[2], scalar=1, in1=X[2], op0=SHR, op1=XOR))
        for sh in (2, 4, 8):
            link(vec.scalar_tensor_tensor(out=m, in0=t1, scalar=sh, in1=t1, op0=SHR, op1=XOR))
            t1, m = m, t1
        link(vec.tensor_scalar(t1, t1, 1, None, SHR))
        for i in range(3):
            link(vec.tensor_tensor(X[i], X[i], t1, XOR))
        q = w.q[:, :].rearrange("p k c v b t -> p (k c v b t)")
        for sh, mask in ((16, 0x030000FF), (8, 0x0300F00F), (4, 0x030C30C3), (2, 0x09249249)):
            link(vec.scalar_tensor_tensor(out=w.spread[:, :], in0=q, scalar=sh, in1=q, op0=SHL, op1=OR))
            link(vec.tensor_scalar(q, w.spread[:, :], mask, None, AND))
        axis = lambda i: w.q[:, :, i].rearrange("p k v b t -> p k (v b t)")
        key = w.key[:, :].rearrange("p (k g) -> p k g", k=2)
        link(vec.scalar_tensor_tensor(out=key, in0=axis(0), scalar=2, in1=axis(2), op0=SHL, op1=OR))
        link(vec.scalar_tensor_tensor(out=key, in0=axis(1), scalar=1, in1=key, op0=SHL, op1=OR))
        top_bit = 1 << (3 * BITS - 1)
        link(vec.tensor_scalar(w.spread[:, 0:NM * B * NT], w.key[:, :], top_bit, 1, AND, SHL))
        link(vec.scalar_tensor_tensor(out=self.k.keys[:, :].bitcast(I32), in0=w.key[:, :], scalar=top_bit,
                                      in1=w.spread[:, 0:NM * B * NT], op0=XOR, op1=OR))
        vec.transpose(w.rows[:, :], self.k.keys[:, :]).then_inc(self.s_key, 1)
        assert self.done + 1 == KEY_STEPS


class Bag:
    pass


def stage_mixer(nc, k, dr):
    TP = L + CK - 1
    NPAR = CK + 3
    G0 = 5
    with ExitStack() as ctx:
        sb = lambda name, shape, dt=F32: k.sb(name, shape, dt, ctx)
        xpad = sb("xpad", [P, GB, B, TP])
        xc = sb("xc", [P, GB, T])
        xsil, sgate = sb("xsil", [P, GB, T]), sb("sgate", [P, GB, T])
        decay = sb("decay", [P, GH, L])
        MT = sb("MT", [P, GH, T])
        seg_rhs = sb("seg_rhs", [P, GH, L])
        xs = sb("xs", [P, GH * HD])
        z, y, ysq, yn = (sb(f"y_{i}", [P, GB, T]) for i in "zysn")
        BT, CT = sb("BT", [P, NG, T]), sb("CT", [P, NG, T])
        gm = sb("gm", [P, NG, L])
        par, parg = sb("par", [P, NG, GB * NPAR]), sb("parg", [P, GB, NPAR])
        parbc = sb("parbc", [P, 2 * NG, CK + 1])
        hp, ea = sb("head_par", [P, 2]), sb("exp_A", [P, 1])
        dtr, dta, dte, dts, dtp, dtq = (sb(f"dt_{i}", [P, T]) for i in "raespq")
        dt_tok, adt_tok = sb("dt_tok", [P, NH]), sb("adt_tok", [P, NH])
        tri_le, tri_gt, tri_s = sb("tri_le", [P, L]), sb("tri_gt", [P, T]), sb("tri_s", [P, P])
        ones = sb("ones_col", [P, 1])
        gstd, grs = sb("group_std", [P, 1]), sb("group_rs", [P, 1])
        krow = sb("krow", [P, N])
        junk, junk_eq = sb("junk", [P, 2, N], BF16), sb("junk_eq", [P, 2, P], BF16)
        kcol, racc = sb("kcol", [P, NT]), sb("racc", [P, NT, 3])
        mchunk = sb("mchunk", [P, D], I32)
        w = Bag()
        w.ext, w.allmax, w.span = sb("w_ext", [P, 12]), sb("w_allmax", [P, 12]), sb("w_span", [P, 6])
        w.u, w.r = sb("w_u", [P, 48]), sb("w_r", [P, 48])
        w.q = sb("w_q", [P, 2, 3, 2, B, NT], I32)
        w.t1, w.m = sb("w_t1", [P, 32], I32), sb("w_m", [P, 32], I32)
        w.spread, w.key = sb("w_spread", [P, 192], I32), sb("w_key", [P, 64], I32)
        w.rows = sb("w_rows", [P, NM * B * NT])

        sem = lambda name: k.sem(f"m_{name}")
        s_par, s_const, s_const0 = sem("params_in"), sem("const"), sem("const0")
        s_proj, s_evac = sem("proj"), sem("evac")
        s_cv = sem("conv_step")
        s_silu = sem("silu")
        s_dtr, s_dt, s_dte, s_dtt, s_dtc = sem("dt_raw"), sem("dt"), sem("dt_exp"), sem("dt_turned"), sem("dt_tok")
        s_gp, s_gm = sem("gram"), sem("gram_masked")
        s_key, s_ext, s_allmax = sem("key_step"), sem("extremes"), sem("allmax")
        s_kd, s_krow, s_mch = sem("keys_stored"), sem("krow_in"), sem("mask_in")
        s_rk, s_msum = sem("rank_step"), sem("mask_sum")
        s_rhs, s_seg, s_dec, s_M = sem("seg_rhs"), sem("seg"), sem("decay"), sem("M")
        s_xT, s_xs, s_Y, s_z = sem("x_turned"), sem("xs"), sem("Y"), sem("z")
        s_pg, s_y, s_ysq, s_yn = sem("parg"), sem("y"), sem("ysq"), sem("yn")
        s_sq = sem("ysq_sum")
        s_var, s_out, s_std, s_rs, s_xup = sem("var"), sem("out"), sem("group_std"), sem("group_rs"), sem("x_updated")
        n = Norm(k, 1)
        keyd = nc.dram_tensor("keys_scratch", [NM * B, N], F32).ap()
        ps = k.ps

        def chunk(j):
            return k.ring[:, 4 * j:4 * j + 4, :]

        block = ctx.enter_context(nc.Block())

        @block.sync
        def _(sp):
            sp.dma_start(par[:, :, :], dr["par"]).then_inc(s_par, 16)
            sp.dma_start(parbc[:, :, :], dr["par_bc"]).then_inc(s_par, 16)
            sp.dma_start(hp[:, :], dr["head_par"]).then_inc(s_par, 16)

            def load_xg(g, q, first):
                if first:
                    sp.wait_ge(s_proj, q + 2)
                else:
                    sp.wait_ge(s_proj, 4 * g + 2 + q)
                blk = g * GB + 4 * (q % 2) + (NBLK if q < 2 else 0)
                src = dr["w_in"][bass.ds(blk, 4)] if not first else dr["w_in"][blk:blk + 4]
                sp.dma_start(chunk(q), src.rearrange("j p c -> p j c")).then_inc(k.ring_in[q], 16)

            def load_out(g, h, first):
                if first:
                    if h == 0:
                        sp.wait_ge(s_proj, 1)
                else:
                    sp.wait_ge(s_out, 2 * g - 1 + h)
                blk = g * GB + 4 * h
                src = dr["w_out"][blk:blk + 4] if first else dr["w_out"][bass.ds(blk, 4)]
                sp.dma_start(chunk(4 + h), src.rearrange("j p c -> p j c")).then_inc(k.ring_in[4 + h], 16)

            for h in range(2):
                load_out(0, h, True)
            for q in range(4):
                load_xg(0, q, True)
            for q in range(4):
                load_xg(1, q, False)
            with sp.Fori(1, NG - 1) as g:
                for q in range(4):
                    load_xg(g + 1, q, False)
                for h in range(2):
                    load_out(g, h, False)
            for h in range(2):
                load_out(NG - 1, h, False)
            sp.wait_ge(s_proj, G0 + 4 * NG)
            sp.wait_ge(s_mch, 16 * NG)
            sp.dma_start(k.ring[:, 0:KC, :], dr["base_w"]).then_inc(k.moe_in, 16)
            sp.dma_start(k.ring[:, 8:10, :].rearrange("p a c -> p (a c)")[:, 0:KC * (ER + NE)], dr["lora_a_router"]).then_inc(k.moe_in, 16)
            sp.dma_start(k.ring[:, 10, :], dr["lora_b"]).then_inc(k.moe_in, 16)

        @block.tensor
        def _(pe):
            norm_tensor(nc, pe, k, n)
            pe.wait_ge(n.copied, n.copies)

            def project(c, q, blocks, slot):
                bank = q % 2
                for j in range(blocks):
                    for kc in range(KC):
                        mm = nc.tensor.matmul(ps[:, bank, j * T:(j + 1) * T], k.ring[:, slot + j, kc * P:(kc + 1) * P],
                                              k.hT[:, kc, :], start=kc == 0, stop=kc == KC - 1)
                mm.then_inc(s_proj, 1)

            pe.wait_ge(k.ring_in[4], 16)
            project(0, 0, 1, 16)
            for j in range(4):
                if j >= 1:
                    pe.wait_ge(s_evac, j)
                pe.wait_ge(k.ring_in[j], 16)
                project(1 + j, 1 + j, 4, 4 * j)
            pe.wait_ge(s_dt, 15)
            nc.tensor.transpose(ps[:, 2, 0:P], dtq[:, :], k.ident[:, :])
            nc.tensor.transpose(ps[:, 2, P:2 * P], dta[:, :], k.ident[:, :]).then_inc(s_dtt, 1)

            def out_projection(g):
                if not (isinstance(g, int) and g == 0):
                    pe.wait_ge(s_xup, 2 * g)
                for h in range(2):
                    pe.wait_ge(s_yn, 2 * g + h + 1)
                    if h:
                        pe.wait_ge(s_sq, 3 * g + 3)
                        nc.tensor.matmul(ps[:, 4, 0:1], ysq[:, 0, :], ones[:, :], start=True, stop=True).then_inc(s_var, 1)
                    pe.wait_ge(k.ring_in[4 + h], 16 * (g + 2 - h))
                    for j in range(4 * h, 4 * h + 4):
                        for c in range(2):
                            mm = nc.tensor.matmul(ps[:, 6 + c, :], yn[:, j, :], k.ring[:, 16 + j, c * HALF:(c + 1) * HALF],
                                                  start=j == 0, stop=j == GB - 1)
                    mm.then_inc(s_out, 1)

            def segments(g, first):
                if first:
                    pe.wait_ge(s_dtc, 2)
                else:
                    pe.wait_ge(s_xs, 2 * g)
                pe.wait_ge(s_rhs, g + 1)
                for h in range(2):
                    mm = nc.tensor.matmul(ps[:, 2 + h, :], tri_gt[:, :], seg_rhs[:, 8 * h:8 * h + 8, :], start=True, stop=True)
                mm.then_inc(s_seg, 1)

            def group(g, first):
                if not first:
                    segments(g, first)
                for q in range(4):
                    pe.wait_ge(s_evac, 4 * g + G0 + q - 1)
                    pe.wait_ge(k.ring_in[q], 16 * (g + 2))
                    project(None, G0 + q, 4, 4 * q)
                    if first and q == 1:
                        segments(g, first)
                        pe.wait_ge(s_silu, 4)
                        for gg in range(NG):
                            for b in range(B):
                                mm = nc.tensor.matmul(ps[b * L:(b + 1) * L, 4, gg * L:(gg + 1) * L], BT[:, gg, b * L:(b + 1) * L],
                                                      CT[:, gg, b * L:(b + 1) * L], start=True, stop=True)
                        mm.then_inc(s_gp, 1)
                pe.wait_ge(s_dec, g + 1)
                for j in range(GB):
                    pe.wait_ge(s_silu, 2 * g + 4 + j // 4 + 1)
                    mm = nc.tensor.transpose(ps[:, 2 + j // 4, j % 4 * P:(j % 4 + 1) * P], xsil[:, j, :], k.ident[:, :])
                    if j % 4 == 3:
                        mm.then_inc(s_xT, 1)
                if first:
                    pe.wait_ge(s_gm, 1)
                else:
                    out_projection(g - 1)
                pe.wait_ge(s_M, 2 * g + 2)
                pe.wait_ge(s_xs, 2 * g + 2)
                if not first:
                    pe.wait_ge(s_z, 8 * g)
                    pe.wait_ge(s_std, g)
                for h in range(GH):
                    j = h // 2
                    mm = nc.tensor.matmul(ps[h % 2 * HD:(h % 2 + 1) * HD, 4 + j // 4, j % 4 * T:(j % 4 + 1) * T],
                                          xs[:, h * HD:(h + 1) * HD], MT[:, h, :], start=True, stop=True)
                mm.then_inc(s_Y, 1)

            pe.wait_ge(s_const, 10)
            group(0, True)
            with pe.Fori(1, NG) as g:
                group(g, False)
            out_projection(NG - 1)
            hold_clock(nc, k, 0, 2 * HOLD)

        @block.scalar
        def _(act):
            norm_scalar(nc, act, k, n)
            norm_copy_scalar(nc, act, k, n)
            act.wait_ge(s_par, 48)
            nc.scalar.activation(ea[:, :], hp[:, 1:2], ACT.Exp).then_inc(s_dtr, 1)
            act.wait_ge(s_proj, 1)
            nc.scalar.activation(dtr[:, :], ps[:, 0, 0:T], ACT.Identity, bias=hp[:, 0:1]).then_inc(s_evac, 1)
            act.wait_ge(s_dt, 1)
            nc.scalar.activation(dte[:, :], dta[:, :], ACT.Exp, scale=-1.0).then_inc(s_dte, 1)
            act.wait_ge(s_const, 10)

            def pad(bank, half):
                for b in range(B):
                    ins = nc.scalar.copy(xpad[:, 4 * half:4 * half + 4, b, CK - 1:TP],
                                         ps[:, bank, :].rearrange("p (j t) -> p j t", t=T)[:, :, b * L:(b + 1) * L])
                ins.then_inc(s_evac, 1)

            def silu(dst, half, c):
                act.wait_ge(s_cv, 16 * c)
                nc.scalar.activation(dst, xc[:, 4 * half:4 * half + 4, :], ACT.Silu).then_inc(s_silu, 1)

            for j in range(4):
                act.wait_ge(s_proj, 2 + j)
                if j >= 2:
                    act.wait_ge(s_cv, 16 * (j - 1))
                pad((1 + j) % 2, j % 2)
                if j >= 1:
                    i = j - 1
                    silu((BT if i < 2 else CT)[:, 4 * (i % 2):4 * (i % 2) + 4, :], i % 2, i + 1)
            silu(CT[:, 4:8, :], 1, 4)

            def after_out(g):
                act.wait_ge(s_var, g + 1)
                nc.scalar.activation(gstd[:, :], ps[:, 4, 0:1], ACT.Sqrt, bias=k.eps[:, 0:1], scale=1.0 / (GB * P)).then_inc(s_std, 1)

            def decays(g, first):
                act.wait_ge(s_seg, g + 1)
                if not first:
                    act.wait_ge(s_M, 2 * g)
                nc.scalar.activation(decay[:, :, :].rearrange("p h l -> p (h l)"),
                                     ps[:, 2:4, :].rearrange("p a c -> p (a c)"), ACT.Exp).then_inc(s_dec, 1)

            def group(g, first):
                if not first:
                    decays(g, first)
                for h in range(2):
                    act.wait_ge(s_proj, 4 * g + G0 + h + 1)
                    act.wait_ge(s_cv, 32 * g + 16 * (3 + h))
                    pad((G0 + h) % 2, h)
                if first:
                    decays(g, first)
                for h in range(2):
                    act.wait_ge(s_proj, 4 * g + G0 + 2 + h + 1)
                    if not first:
                        act.wait_ge(s_y, 2 * g)
                    nc.scalar.activation(sgate[:, 4 * h:4 * h + 4, :].rearrange("p j t -> p (j t)"), ps[:, (G0 + h) % 2, :],
                                         ACT.Silu).then_inc(s_evac, 1)
                    if not first:
                        act.wait_ge(s_z, 8 * g)
                    silu(xsil[:, 4 * h:4 * h + 4, :], h, 2 * g + 5 + h)
                if not first:
                    after_out(g - 1)
                for h in range(2):
                    act.wait_ge(s_y, 2 * g + h + 1)
                    if not first and h == 0:
                        act.wait_ge(s_out, 2 * g)
                    for j in range(4 * h, 4 * h + 4):
                        ins = nc.scalar.mul(yn[:, j, :], y[:, j, :], parg[:, j, CK + 2:CK + 3])
                    ins.then_inc(s_yn, 1)
                nc.scalar.activation(ysq[:, :, :], y[:, :, :], ACT.Square).then_inc(s_ysq, 1)

            group(0, True)
            with act.Fori(1, NG) as g:
                group(g, False)
            after_out(NG - 1)

        @block.vector
        def _(v):
            norm_vector(nc, v, k, n)
            norm_copy_vector(nc, v, k, n)
            vec = nc.vector
            keys = SortKeys(nc, v, k, w, s_key, s_ext, s_allmax)
            keys.extremes()
            keys.quantise()
            v.wait_ge(s_evac, 1)
            vec.scalar_tensor_tensor(out=dta[:, :], in0=dtr[:, :], scalar=-1.0, in1=dtr[:, :], op0=ALU.mult, op1=ALU.max).then_inc(s_dt, 1)
            v.wait_ge(s_dte, 1)
            vec.tensor_scalar(dts[:, :], dte[:, :], 2.0, None, ALU.add).then_inc(s_dt, 1)
            v.wait_ge(s_dt, 2)
            vec.reciprocal(dts[:, :], dts[:, :]).then_inc(s_dt, 1)
            v.wait_ge(s_dt, 3)
            vec.tensor_tensor(dts[:, :], dts[:, :], dte[:, :], ALU.mult).then_inc(s_dt, 1)
            v.wait_ge(s_dt, 4)
            vec.tensor_tensor(dtp[:, :], dts[:, :], dts[:, :], ALU.mult).then_inc(s_dt, 1)
            v.wait_ge(s_dt, 5)
            vec.tensor_scalar(dtq[:, :], dtp[:, :], 1.0 / 15, None, ALU.mult).then_inc(s_dt, 1)
            for i, c in enumerate((13, 11, 9, 7, 5, 3)):
                v.wait_ge(s_dt, 6 + i)
                vec.scalar_tensor_tensor(out=dtq[:, :], in0=dtq[:, :], scalar=1.0 / c, in1=dtp[:, :], op0=ALU.add,
                                         op1=ALU.mult).then_inc(s_dt, 1)
            v.wait_ge(s_dt, 12)
            vec.scalar_tensor_tensor(out=dtq[:, :], in0=dtq[:, :], scalar=1.0, in1=dts[:, :], op0=ALU.add, op1=ALU.mult).then_inc(s_dt, 1)
            vec.tensor_scalar(dtr[:, :], dtr[:, :], 0.0, None, ALU.max).then_inc(s_dt, 1)
            v.wait_ge(s_dt, 14)
            vec.scalar_tensor_tensor(out=dtq[:, :], in0=dtq[:, :], scalar=2.0, in1=dtr[:, :], op0=ALU.mult, op1=ALU.add).then_inc(s_dtr, 1)
            v.wait_ge(s_dtr, 2)
            vec.tensor_scalar(dta[:, :], dtq[:, :], ea[:, 0:1], -1.0, ALU.mult, ALU.mult).then_inc(s_dt, 1)

            def convolve(half, params, c):
                for i in range(CK):
                    tap = CK - 1 - i
                    if i:
                        v.wait_ge(s_cv, 16 * c + 4 * i)
                    for j in range(4):
                        src, dst = xpad[:, 4 * half + j, :, tap:tap + L], xc[:, 4 * half + j, :].rearrange("p (b l) -> p b l", b=B)
                        if i == 0:
                            ins = vec.tensor_scalar(dst, src, params(j, tap), params(j, CK), ALU.mult, ALU.add)
                        else:
                            ins = vec.scalar_tensor_tensor(out=dst, in0=src, scalar=params(j, tap), in1=dst, op0=ALU.mult, op1=ALU.add)
                        ins.then_inc(s_cv, 1)

            v.wait_ge(s_par, 48)
            for j in range(4):
                v.wait_ge(s_evac, 2 + j)
                if j >= 2:
                    v.wait_ge(s_silu, j - 1)
                convolve(j % 2, lambda i, c: parbc[:, 4 * j + i, c:c + 1], j)
                if j < 3:
                    keys.transform([BITS - 1 - j])
            v.wait_ge(s_dtt, 1)
            vec.tensor_copy(dt_tok[:, :], ps[:, 2, 0:P]).then_inc(s_dtc, 1)
            vec.tensor_copy(adt_tok[:, :], ps[:, 2, P:2 * P]).then_inc(s_dtc, 1)
            vec.memset(racc[:, :, :], 0.0).then_inc(s_rk, 1)

            def rank(g):
                vec.tensor_copy(kcol[:, :], k.keys[:, bass.ds(g * NT, NT)]).then_inc(s_rk, 1)
                v.wait_ge(s_krow, 16 * (g + 1))
                v.wait_ge(s_rk, 25 * g + 2)
                for t in range(NT):
                    col, u = kcol[:, t:t + 1], t % 2
                    if t >= 2:
                        v.wait_ge(s_rk, 25 * g + 4 + 3 * (t - 2))
                    if t:
                        vec.tensor_scalar(junk[:, u, 0:t * P], krow[:, 0:t * P], col, None, ALU.is_le, ALU.add,
                                          accum_out=racc[:, t, 0:1]).then_inc(s_rk, 1)
                    vec.tensor_scalar(junk[:, u, t * P:N], krow[:, t * P:N], col, None, ALU.is_lt, ALU.add,
                                      accum_out=racc[:, t, 1:2]).then_inc(s_rk, 1)
                    vec.scalar_tensor_tensor(out=junk_eq[:, u, :], in0=krow[:, t * P:(t + 1) * P], scalar=col, in1=tri_s[:, :],
                                             op0=ALU.is_equal, op1=ALU.mult, accum_out=racc[:, t, 2:3]).then_inc(s_rk, 1)
                v.wait_ge(s_rk, 25 * g + 25)
                vec.tensor_reduce(k.rank[:, bass.ds(g * NT, NT)], racc[:, :, :], AX, ALU.add).then_inc(s_rk, 1)
                v.wait_ge(s_mch, 16 * (g + 1))
                vec.tensor_reduce(k.msum[:, bass.ds(g * 32, 32)], mchunk[:, :].rearrange("p (b c) -> p b c", c=32), AX,
                                  ALU.add).then_inc(s_msum, 1)

            def after_out(g, first=False):
                v.wait_ge(s_std, g + 1)
                vec.reciprocal(grs[:, :], gstd[:, :]).then_inc(s_rs, 1)
                v.wait_ge(s_rs, g + 1)
                v.wait_ge(s_out, 2 * g + 2)
                if not (isinstance(g, int) and g == 0):
                    v.wait_ge(s_xup, 2 * g)
                for c in range(2):
                    cols = slice(c * HALF, (c + 1) * HALF)
                    vec.scalar_tensor_tensor(out=k.x[:, cols], in0=ps[:, 6 + c, :], scalar=grs[:, 0:1], in1=k.x[:, cols],
                                             op0=ALU.mult, op1=ALU.add).then_inc(s_xup, 1)

            def group(g, first):
                if not first:
                    v.wait_ge(s_yn, 2 * g)
                vec.tensor_copy(parg[:, :, :].rearrange("p j c -> p (j c)"), par[:, bass.ds(g, 1), :].rearrange("p a c -> p (a c)")).then_inc(s_pg, 1)
                v.wait_ge(s_pg, g + 1)
                for h in range(2):
                    v.wait_ge(s_evac, 4 * g + G0 + h + 1)
                    v.wait_ge(s_silu, 2 * g + 3 + h)
                    convolve(h, lambda i, c: parg[:, 4 * h + i, c:c + 1], 2 * g + 4 + h)
                if first:
                    v.wait_ge(s_gp, 1)
                    v.wait_ge(s_const, 10)
                    vec.tensor_tensor(gm[:, :, :], ps[:, 4, :].rearrange("p (g l) -> p g l", g=NG), fcopy(tri_le[:, :], [[0, NG], [1, L]]),
                                      ALU.mult).then_inc(s_gm, 1)
                    v.wait_ge(s_gm, 1)
                v.wait_ge(s_dec, g + 1)
                if not first:
                    v.wait_ge(s_Y, g)
                for b in range(B):
                    tok = slice(b * L, (b + 1) * L)
                    vec.tensor_tensor(MT[tok, :, b * L:(b + 1) * L], decay[tok, :, :],
                                      fcopy(gm[tok, bass.ds(g, 1), :], [[0, GH], [1, L]]), ALU.mult).then_inc(s_M, 1)
                if first:
                    keys.transform(range(BITS - 4, BITS - 6, -1))
                for h in range(2):
                    v.wait_ge(s_xT, 2 * g + h + 1)
                    vec.tensor_tensor(xs[:, h * HALF:(h + 1) * HALF].rearrange("p (a d) -> p a d", d=HD),
                                      ps[:, 2 + h, :].rearrange("p (a d) -> p a d", d=HD),
                                      fcopy(dt_tok[:, bass.ds(g * GH + 8 * h, 8)], [[1, 8], [0, HD]]), ALU.mult).then_inc(s_xs, 1)
                if not first:
                    rank(g - 1)
                    after_out(g - 1)
                v.wait_ge(s_Y, g + 1)
                if not first:
                    v.wait_ge(s_y, 2 * g)
                for j in range(GB):
                    vec.scalar_tensor_tensor(out=z[:, j, :], in0=xsil[:, j, :], scalar=parg[:, j, CK + 1:CK + 2],
                                             in1=ps[:, 4 + j // 4, j % 4 * T:(j % 4 + 1) * T], op0=ALU.mult, op1=ALU.add).then_inc(s_z, 1)

            group(0, True)
            keys.transform(range(BITS - 6, 0, -1))
            keys.finish()
            with v.Fori(1, NG) as g:
                group(g, False)
            rank(NG - 1)
            after_out(NG - 1)
            for half in range(2):
                v.wait_ge(s_xup, 2 * NG - 1 + half)
                norm_statistics(nc, k, Norm(k, 2), half)

        @block.gpsimd
        def _(pool):
            gp = nc.gpsimd
            gp.memset(tri_le[:, :], 1.0).then_inc(s_const0, 1)
            gp.memset(tri_gt[:, :], 0.0).then_inc(s_const0, 1)
            gp.memset(tri_s[:, :], 1.0).then_inc(s_const0, 1)
            gp.memset(ones[:, :], 1.0).then_inc(s_const, 1)
            gp.memset(xpad[:, :, :, :], 0.0).then_inc(s_const, 1)
            gp.memset(MT[:, :, :], 0.0).then_inc(s_const, 1)
            pool.wait_ge(s_const0, 3)
            gp.affine_select(out=tri_s[:, :], in_=tri_s[:, :], compare_op=ALU.is_gt, fill=0.0, base=0,
                             pattern=[[-1, P]], channel_multiplier=1).then_inc(s_const, 1)
            pool.wait_ge(s_const, 4)
            for b in range(B):
                rows, cols = slice(b * L, (b + 1) * L), slice(b * L, (b + 1) * L)
                gp.affine_select(out=tri_le[rows, :], in_=tri_le[rows, :], compare_op=ALU.is_ge, fill=0.0, base=0,
                                 pattern=[[1, L]], channel_multiplier=-1).then_inc(s_const, 1)
                pool.wait_ge(s_const, 5 + 3 * b)
                gp.memset(tri_gt[rows, cols], 1.0).then_inc(s_const, 1)
                pool.wait_ge(s_const, 6 + 3 * b)
                gp.affine_select(out=tri_gt[rows, cols], in_=tri_gt[rows, cols], compare_op=ALU.is_gt, fill=0.0, base=0,
                                 pattern=[[-1, L]], channel_multiplier=1).then_inc(s_const, 1)
                pool.wait_ge(s_const, 7 + 3 * b)

            def scaled_steps(g, first):
                if first:
                    pool.wait_ge(s_dtc, 2)
                else:
                    pool.wait_ge(s_seg, g)
                gp.tensor_tensor(seg_rhs[:, :, :], fcopy(adt_tok[:, bass.ds(g * GH, GH)], [[1, GH], [0, L]]),
                                 fcopy(tri_le[:, :], [[0, GH], [1, L]]), ALU.mult).then_inc(s_rhs, 1)

            def load_keys(g, first):
                if not first:
                    pool.wait_ge(s_rk, 25 * g + 1)
                    pool.wait_ge(s_msum, g)
                row = keyd[bass.ds(g, 1), :]
                pool.dma_start(krow[:, :], bass.AP(tensor=row.tensor, offset=row.offset, ap=[[0, P], [1, N]])).then_inc(s_krow, 16)
                pool.dma_start(mchunk[:, :], dr["mask_t"][bass.ds(g * P, P), :]).then_inc(s_mch, 16)

            def gated(g, first):
                for h in range(2):
                    pool.wait_ge(s_z, 8 * g + 4 * h + 4)
                    if not first and h == 0:
                        pool.wait_ge(s_ysq, g)
                    half = lambda x: x[:, 4 * h:4 * h + 4, :].rearrange("p j t -> p (j t)")
                    gp.tensor_tensor(half(y), half(z), half(sgate), ALU.mult).then_inc(s_y, 1)
                pool.wait_ge(s_ysq, g + 1)
                for i, n in enumerate((4, 2, 1)):
                    if i:
                        pool.wait_ge(s_sq, 3 * g + i)
                    flat = lambda at: ysq[:, at:at + n, :].rearrange("p j t -> p (j t)")
                    gp.tensor_tensor(flat(0), flat(0), flat(n), ALU.add).then_inc(s_sq, 1)

            pool.wait_ge(s_ext, 2)
            gp.partition_all_reduce(w.allmax[:, :], w.ext[:, :], P, bass.bass_isa.ReduceOp.max).then_inc(s_allmax, 1)
            scaled_steps(0, True)
            scaled_steps(1, False)
            gated(0, True)
            pool.wait_ge(s_key, KEY_STEPS)
            row = P // 4
            for q in range(4):
                pool.dma_start(bass.AP(tensor=keyd.tensor, offset=keyd.offset + q * row, ap=[[P, row], [row * P, 2], [1, row]]),
                               w.rows[q * row:(q + 1) * row, :].rearrange("c (a p) -> c a p", a=2)).then_inc(s_kd, 16)
            pool.wait_ge(s_kd, 64)
            load_keys(0, True)
            with pool.Fori(1, NG - 1) as g:
                scaled_steps(g + 1, False)
                gated(g, False)
                load_keys(g, False)
            load_keys(NG - 1, False)
            gated(NG - 1, False)


def stage_lora_experts(nc, k):
    SCALING = 2.0
    with ExitStack() as ctx:
        sb = lambda name, shape, dt=F32: k.sb(name, shape, dt, ctx)
        prob, nmax, esum, ersum = sb("prob", [P, NE]), sb("nmax", [P, 1]), sb("esum", [P, 1]), sb("ersum", [P, 1])
        gt, eq, before = sb("gt", [P, NE, NE]), sb("eq", [P, NE, NE]), sb("before", [P, NE, NE])
        place, wsel = sb("place", [P, NE]), sb("wsel", [P, NE])
        mid, midT = sb("mid", [P, ER]), sb("midT", [P, T])
        sem = lambda name: k.sem(f"e_{name}")
        s_c, s_lr, s_base, s_exp, s_r = sem("const"), sem("logits"), sem("base"), sem("exp"), sem("route")
        s_mt, s_mc, s_out, s_x = sem("mid_turned"), sem("mid_copied"), sem("out"), sem("x")
        n = Norm(k, 2)
        ps = k.ps
        lar = k.ring[:, 8:10, :].rearrange("p a c -> p (a c)")[:, 0:KC * (ER + NE)].rearrange("p (k e) -> p k e", k=KC)
        block = ctx.enter_context(nc.Block())

        @block.tensor
        def _(pe):
            hold_clock(nc, k, 7, HOLD)
            norm_tensor(nc, pe, k, n)
            pe.wait_ge(n.copied, n.copies)
            pe.wait_ge(k.moe_in, 48)
            for kc in range(KC):
                mm = nc.tensor.matmul(ps[:, 2, 0:ER + NE], k.hT[:, kc, :], lar[:, kc, :], start=kc == 0, stop=kc == KC - 1)
            mm.then_inc(s_lr, 1)
            for c in range(2):
                for kc in range(KC):
                    mm = nc.tensor.matmul(ps[:, 3 + c, :], k.hT[:, kc, :], k.ring[:, kc, c * HALF:(c + 1) * HALF],
                                          start=kc == 0, stop=False)
            pe.wait_ge(s_r, 12)
            nc.tensor.transpose(ps[:, 5, 0:P], mid[:, :], k.ident[:, :]).then_inc(s_mt, 1)
            pe.wait_ge(s_mc, 1)
            for c in range(2):
                nc.tensor.matmul(ps[:, 3 + c, :], midT[:, :], k.ring[:, 10, c * HALF:(c + 1) * HALF], start=False, stop=True).then_inc(s_out, 1)
            hold_clock(nc, k, 7, 2 * HOLD)

        @block.scalar
        def _(act):
            norm_scalar(nc, act, k, n)
            norm_copy_scalar(nc, act, k, n)
            act.wait_ge(s_r, 1)
            nc.scalar.activation(prob[:, :], ps[:, 2, ER:ER + NE], ACT.Exp, bias=nmax[:, 0:1], accum_out=esum[:, 0:1]).then_inc(s_exp, 1)
            act.wait_ge(s_mt, 1)
            nc.scalar.copy(midT[:, :], ps[:, 5, 0:P]).then_inc(s_mc, 1)
            load_root(nc, k)

        @block.vector
        def _(v):
            norm_vector(nc, v, k, n)
            norm_copy_vector(nc, v, k, n)
            vec = nc.vector
            done = [0]

            def link(ins):
                done[0] += 1
                ins.then_inc(s_r, 1)
                v.wait_ge(s_r, done[0])

            v.wait_ge(s_lr, 1)
            link(vec.tensor_reduce(nmax[:, :], ps[:, 2, ER:ER + NE], AX, ALU.max, negate=True))
            v.wait_ge(s_exp, 1)
            link(vec.reciprocal(ersum[:, :], esum[:, :]))
            link(vec.tensor_scalar(prob[:, :], prob[:, :], ersum[:, 0:1], None, ALU.mult))
            other, own = fcopy(prob[:, :], [[0, NE], [1, NE]]), fcopy(prob[:, :], [[1, NE], [0, NE]])
            link(vec.tensor_tensor(gt[:, :, :], other, own, ALU.is_gt))
            link(vec.tensor_tensor(eq[:, :, :], other, own, ALU.is_equal))
            v.wait_ge(s_c, 2)
            link(vec.tensor_tensor(eq[:, :, :], eq[:, :, :], before[:, :, :], ALU.mult))
            link(vec.tensor_tensor(gt[:, :, :], gt[:, :, :], eq[:, :, :], ALU.add))
            link(vec.tensor_reduce(place[:, :], gt[:, :, :], AX, ALU.add))
            link(vec.scalar_tensor_tensor(out=wsel[:, :], in0=place[:, :], scalar=2.0, in1=prob[:, :], op0=ALU.is_lt, op1=ALU.mult))
            link(vec.tensor_reduce(esum[:, :], wsel[:, :], AX, ALU.add))
            link(vec.reciprocal(ersum[:, :], esum[:, :]))
            v.wait_ge(s_r, 11)
            vec.tensor_scalar(wsel[:, :], wsel[:, :], ersum[:, 0:1], SCALING, ALU.mult, ALU.mult).then_inc(s_x, 1)
            v.wait_ge(s_x, 1)
            vec.tensor_tensor(mid[:, :].rearrange("p (e r) -> p e r", e=NE), ps[:, 2, 0:ER].rearrange("p (e r) -> p e r", e=NE),
                              fcopy(wsel[:, :], [[1, NE], [0, RANK]]), ALU.mult).then_inc(s_r, 1)
            for c in range(2):
                cols = slice(c * HALF, (c + 1) * HALF)
                v.wait_ge(s_out, c + 1)
                vec.tensor_tensor(k.x[:, cols], ps[:, 3 + c, :], k.x[:, cols], ALU.add).then_inc(s_x, 1)
                v.wait_ge(s_x, c + 2)
                norm_statistics(nc, k, Norm(k, 3), c)

        @block.gpsimd
        def _(pool):
            nc.gpsimd.memset(before[:, :, :], 1.0).then_inc(s_c, 1)
            pool.wait_ge(s_c, 1)
            nc.gpsimd.affine_select(out=before[:, :, :], in_=before[:, :, :], compare_op=ALU.is_gt, fill=0.0, base=0,
                                    pattern=[[1, NE], [-1, NE]], channel_multiplier=0).then_inc(s_c, 1)


def stage_sparse_linear_and_ffn(nc, k, dr, out):
    MB = D // P
    with ExitStack() as ctx:
        sb = lambda name, shape, dt=F32: k.sb(name, shape, dt, ctx)
        w12 = sb("w12", [P, 2 * MB, D])
        b12, b3, ones_row = sb("b12", [P, 2 * MB]), sb("b3", [1, D]), sb("ones_row", [1, P])
        gate, x4 = sb("ffn_gate", [P, MB, T]), sb("x4", [P, MB, T])
        sem = lambda name: k.sem(f"f_{name}")
        s_w12 = [sem(f"w12_in{i}") for i in range(4)]
        s_b, s_c = sem("bias_in"), sem("const")
        s_sp, s_x, s_up, s_gate, s_x4, s_out, s_fin, s_store = (sem(i) for i in ("sparse", "x", "up", "gate", "x4", "out", "fin", "stored"))
        n5, n6 = Norm(k, 4), Norm(k, 5)
        ps = k.ps
        block = ctx.enter_context(nc.Block())

        @block.sync
        def _(sp):
            sp.dma_start(b12[:, :], dr["b12"]).then_inc(s_b, 16)
            sp.dma_start(b3[:, :], dr["L1_ffn_b3"].rearrange("(a d) -> a d", a=1)).then_inc(s_b, 16)
            for i in range(4):
                for half in range(2):
                    blk = half * MB + 2 * i
                    sp.dma_start(w12[:, blk:blk + 2, :], dr["w12"][blk:blk + 2].rearrange("j p c -> p j c")).then_inc(s_w12[i], 16)
            for c in range(2):
                sp.wait_ge(s_fin, c + 1)
                sp.dma_start(out.rearrange("b l d -> (b l) d")[:, c * HALF:(c + 1) * HALF], k.x[:, c * HALF:(c + 1) * HALF]).then_inc(s_store, 16)
            sp.wait_ge(s_store, 32)

        @block.gpsimd
        def _(pool):
            nc.gpsimd.memset(ones_row[:, :], 1.0).then_inc(s_c, 1)

        @block.tensor
        def _(pe):
            hold_clock(nc, k, 4, 2 * HOLD)
            norm_tensor(nc, pe, k, n5)
            pe.wait_ge(k.wt_in, 16)
            pe.wait_ge(n5.copied, n5.copies)
            for c in range(2):
                for kc in range(KC):
                    mm = nc.tensor.matmul(ps[:, 2 + c, :], k.hT[:, kc, :], k.wt[:, kc, c * HALF:(c + 1) * HALF],
                                          start=kc == 0, stop=kc == KC - 1)
                mm.then_inc(s_sp, 1)
            pe.wait_ge(s_c, 1)
            pe.wait_ge(s_b, 32)
            for c in range(2):
                nc.tensor.matmul(ps[:, 6 + c, :], ones_row[:, :], b3[:, c * HALF:(c + 1) * HALF], start=True, stop=False)
            norm_tensor(nc, pe, k, n6)
            pe.wait_ge(n6.copied, n6.copies)
            pe.wait_ge(s_x, 2)
            for j in range(MB):
                if j >= 2:
                    pe.wait_ge(s_x4, j - 1)
                if j % 2 == 0:
                    pe.wait_ge(s_w12[j // 2], 32)
                for half in range(2):
                    for kc in range(KC):
                        mm = nc.tensor.matmul(ps[:, 2 + 2 * half + j % 2, 0:T],
                                              w12[:, half * MB + j, kc * P:(kc + 1) * P], k.hT[:, kc, :], start=kc == 0, stop=kc == KC - 1)
                    mm.then_inc(s_up, 1)
            pe.wait_ge(k.w3_in, 16)
            for c in range(2):
                for j in range(MB):
                    if c == 0:
                        pe.wait_ge(s_x4, j + 1)
                    mm = nc.tensor.matmul(ps[:, 6 + c, :], x4[:, j, :], k.w3[:, j, c * HALF:(c + 1) * HALF], start=False, stop=j == MB - 1)
                mm.then_inc(s_out, 1)

        @block.scalar
        def _(act):
            norm_scalar(nc, act, k, n5)
            norm_copy_scalar(nc, act, k, n5)
            norm_scalar(nc, act, k, n6)
            norm_copy_scalar(nc, act, k, n6)
            act.wait_ge(s_b, 32)
            for j in range(MB):
                act.wait_ge(s_up, 2 * j + 1)
                nc.scalar.activation(gate[:, j, :], ps[:, 2 + j % 2, 0:T], ACT.Silu, bias=b12[:, j:j + 1]).then_inc(s_gate, 1)

        @block.vector
        def _(v):
            norm_vector(nc, v, k, n5)
            norm_copy_vector(nc, v, k, n5)
            for c in range(2):
                cols = slice(c * HALF, (c + 1) * HALF)
                v.wait_ge(s_sp, c + 1)
                nc.vector.tensor_tensor(k.x[:, cols], ps[:, 2 + c, :], k.x[:, cols], ALU.add).then_inc(s_x, 1)
                v.wait_ge(s_x, c + 1)
                norm_statistics(nc, k, n6, c)
            norm_vector(nc, v, k, n6)
            norm_copy_vector(nc, v, k, n6)
            v.wait_ge(s_b, 32)
            for j in range(MB):
                v.wait_ge(s_up, 2 * j + 2)
                v.wait_ge(s_gate, j + 1)
                nc.vector.scalar_tensor_tensor(out=x4[:, j, :], in0=ps[:, 4 + j % 2, 0:T], scalar=b12[:, MB + j:MB + j + 1],
                                               in1=gate[:, j, :], op0=ALU.add, op1=ALU.mult).then_inc(s_x4, 1)
            for c in range(2):
                cols = slice(c * HALF, (c + 1) * HALF)
                v.wait_ge(s_out, c + 1)
                nc.vector.tensor_tensor(k.x[:, cols], ps[:, 6 + c, :], k.x[:, cols], ALU.add).then_inc(s_fin, 1)


STEP, TRIO = 24, 3
STEPS = -(-N // STEP)
LEAD = WIN // 2
ROWS = TRIO * WIN
COLS = STEP * WIN
LASTN = N - LEAD - (STEPS - 1) * STEP + LEAD
REG = LASTN - LEAD
SLOTS = 2 * B * 2
FAR = -2.0 ** 100
S_BANK = (0, 5)
PERMS = 4
SCALE = 256.0
PARTS_AND_WEIGHTS = 2 + B + 1 + 5 + B


class Cloud:

    def __init__(self, k, ctx):
        sb = lambda name, shape, dt=F32: k.sb(name, shape, dt, ctx)
        self.iota = sb("iota", [P, N], F16)
        self.perm = sb("perm", [P, PERMS, N], F16)
        self.spl = sb("split", [P, 2, NT, P], F16)
        self.f16 = sb("f16", [P, N], F16)
        self.fsg = sb("sorted_rows", [P, NT, 2 * P])
        self.W = N + WIN - 1 - LEAD
        self.fsT = sb("sortedT", [P, 4, self.W])
        self.pre = sb("first_windows", [P, 4, LEAD, WIN])
        self.fTr = sb("centreT", [P, 4, N])
        self.fcl = sb("f16_last", [P, STEP], F16)
        self.X = [sb(f"X{u}", [P, 4, STEP // TRIO * 32], F16) for u in range(2)]
        self.S = [sb(f"S{u}", [P, 2 * SLOTS, ROWS]) for u in range(2)]
        self.mx = [sb(f"mx{u}", [P, 2 * SLOTS]) for u in range(2)]
        self.den = [sb(f"den{u}", [P, 2 * SLOTS]) for u in range(2)]
        self.PP = [sb(f"PP{u}", [P, 2 * SLOTS, 32, 2], F16) for u in range(2)]
        self.PT = [sb(f"PT{u}", [P, 2 * SLOTS, 4, 32, 2], F16) for u in range(2)]
        self.PC = sb("P_turned", [P, 2 * SLOTS, 32, 2], F16)
        self.XR = [sb(f"XR{u}", [P, SLOTS, P], F16) for u in range(2)]
        self.OT = [sb(f"OT{u}", [P, 2, B, COLS]) for u in range(2)]
        self.step_sems = [k.sem(f"c_{i}") for i in ("X", "scores", "max", "shifted", "exp", "den", "P", "P_high", "P_low", "P_turned", "P_placed",
                                                    "X_turned", "X_rows", "PV", "O", "H", "reduced")]
        self.order_sems = [k.sem(f"c_{i}") for i in ("split", "f16", "weight_products", "parts_and_weights", "centre_turned", "centre_copied", "perm",
                                                     "ordered", "rows", "sorted_turned", "sorted_copied", "windows")]
        self.rows_u, self.cols_v = sb("mask_rows", [32, P], BF16), sb("mask_cols", [32, SLOTS, ROWS], BF16)
        self.stats = sb("stats", [P, B, STEPS, 6])
        self.mvb, self.stdb, self.rsb, self.shift, self.cb = sb("mvb", [P, B, 2]), sb("stdb", [P, B]), sb("rsb", [P, B]), sb("shift", [P, B]), sb("cb", [P, 1])
        self.f1, self.f2 = sb("f1", [P, N]), sb("f2", [P, B, N])
        self.lin_n, self.lin_c = sb("lin_n", [P, 2, P]), sb("lin_c", [P, NM, P])
        self.sel = sb("repeats", [P, 4, P], F16)
        self.conv, self.blin = sb("conv_t", [P, P]), sb("b_lin", [P, 1])
        self.conv_d, self.conv_2 = sb("conv3_diagonal", [P, 2, P]), sb("conv3_last", [P, C])
        self.blocks, self.flag = sb("blocks", [P, P]), sb("block_flags", [P, KC * 32])
        self.conv3_in = k.sem("conv3_in")
        self.WN = sb("WN", [P, 2, B, P])
        self.WC = sb("WC", [P, 3, B, P], BF16)
        self.wparts, self.wrest = sb("WC_parts", [P, 3, P], BF16), sb("WC_rest", [P, P])


def stage_cloud_layer(nc, k, dr, c, layer):
    O = C * layer
    nb = 1 if layer == 1 else B
    with ExitStack() as ctx:
        sem = lambda name: k.sem(f"c{layer}_{name}")
        s_w, s_c, s_sel, s_c0 = sem("weights_in"), sem("const"), sem("repeats"), sem("const0")
        s_turn, s_hT = (k.norm_turned, k.norm_copied) if layer == 1 else (sem("turned"), sem("hT"))
        s_spl, s_f16, s_wp, s_wc, s_ct, s_cc, s_perm, s_ord, s_row, s_st, s_sc, s_fs = c.order_sems
        spl0, f160, wp0, wc0, ct0, cc0, perm0, ord0, row0, st0, sc0, fs0 = ((layer - 1) * i for i in (
            2, 1, 1, PARTS_AND_WEIGHTS, 8, 8, B * NM * NT, B * NM * NT, B * NM, 8, 8, 2 * LEAD))
        (s_X, s_S, s_max, s_sub, s_E, s_den, s_P, s_hi, s_lo, s_turned, s_PT, s_xt, s_XR, s_PV, s_O, s_H, s_red) = c.step_sems
        t0 = STEPS * (layer - 1)
        s_end, s_std = sem("end"), sem("std")
        if layer == 1:
            s_blk, s_sum, s_flag = sem("blocks"), sem("block_sums"), sem("flags")
        else:
            s_early = sem("early_products")
        n = Norm(k, 3) if layer == 1 else None
        turns, hT_done = (n.turns, n.copies) if n else (lambda count: count, 2)
        src = k.h if layer == 1 else c.f1
        ps = k.ps
        xt = ps[:, 2, :].bitcast(F16)
        parts = c.fsg[:, :, :].rearrange("p t d -> p (t d)").bitcast(F16).rearrange("p (s n) -> p s n", n=N)
        block = ctx.enter_context(nc.Block())

        def walk(eng, body, tail):
            for it in range(4):
                body(it, it % 2)
            with eng.Fori(2, (STEPS - 1) // 2 - 1) as pair:
                for u in range(2):
                    body(pair * 2 + u, u)
            for it in range(STEPS - 3, STEPS):
                body(it, it % 2)
            tail()

        after = lambda it, lag: not isinstance(it, int) or it >= lag

        @block.sync
        def _(sp):
            sp.dma_start(c.lin_n[:, :, :], dr[f"lin_n{layer}"]).then_inc(s_w, 16)
            sp.dma_start(c.lin_c[:, :, :], dr[f"lin_c{layer}"]).then_inc(s_w, 16)
            sp.dma_start(c.conv[:, :], dr[f"conv_t{layer}"]).then_inc(s_w, 16)
            sp.dma_start(c.blin[:, :], dr[f"b_lin{layer}"]).then_inc(s_w, 16)
            if layer == 1:
                sp.dma_start(k.wt[:, :, :], dr["wt"]).then_inc(k.wt_in, 16)
                sp.dma_start(k.w3[:, :, :], dr["w3"]).then_inc(k.w3_in, 16)
                sp.dma_start(c.conv_2[:, :], dr["conv3_last"]).then_inc(c.conv3_in, 16)
                sp.wait_ge(s_blk, 2)
                for b in range(B):
                    rows = slice(b * C, (b + 1) * C)
                    sp.dma_start(c.conv_d[rows, :, rows], dr["conv3_diag"]).then_inc(c.conv3_in, 16)

        @block.tensor
        def _(pe):
            hold_clock(nc, k, 7, HOLD)
            if layer == 1:
                norm_tensor(nc, pe, k, n)
            else:
                for i in range(2):
                    for j in range(4):
                        mm = nc.tensor.transpose(ps[:, i, j * P:(j + 1) * P], src[:, (4 * i + j) * P:(4 * i + j + 1) * P], k.ident[:, :])
                    mm.then_inc(s_turn, 1)
            pe.wait_ge(s_w, 64)
            for a in range(2):
                nc.tensor.matmul(ps[:, 6, a * O:(a + 1) * O], c.lin_n[:, a, :], c.conv[:, 0:O], start=True, stop=True)
            for m in range(NM):
                nc.tensor.matmul(ps[:, 6, 2 * O:3 * O], c.lin_c[:, m, :], c.conv[:, 0:O], start=m == 0, stop=m == NM - 1)
            nc.tensor.matmul(ps[:, 6, 3 * P:3 * P + 1], c.conv[:, :], c.blin[:, :], start=True, stop=True).then_inc(s_wp, 1)
            pe.wait_ge(s_wc, wc0 + 1)
            if layer == 1:
                pe.wait_ge(s_sel, 4)
            for g in range(8):
                ab, half = g // 2, g % 2
                if g >= 2:
                    pe.wait_ge(s_cc, cc0 + g - 1)
                for s in range(2):
                    mm = nc.tensor.matmul(ps[:, 4 + g % 2, :], c.sel[:, ab, :], parts[:, s, half * HALF:(half + 1) * HALF], start=s == 0, stop=s == 1)
                mm.then_inc(s_ct, 1)
            if layer == 1:
                pe.wait_ge(s_blk, 6)
                nc.tensor.matmul(ps[:, 7, 0:KC * 32], c.blocks[:, :], k.msum[:, :], start=True, stop=True).then_inc(s_sum, 1)
            pe.wait_ge(s_wc, wc0 + 2)
            for b in range(B):
                for m in range(NM):
                    i = b * NM + m
                    if i >= 2:
                        pe.wait_ge(s_row, row0 + i - 1)
                    for t in range(NT):
                        pe.wait_ge(s_perm, perm0 + i * NT + t + 1)
                        for pt in range(NT):
                            for s in range(2):
                                mm = nc.tensor.matmul(ps[:, i % 2, pt * C:(pt + 1) * C], c.perm[:, t % PERMS, pt * P:(pt + 1) * P],
                                                      c.spl[:, s, t, b * C:(b + 1) * C], start=t + pt + s == 0,
                                                      stop=t == NT - 1 and pt == NT - 1 and s == 1)
                        mm.then_inc(s_ord, 1)
                pe.wait_ge(s_row, row0 + NM * (b + 1))
                for a in range(2):
                    for half in range(2):
                        g = (b * 2 + a) * 2 + half
                        if g >= 2:
                            pe.wait_ge(s_sc, sc0 + g - 1)
                        for j in range(4):
                            mm = nc.tensor.transpose(ps[:, 2 + half, j * P:(j + 1) * P], c.fsg[:, 4 * half + j, a * P:(a + 1) * P], k.ident[:, :])
                        mm.then_inc(s_st, 1)
            pe.wait_ge(s_cc, cc0 + 8)
            pe.wait_ge(s_sc, sc0 + 8)
            pe.wait_ge(s_wc, wc0 + PARTS_AND_WEIGHTS)
            pe.wait_ge(s_f16, f160 + 1)

            def rows(it, u):
                if after(it, 1):
                    pe.wait_ge(s_XR, t0 + it)
                for slot in range(SLOTS):
                    ab, G = slot // 2, slot % 2
                    mm = nc.tensor.transpose(xt[:, slot * P:(slot + 1) * P], c.X[u][:, ab, G * P:(G + 1) * P], k.identh[:, :])
                mm.then_inc(s_xt, 1)

            def scores(it, u):
                pe.wait_ge(s_X, t0 + it + 1)
                if after(it, 2):
                    pe.wait_ge(s_sub, t0 + it - 1)
                X = c.X[u]
                for r in range(2):
                    nc.tensor.matmul(ps[:, S_BANK[u] + r, 0:COLS], c.rows_u[:, :], c.cols_v[:, :, :].rearrange("p s i -> p (s i)"), start=True, stop=False)
                for slot in range(SLOTS):
                    ab, G = slot // 2, slot % 2
                    for q in range(4):
                        at = (G * 4 + q) * 32
                        for r in range(2):
                            half = slice(r * C, (r + 1) * C)
                            mm = nc.tensor.matmul(ps[32 * q:32 * q + 32, S_BANK[u] + r, slot * ROWS:(slot + 1) * ROWS], X[half, ab, at:at + 32],
                                                  X[half, ab, at:at + ROWS], start=False, stop=slot == SLOTS - 1)
                mm.then_inc(s_S, 1)

            def weighted_rows(it, u):
                pe.wait_ge(s_PT, t0 + it + 1)
                if after(it, 1):
                    pe.wait_ge(s_O, t0 + it)
                XR, PT = c.XR[u], c.PT[u]
                for slot in range(SLOTS):
                    at = slot % 4 * 4 * ROWS
                    for part in range(2):
                        for r in range(2):
                            half = slice(r * C, (r + 1) * C)
                            mm = nc.tensor.matmul(ps[half, 3 + slot // 4, at:at + 4 * ROWS], XR[:, slot, half], PT[:, r * SLOTS + slot, :, 0:ROWS, part],
                                                  start=part == 0, stop=part == 1)
                mm.then_inc(s_PV, 1)

            def linear(it, u):
                if after(it, 1):
                    pe.wait_ge(s_red, t0 + it)
                pe.wait_ge(s_O, t0 + it + 1)
                last = isinstance(it, int) and it == STEPS - 1
                centre = c.fcl[:, :] if last else c.f16[:, bass.ds(it * STEP + LEAD, STEP)]
                centre = fcopy(centre, [[1, STEP], [0, WIN]])
                if layer == 1:
                    for s in range(3):
                        nc.tensor.matmul(ps[:, 7, 0:COLS], c.WC[:, s, 0, :], centre, start=s == 0, stop=False)
                    for b in range(B):
                        for a in range(2):
                            mm = nc.tensor.matmul(ps[:, 7, 0:COLS], c.WN[:, a, b, :], c.OT[u][:, a, b, :], start=False, stop=a == 1 and b == B - 1)
                else:
                    for b in range(B):
                        cols = slice(b * COLS, (b + 1) * COLS)
                        for s in range(3):
                            nc.tensor.matmul(ps[:, 7, cols], c.WC[:, s, b, :], centre, start=s == 0, stop=False)
                        for a in range(2):
                            mm = nc.tensor.matmul(ps[:, 7, cols], c.WN[:, a, 0, :], c.OT[u][:, a, b, :], start=False, stop=a == 1)
                mm.then_inc(s_H, 1)

            def step(it, u):
                scores(it, u)
                if after(it, 1):
                    rows(it - 1, 1 - u)
                if isinstance(it, int) and it in (1, 2, 3):
                    hold_clock(nc, k, 7, 3 * HOLD if it == 1 else HOLD)
                if after(it, 3):
                    weighted_rows(it - 3, 1 - u)
                if after(it, 4):
                    linear(it - 4, u)

            def tail():
                rows(STEPS - 1, 0)
                weighted_rows(STEPS - 3, 0)
                linear(STEPS - 4, 1)
                weighted_rows(STEPS - 2, 1)
                linear(STEPS - 3, 0)
                pe.wait_ge(s_XR, t0 + STEPS)
                weighted_rows(STEPS - 1, 0)
                linear(STEPS - 2, 1)
                linear(STEPS - 1, 0)

            walk(pe, step, tail)
            if layer == 2:
                pe.wait_ge(c.conv3_in, 16 * (1 + B))
                pe.wait_ge(s_sub, t0 + STEPS)
                for half in range(2):
                    cols = slice(half * HALF, (half + 1) * HALF)
                    nc.tensor.matmul(ps[:, half, :], c.conv_d[:, 0, :], k.h[:, cols], start=True, stop=False)
                    mm = nc.tensor.matmul(ps[:, half, :], c.conv_d[:, 1, :], c.f1[:, cols], start=False, stop=False)
                mm.then_inc(s_early, 1)
                pe.wait_ge(s_early, 1)
            hold_clock(nc, k, 4, 2 * HOLD)

        @block.scalar
        def _(act):
            sc = nc.scalar
            if layer == 1:
                norm_scalar(nc, act, k, n)
            if n:
                act.wait_ge(n.stat, n.stats(6))
            sc.mul(parts[:, 0, :], src[:, :], SCALE).then_inc(s_spl, 1)
            act.wait_ge(s_turn, turns(1))
            sc.copy(k.hT[:, 0:4, :], ps[:, 0, :].rearrange("p (c t) -> p c t", t=P)).then_inc(s_hT, 1)
            act.wait_ge(s_hT, hT_done)
            sc.mul(c.spl[:, 0], k.hT[:, :, :], SCALE).then_inc(s_spl, 1)
            for g in range(8):
                act.wait_ge(s_ct, ct0 + g + 1)
                sc.mul(c.fTr[:, g // 2, g % 2 * HALF:(g % 2 + 1) * HALF], ps[:, 4 + g % 2, :], 1 / SCALE).then_inc(s_cc, 1)
            for b in range(B):
                for m in range(NM):
                    i = b * NM + m
                    act.wait_ge(s_ord, ord0 + NT * (i + 1))
                    if b and m == 0:
                        act.wait_ge(s_st, st0 + 4)
                    sc.mul(fcopy(c.fsg[:, :, m * CH:], [[2 * P, NT], [C, NHEAD], [1, CH]]),
                           ps[:, i % 2, :].rearrange("p (t h c) -> p t h c", t=NT, h=NHEAD), 1 / SCALE).then_inc(s_row, 1)
                for a in range(2):
                    for half in range(2):
                        g = (b * 2 + a) * 2 + half
                        act.wait_ge(s_st, st0 + g + 1)
                        sc.copy(c.fsT[:, a * B + b, half * HALF:(half + 1) * HALF], ps[:, 2 + half, :]).then_inc(s_sc, 1)

            def unload(it, u):
                act.wait_ge(s_PV, t0 + it + 1)
                if after(it, 2):
                    act.wait_ge(s_H, t0 + it - 1)
                sc.copy(c.OT[u][:, :, :, :].rearrange("p a b n -> p a (b n)"), ps[:, 3:5, 0:2 * COLS]).then_inc(s_O, 1)

            def place(it, u):
                act.wait_ge(s_turned, t0 + it + 1)
                for q in (2, 3):
                    quad = slice(32 * q, 32 * q + 32)
                    ins = sc.copy(c.PT[u][quad, :, q, 0:ROWS, :], c.PC[quad, :, 0:ROWS, :])
                ins.then_inc(s_PT, 1)

            def copy_rows(it, u):
                act.wait_ge(s_xt, t0 + it + 1)
                sc.copy(c.XR[u][:, :, :].rearrange("p s d -> p (s d)"), xt).then_inc(s_XR, 1)

            def step(it, u):
                act.wait_ge(s_sub, t0 + it + 1)
                S = c.S[u][:, :, :].rearrange("p s i -> p (s i)")
                sc.activation(S, S, ACT.Exp, scale=float((NM * CH) ** -0.5)).then_inc(s_E, 1)
                if after(it, 3):
                    unload(it - 3, 1 - u)
                if after(it, 1):
                    copy_rows(it - 1, 1 - u)
                act.wait_ge(s_P, t0 + it + 1)
                if after(it, 2):
                    act.wait_ge(s_turned, t0 + it - 1)
                sc.copy(c.PP[u][:, :, 0:ROWS, 0], c.S[u][:, :, :]).then_inc(s_hi, 1)
                if after(it, 1):
                    place(it - 1, 1 - u)

            def tail():
                unload(STEPS - 3, 0)
                copy_rows(STEPS - 1, 0)
                place(STEPS - 1, 0)
                unload(STEPS - 2, 1)
                unload(STEPS - 1, 0)

            walk(act, step, tail)
            for b in range(nb):
                act.wait_ge(s_end, nb)
                sc.activation(c.stdb[:, b:b + 1], c.mvb[:, b, 1:2], ACT.Sqrt, bias=k.eps[:, 0:1]).then_inc(s_std, 1)

        @block.vector
        def _(v):
            vec = nc.vector
            if layer == 1:
                norm_vector(nc, v, k, n)
            def second_part(at, whole, first, made):
                v.wait_ge(s_spl, spl0 + made)
                vec.scalar_tensor_tensor(out=at, in0=whole, scalar=SCALE, in1=first, op0=ALU.mult, op1=ALU.subtract).then_inc(s_wc, 1)

            v.wait_ge(s_turn, turns(2))
            vec.tensor_copy(k.hT[:, 4:8, :], ps[:, 1, :].rearrange("p (c t) -> p c t", t=P)).then_inc(s_hT, 1)
            second_part(parts[:, 1, :], src[:, :], parts[:, 0, :], 1)
            second_part(c.spl[:, 1], k.hT[:, :, :], c.spl[:, 0], 2)
            def weights():
                v.wait_ge(s_c, 1)
                v.wait_ge(s_wp, wp0 + 1)
                for b in range(B):
                    at = b * C if layer == 1 else 0
                    vec.tensor_copy(c.WN[:, :, b, at:at + O], ps[:, 6, 0:2 * O].rearrange("p (a o) -> p a o", a=2)).then_inc(s_wc, 1)
                vec.tensor_copy(c.cb[:, :], ps[:, 6, 3 * P:3 * P + 1]).then_inc(s_wc, 1)
                rest = ps[:, 6, 2 * O:3 * O]
                for s in range(3):
                    if s:
                        v.wait_ge(s_wc, wc0 + 2 + B + 2 * s)
                        vec.tensor_tensor(c.wrest[:, 0:O], rest, c.wparts[:, s - 1, 0:O], ALU.subtract).then_inc(s_wc, 1)
                        rest = c.wrest[:, 0:O]
                        v.wait_ge(s_wc, wc0 + 3 + B + 2 * s)
                    vec.tensor_copy(c.wparts[:, s, 0:O], rest).then_inc(s_wc, 1)
                v.wait_ge(s_wc, wc0 + 2 + B + 1 + 5)
                for b in range(B):
                    rows = slice(b * C, (b + 1) * C)
                    dst = c.WC[rows, :, 0, b * C:(b + 1) * C] if layer == 1 else c.WC[rows, :, b, :]
                    vec.tensor_copy(dst, c.wparts[rows, :, 0:O]).then_inc(s_wc, 1)

            v.wait_ge(s_c, 2)
            for b in range(B):
                for m in range(NM):
                    i = b * NM + m
                    for t in range(NT):
                        if i * NT + t >= PERMS:
                            v.wait_ge(s_ord, ord0 + i * NT + t + 1 - PERMS)
                        at = (m * B + b) * NT + t
                        vec.tensor_scalar(c.perm[:, t % PERMS, :], c.iota[:, :], k.rank[:, at:at + 1], None, ALU.is_equal).then_inc(s_perm, 1)
                        if i * NT + t == PERMS - 1:
                            weights()
                    if layer == 1 and i == 0:
                        v.wait_ge(s_sum, 1)
                        vec.tensor_scalar(c.flag[:, :], ps[:, 7, 0:KC * 32], 0.0, None, ALU.is_gt).then_inc(s_flag, 1)
            v.wait_ge(s_sc, sc0 + 8)
            row = c.W
            ends = lambda at, dims: fcopy(c.fsT[:, 0, at:], [[row, 4]] + dims)
            vec.tensor_copy(c.fsT[:, :, N:row], ends(N - 1, [[0, row - N]])).then_inc(s_fs, 1)
            for i in range(LEAD):
                vec.tensor_copy(c.pre[:, :, i, 0:i + LEAD + 1], c.fsT[:, :, 0:i + LEAD + 1]).then_inc(s_fs, 1)
                if i < LEAD - 1:
                    vec.tensor_copy(c.pre[:, :, i, i + LEAD + 1:WIN], ends(i + LEAD, [[0, WIN - i - LEAD - 1]])).then_inc(s_fs, 1)
            v.wait_ge(s_c, 5)

            def reduce(it):
                v.wait_ge(s_H, t0 + it + 1)
                last = isinstance(it, int) and it == STEPS - 1
                cols = LASTN * WIN if last else COLS
                raw = c.f1 if layer == 1 else c.f2
                for b in range(nb):
                    H = ps[:, 7, b * COLS:b * COLS + cols]
                    st = c.stats[:, b, it, :] if isinstance(it, int) else c.stats[:, b, bass.ds(it, 1), :].rearrange("p a s -> p (a s)")
                    vec.bn_stats(st, H)
                    win = H.rearrange("p (n j) -> p n j", j=WIN)
                    out = lambda at, cnt: raw[:, bass.ds(at, cnt)] if layer == 1 else raw[:, b, bass.ds(at, cnt)]
                    if last:
                        vec.tensor_reduce(out(N - REG, REG), win[:, 0:REG, :], AX, ALU.max)
                        ins = vec.tensor_reduce(out(0, LEAD), win[:, REG:LASTN, :], AX, ALU.max)
                    else:
                        ins = vec.tensor_reduce(out(it * STEP + LEAD, STEP), win, AX, ALU.max)
                ins.then_inc(s_red, 1)

            def step(it, u):
                S = c.S[u]
                v.wait_ge(s_S, t0 + it + 1)
                if after(it, 2):
                    v.wait_ge(s_lo, t0 + it - 1)
                scores = ps[:, S_BANK[u]:S_BANK[u] + 2, 0:COLS].rearrange("p r (s i) -> p r s i", i=ROWS)
                vec.tensor_reduce(c.mx[u][:, :].rearrange("p (r s) -> p r s", r=2), scores, AX, ALU.max).then_inc(s_max, 1)
                v.wait_ge(s_max, t0 + it + 1)
                vec.tensor_tensor(S[:, :, :].rearrange("p (r s) i -> p r s i", r=2), scores,
                                  fcopy(c.mx[u][:, :], [[SLOTS, 2], [1, SLOTS], [0, ROWS]]), ALU.subtract).then_inc(s_sub, 1)
                if after(it, 1):
                    turn(it - 1, 1 - u)
                v.wait_ge(s_E, t0 + it + 1)
                vec.tensor_reduce(c.den[u][:, :], S[:, :, :], AX, ALU.add).then_inc(s_den, 1)
                v.wait_ge(s_den, 2 * t0 + it * 2 + 1)
                vec.reciprocal(c.den[u][:, :], c.den[u][:, :]).then_inc(s_den, 1)
                if after(it, 1):
                    turn_rest(it - 1, 1 - u)
                if after(it, 4):
                    reduce(it - 4)

            words = lambda x: x[:, :, :, :].rearrange("p s j w -> p (s j w)").bitcast(F32).rearrange("p (s j) -> p s j", j=32)

            def turn(it, u):
                v.wait_ge(s_lo, t0 + it + 1)
                if after(it, 2):
                    v.wait_ge(s_PV, t0 + it - 1)
                turned = c.PT[u][:, :, :, :, :].rearrange("p s q i w -> p (s q i w)").bitcast(F32).rearrange("p (s q i) -> p s q i", q=4, i=32)
                for q in (0, 1):
                    quad = slice(32 * q, 32 * q + 32)
                    vec.transpose(turned[quad, :, q, :], words(c.PP[u])[quad])

            def turn_rest(it, u):
                if after(it, 1):
                    v.wait_ge(s_PT, t0 + it)
                vec.transpose(words(c.PC)[C:P], words(c.PP[u])[C:P]).then_inc(s_turned, 1)

            def tail():
                turn(STEPS - 1, 0)
                turn_rest(STEPS - 1, 0)
                for it in range(STEPS - 4, STEPS):
                    reduce(it)

            walk(v, step, tail)
            v.wait_ge(s_red, t0 + STEPS)
            for b in range(nb):
                vec.bn_aggr(c.mvb[:, b, :], c.stats[:, b, :, :].rearrange("p s w -> p (s w)")).then_inc(s_end, 1)
            v.wait_ge(s_end, nb)
            vec.tensor_scalar(c.shift[:, 0:nb], c.mvb[:, 0:nb, 0], c.cb[:, 0:1], c.cb[:, 0:1], ALU.add, ALU.subtract).then_inc(s_end, 1)
            v.wait_ge(s_std, nb)
            vec.reciprocal(c.rsb[:, 0:nb], c.stdb[:, 0:nb]).then_inc(s_end, 1)
            v.wait_ge(s_end, nb + 2)
            raws = [c.f1[:, :] if layer == 1 else c.f2[:, b, :] for b in range(nb)]
            for b in range(nb):
                vec.tensor_scalar(raws[b], raws[b], c.shift[:, b:b + 1], c.rsb[:, b:b + 1], ALU.subtract, ALU.mult).then_inc(s_end, 1)
            for b in range(nb):
                v.wait_ge(s_end, nb + 3 + b)
                vec.scalar_tensor_tensor(out=raws[b], in0=raws[b], scalar=0.2, in1=raws[b], op0=ALU.mult, op1=ALU.max).then_inc(s_end, 1)
            v.wait_ge(s_end, 3 * nb + 2)

        @block.gpsimd
        def _(pool):
            gp = nc.gpsimd
            gp.memset(c.WN[:, :, :, :], 0.0)
            gp.memset(c.WC[:, :, :, :], 0.0).then_inc(s_c, 1)
            if layer == 1:
                gp.iota(c.iota[:, :], [[1, N]], base=0, channel_multiplier=0, allow_small_or_imprecise_dtypes=True).then_inc(s_c, 1)
                for a in range(2):
                    for b in range(B):
                        at = b * C + a * 2 * CH
                        gp.tensor_copy(c.sel[:, a * B + b, :].rearrange("p (r m c) -> p r m c", r=2, m=NM),
                                       fcopy(k.ident[:, at:], [[CH, 2], [0, NM], [1, CH]])).then_inc(s_sel, 1)
                gp.memset(c.conv_d[:, :, :], 0.0).then_inc(s_blk, 1)
                gp.memset(c.blocks[:, :], 0.0).then_inc(s_blk, 1)
                pool.wait_ge(s_blk, 2)
                for q in range(4):
                    gp.memset(c.blocks[32 * q:32 * q + 32, 32 * q:32 * q + 32], 1.0).then_inc(s_blk, 1)
                pool.wait_ge(s_blk, 6)
                for u in range(2):
                    gp.memset(c.X[u][:, :, :], 0.0).then_inc(s_c0, 1)
                    gp.memset(c.PP[u][:, :, :, :], 0.0).then_inc(s_c0, 1)
                    gp.memset(c.PT[u][:, :, :, :, :], 0.0).then_inc(s_c0, 1)
                gp.memset(c.rows_u[:, :], 1.0).then_inc(s_c0, 1)
                gp.memset(c.cols_v[:, :, :], -FAR).then_inc(s_c0, 1)
                pool.wait_ge(s_c0, 8)
                masks = ((c.rows_u[:, :].rearrange("p (q i) -> p q i", i=32), 4), (c.cols_v[:, :, :], SLOTS))
                for i, (m, cnt) in enumerate(masks):
                    gp.affine_select(out=m, in_=m, compare_op=ALU.is_ge, fill=0.0, base=0, pattern=[[0, cnt], [1, m.shape[2]]],
                                     channel_multiplier=-WIN).then_inc(s_c0, 1)
                    pool.wait_ge(s_c0, 9 + 2 * i)
                    gp.affine_select(out=m, in_=m, compare_op=ALU.is_ge, fill=0.0, base=WIN - 1, pattern=[[0, cnt], [-1, m.shape[2]]],
                                     channel_multiplier=WIN).then_inc(s_c0, 1)
                    pool.wait_ge(s_c0, 10 + 2 * i)
                for i, (m, value) in enumerate(((c.rows_u[:, :], 1.0), (c.cols_v[:, :, :], FAR))):
                    gp.affine_select(out=m, in_=m, compare_op=ALU.is_ge, fill=value, base=30, pattern=[[0, x] for x in m.shape[1:]],
                                     channel_multiplier=-1).then_inc(s_c0, 1)
                pool.wait_ge(s_c0, 14)
                gp.memset(c.fcl[:, :], 0.0).then_inc(s_c, 1)
                pool.wait_ge(n.stat, n.stats(6))
            else:
                gp.memset(c.fcl[:, :], 0.0).then_inc(s_c, 1)
                gp.memset(c.X[0][:, :, :], 0.0).then_inc(s_c, 1)
            pool.wait_ge(s_c, 3)
            gp.tensor_copy(c.f16[:, :], src[:, :]).then_inc(s_f16, 1)
            pool.wait_ge(s_f16, f160 + 1)
            gp.tensor_copy(c.fcl[:, 0:REG], c.f16[:, N - REG:N]).then_inc(s_c, 1)
            gp.tensor_copy(c.fcl[:, REG:LASTN], c.f16[:, 0:LEAD]).then_inc(s_c, 1)
            if layer == 1:
                pool.wait_ge(k.wt_in, 16)
                pool.wait_ge(s_flag, 1)
                w = k.wt[:, :, :].rearrange("p k (n j) -> p (k n) j", j=32)
                gp.tensor_tensor(w, w, fcopy(c.flag[:, :], [[1, KC * 32], [0, 32]]), ALU.mult)
            else:
                pool.wait_ge(s_c, 5)
            pool.wait_ge(s_cc, cc0 + 8)
            pool.wait_ge(s_sc, sc0 + 7)

            def differences(it, u):
                if after(it, 2):
                    pool.wait_ge(s_xt, t0 + it - 1)
                start, point, trio = [[c.W, 4], [1, WIN]], [[N, 4], [0, WIN]], lambda dims, cnt, step: [dims[0], [TRIO * step, cnt], [step, TRIO], dims[1]]
                full = lambda cnt: [[STEP // TRIO * 32, 4], [32, cnt], [WIN, TRIO], [1, WIN]]
                last = isinstance(it, int) and it == STEPS - 1
                if isinstance(it, int) and it == 1:
                    pool.wait_ge(s_sc, sc0 + 8)
                if last:
                    pool.wait_ge(s_fs, fs0 + 2 * LEAD)
                cnt = REG // TRIO if last else STEP // TRIO
                ins = gp.tensor_tensor(fcopy(c.X[u][:, 0, 0:1], full(cnt)),
                                       fcopy(c.fsT[:, 0, bass.ds(it * STEP, 1)], trio(start, cnt, 1)),
                                       fcopy(c.fTr[:, 0, bass.ds(it * STEP + LEAD, 1)], trio(point, cnt, 1)), ALU.subtract)
                if last:
                    gp.memset(c.X[u][:, :, LASTN // TRIO * 32 + LASTN % TRIO * WIN:], 0.0)
                    for i in range(cnt * TRIO, LASTN):
                        at = i // TRIO * 32 + i % TRIO * WIN
                        n0 = it * STEP + LEAD + i if i < REG else i - REG
                        near = c.fsT[:, :, n0 - LEAD:n0 - LEAD + WIN] if i < REG else c.pre[:, :, n0, :]
                        ins = gp.tensor_tensor(c.X[u][:, :, at:at + WIN], near, fcopy(c.fTr[:, 0, n0:n0 + 1], [[N, 4], [0, WIN]]), ALU.subtract)
                ins.then_inc(s_X, 1)

            def step(it, u):
                S = c.S[u][:, :, :]
                over = lambda x: fcopy(x[:, :], [[1, 2 * SLOTS], [0, ROWS]])
                if not (isinstance(it, int) and it == STEPS - 1):
                    differences(it + 1, 1 - u)
                pool.wait_ge(s_den, 2 * t0 + it * 2 + 2)
                gp.tensor_tensor(S, S, over(c.den[u]), ALU.mult).then_inc(s_P, 1)
                pool.wait_ge(s_hi, t0 + it + 1)
                gp.tensor_tensor(c.PP[u][:, :, 0:ROWS, 1], S, c.PP[u][:, :, 0:ROWS, 0], ALU.subtract).then_inc(s_lo, 1)

            differences(0, 0)
            walk(pool, step, lambda: None)


def stage_cloud_output(nc, k, dr, c):
    with ExitStack() as ctx:
        sb = lambda name, shape, dt=F32: k.sb(name, shape, dt, ctx)
        res = c.fsg[:, 0:NT // 2, :].rearrange("p t d -> p (t d)")
        stats, mv, std, rs = sb("o_stats", [P, 2, 6]), sb("o_mv", [P, 2]), sb("o_std", [P, 1]), sb("o_rs", [P, 1])
        sem = lambda name: k.sem(f"o_{name}")
        s_h, s_st, s_std, s_x = (sem(i) for i in ("h", "stat", "std", "x"))
        ps = k.ps
        block = ctx.enter_context(nc.Block())

        @block.tensor
        def _(pe):
            for half in range(2):
                cols = slice(half * HALF, (half + 1) * HALF)
                for b in range(B):
                    mm = nc.tensor.matmul(ps[b * C:(b + 1) * C, half, :], c.conv_2[:, :], c.f2[:, b, cols], start=False, stop=True)
                mm.then_inc(s_h, 1)
            hold_clock(nc, k, 4, 5 * HOLD)

        @block.scalar
        def _(act):
            act.wait_ge(s_st, 3)
            nc.scalar.activation(std[:, :], mv[:, 1:2], ACT.Sqrt, bias=k.eps[:, 0:1]).then_inc(s_std, 1)

        @block.vector
        def _(v):
            vec = nc.vector
            for half in range(2):
                v.wait_ge(s_h, half + 1)
                vec.bn_stats(stats[:, half, :], ps[:, half, :]).then_inc(s_st, 1)
            v.wait_ge(s_st, 2)
            vec.bn_aggr(mv[:, :], stats[:, :, :]).then_inc(s_st, 1)
            v.wait_ge(s_std, 1)
            vec.reciprocal(rs[:, :], std[:, :]).then_inc(s_st, 1)
            v.wait_ge(s_st, 4)
            for half in range(2):
                cols = slice(half * HALF, (half + 1) * HALF)
                vec.tensor_scalar(res[:, cols], ps[:, half, :], mv[:, 0:1], rs[:, 0:1], ALU.subtract, ALU.mult).then_inc(s_st, 1)
            v.wait_ge(s_st, 6)
            vec.scalar_tensor_tensor(out=res[:, :], in0=res[:, :], scalar=0.2, in1=res[:, :], op0=ALU.mult, op1=ALU.max).then_inc(s_st, 1)
            v.wait_ge(s_st, 7)
            for half in range(2):
                cols = slice(half * HALF, (half + 1) * HALF)
                vec.tensor_tensor(k.x[:, cols], res[:, cols], k.x[:, cols], ALU.add).then_inc(s_x, 1)
            for half in range(2):
                v.wait_ge(s_x, half + 1)
                norm_statistics(nc, k, Norm(k, 4), half)


def stage_point_cloud(nc, k, dr):
    with ExitStack() as ctx:
        c = Cloud(k, ctx)
        stage_cloud_layer(nc, k, dr, c, 1)
        stage_cloud_layer(nc, k, dr, c, 2)
        stage_cloud_output(nc, k, dr, c)


def host_layout(inp, np):
    a = {n: np.asarray(v) for n, v in inp.items()}
    d = {"x": a["x"].reshape(T, D), "ctx_4096": a["ctx_4096"]}
    for n in ("L0_xattn_x1_scale", "L0_xattn_x1_zp", "L0_xattn_x2_scale", "L0_xattn_x2_zp"):
        d[n] = a[n]
    w = a["L0_attn_in_proj_w"].reshape(-1, P, KC, P)
    d["w_in"] = w.transpose(0, 3, 2, 1).reshape(-1, P, D)
    d["w_out"] = a["L0_attn_out_proj_w"].T.reshape(-1, P, D)
    conv = np.concatenate([a["L0_attn_conv_w"][:, 0, :], a["L0_attn_conv_b"][:, None]], axis=1)
    more = np.stack([np.repeat(a["L0_attn_D"], HD), a["L0_attn_norm_w"]], axis=1)
    par = np.concatenate([conv[:DIN], more], axis=1)
    d["par"] = par.reshape(NG, GB, P, -1).transpose(2, 0, 1, 3).reshape(P, NG, -1)
    d["par_bc"] = conv[DIN:].reshape(2 * NG, P, CK + 1).transpose(1, 0, 2)
    d["head_par"] = np.stack([a["L0_attn_dt_bias"], a["L0_attn_A_log"]], axis=1)
    by_chunk = lambda m: m.reshape(KC, P, -1).transpose(1, 0, 2)
    d["base_w"] = by_chunk(a["L0_ffn_base_W"].T)
    lora = a["L0_ffn_lora_A"].transpose(1, 0, 2).reshape(D, ER)
    d["lora_a_router"] = by_chunk(np.concatenate([lora, a["L0_ffn_router_W"].T], axis=1)).reshape(P, -1)
    d["lora_b"] = a["L0_ffn_lora_B"].reshape(ER, D)
    d["mask_t"] = a["L1_attn_mask"].T
    d["wt"] = by_chunk(a["L1_attn_weight"].T)
    d["w3"] = by_chunk(a["L1_ffn_w3"].T)
    d["w12"] = a["L1_ffn_w12"].reshape(-1, P, KC, P).transpose(0, 3, 2, 1).reshape(-1, P, D)
    d["b12"] = a["L1_ffn_b12"].reshape(-1, P).T
    d["L1_ffn_b3"] = a["L1_ffn_b3"]
    for layer, perm in ((1, (2, 0, 3, 1)), (2, (1, 3, 0, 2))):
        w = a[f"L1_xattn_W_lin{layer}"].reshape(P, 2, C, NM)
        near = w[:, 1].reshape(P, 2, 2, CH, NM)[..., np.argsort(perm)]
        d[f"lin_n{layer}"] = near.transpose(0, 1, 2, 4, 3).reshape(P, 2, P)
        d[f"lin_c{layer}"] = np.concatenate([w[:, 0].transpose(0, 2, 1)] * B, axis=2)
        d[f"b_lin{layer}"] = a[f"L1_xattn_b_lin{layer}"][:, None]
        d[f"conv_t{layer}"] = np.concatenate([a[f"L1_xattn_W_conv{layer}"].T] * (B // layer), axis=1)
    w = a["L1_xattn_W_conv3"].T
    d["conv3_diag"] = w[:2 * C].reshape(2, C, C).transpose(1, 0, 2)
    d["conv3_last"] = w[2 * C:]
    return {n: np.ascontiguousarray(v) for n, v in d.items()}


def build(nc, dr, out):
    with ExitStack() as ctx:
        k = Kit(nc, ctx)
        k.x = k.sb("x_sb", [P, D], F32)
        k.h = k.sb("h_sb", [P, D], F32)
        k.hT = k.sb("hT", [P, KC, T], F32)
        k.ident = k.sb("ident", [P, P], F32)
        k.identb = k.sb("identb", [P, P], BF16)
        k.identh = k.sb("identh", [P, P], F16)
        k.eps = k.sb("eps", [P, 1], F32)
        k.root = k.sb("root", [P, 1], F32)
        k.bn = k.sb("bn", [P, 2, 6], F32)
        k.mv = k.sb("mv", [P, 2], F32)
        k.std = k.sb("std", [P, 1], F32)
        k.rstd = k.sb("rstd", [P, 1], F32)
        k.coord = k.sb("coord", [P, B * 3 * NT], F32)
        k.keys = k.sb("keys", [P, NM * B * NT], F32)
        k.rank = k.sb("rank", [P, NM * B * NT], F32)
        k.msum = k.sb("msum", [P, KC * 32], F32)
        k.ring_in = [k.sem(f"ring_in{i}") for i in range(6)]
        k.norm_stat, k.norm_std, k.norm_turned, k.norm_copied = (k.sem(f"norm_{i}") for i in ("stat", "std", "turned", "copied"))
        k.moe_in = k.sem("moe_in")
        k.coord_ready = k.sem("coord_ready")
        k.ps = ctx.enter_context(nc.psum_tensor("ps", [P, 8, HALF], F32))
        with ExitStack() as early:
            k.ring = k.sb("ring", [P, 24, D], F32, early)
            stage_quantised_product(nc, k, dr)
            stage_mixer(nc, k, dr)
            stage_lora_experts(nc, k)
        k.wt = k.sb("wt", [P, KC, D], F32)
        k.w3 = k.sb("w3", [P, D // P, D], F32)
        k.wt_in, k.w3_in = k.sem("wt_in"), k.sem("w3_in")
        stage_point_cloud(nc, k, dr)
        stage_sparse_linear_and_ffn(nc, k, dr, out)


def kernel(**inputs):
    import numpy as np
    import concourse.bacc as bacc
    from concourse.bass_utils import run_bass_kernel_spmd
    arrays = host_layout(inputs, np)
    nc = bacc.Bacc("TRN2", target_bir_lowering=False, num_devices=1)
    dr = {n: nc.dram_tensor(f"in_{n}", a.shape, mybir.dt.from_np(a.dtype), kind="ExternalInput").ap() for n, a in arrays.items()}
    out = nc.dram_tensor("out_0", (B, L, D), F32, kind="ExternalOutput").ap()
    build(nc, dr, out)
    result = run_bass_kernel_spmd(nc, [{f"in_{n}": a for n, a in arrays.items()}], core_ids=[0])
    return result.results[0]["out_0"]
```
